# Optimizing a Trainium2 kernel written in Bass

```python
import numpy as np
import jax
import jax.numpy as jnp

def _softmax(x, axis=-1):
    return jax.nn.softmax(x, axis=axis)

def _gelu(x):
    return jax.nn.gelu(x, approximate=True)

def _silu(x):
    return jax.nn.silu(x)

def _sigmoid(x):
    return jax.nn.sigmoid(x)

def _layernorm(x, axis=-1, eps=1e-05):
    m = jnp.mean(x, axis=axis, keepdims=True)
    v = jnp.var(x, axis=axis, keepdims=True)
    return (x - m) / jnp.sqrt(v + eps)

def _scatter_add(tgt, idx, src, axis=0):
    return tgt.at[idx].add(src)

def _segment_sum(src, seg, n):
    return jax.ops.segment_sum(src, seg, n)
kernel_name = 'mk_decoder_postln_d2_seqx_r4_cc1688'

def setup_inputs(seed: int=0):
    np.random.seed(seed)
    _w = jnp.asarray

    def _rec_inputs():
        import jax
        import jax.numpy as jnp
        _rk = jax.random.key(seed)
        x = -0.0002928 + 1 * jax.random.normal(jax.random.fold_in(_rk, 1), (16, 128, 512), jnp.float32)
        _lenS = 128 - jax.random.randint(jax.random.fold_in(_rk, 7), (16,), 0, max(1, 128 // 4) + 1, jnp.int32)
        _lenS2 = 128 - jax.random.randint(jax.random.fold_in(_rk, 8), (16,), 0, max(1, 128 // 4) + 1, jnp.int32)
        _ctx_2048P = jax.random.normal(jax.random.fold_in(_rk, 11), (16, 16, 512), jnp.float32)
        _ctx_2048c = jax.random.dirichlet(jax.random.fold_in(_rk, 511), 0.3 * jnp.ones((16,), jnp.float32), (16, 128))
        _ctx_2048t = jnp.einsum('bsk,bkd->bsd', _ctx_2048c, _ctx_2048P)
        _ctx_2048t = _ctx_2048t * jax.lax.rsqrt(jnp.mean(jnp.square(_ctx_2048t)) + 1e-12) * 0.953939
        ctx_2048 = -1.39393e-06 + 0.999914 * (_ctx_2048t + 0.3 * jax.random.normal(jax.random.fold_in(_rk, 611), (16, 128, 512), jnp.float32))
        return (x, ctx_2048)
    x, ctx_2048 = _rec_inputs()

    def _L0_attn_setup():
        import jax, jax.numpy as jnp
        import numpy as np
        D_MODEL = 512
        N_HEADS = 32
        N_KV_HEADS = 8
        HEAD_DIM = D_MODEL // N_HEADS
        N_GROUPS = N_HEADS // N_KV_HEADS
        THETA = 10000.0

        def _rope_tables(T, dim):
            inv_freq = 1.0 / THETA ** (jnp.arange(0, dim, 2, dtype=jnp.float32) / dim)
            t = jnp.arange(T, dtype=jnp.float32)
            freqs = jnp.outer(t, inv_freq)
            return (jnp.cos(freqs), jnp.sin(freqs))

        def _apply_rope(x, cos, sin):
            half = x.shape[-1] // 2
            x1, x2 = (x[..., :half], x[..., half:])
            c = cos[None, None, :, :]
            s = sin[None, None, :, :]
            return jnp.concatenate([x1 * c - x2 * s, x2 * c + x1 * s], axis=-1)
        key = jax.random.key(seed)
        ks = jax.random.split(key, 6)
        b, T = (2, 512)
        d = D_MODEL
        dkv = N_KV_HEADS * HEAD_DIM
        sc = 1.0 / np.sqrt(d)
        x = jax.random.normal(ks[0], (b, T, d), dtype=jnp.float32)
        Wq = jax.random.normal(ks[1], (d, d), dtype=jnp.float32) * sc
        Wk = jax.random.normal(ks[2], (d, dkv), dtype=jnp.float32) * sc
        Wv = jax.random.normal(ks[3], (d, dkv), dtype=jnp.float32) * sc
        Wo = jax.random.normal(ks[4], (d, d), dtype=jnp.float32) * sc
        b_out = jax.random.normal(ks[5], (d,), dtype=jnp.float32) * 0.01
        return {'x': x, 'Wq': Wq, 'Wk': Wk, 'Wv': Wv, 'Wo': Wo, 'b_out': b_out}
    _L0_attn_all = _L0_attn_setup()
    _L0_attn_in = {k: v for k, v in _L0_attn_all.items() if k in ('Wq', 'Wk', 'Wv', 'Wo', 'b_out')}
    del _L0_attn_all

    def _L0_xattn_setup():
        import math
        import jax, jax.numpy as jnp
        import numpy as np
        N_HEADS = 8
        CHANNELS = 128
        K_CH = CHANNELS // N_HEADS
        THETA = 10000.0

        def _rope_freqs(length, dim):
            inv_freq = 1.0 / THETA ** (jnp.arange(0, dim, 2, dtype=jnp.float32) / dim)
            f = jnp.arange(length, dtype=jnp.float32)[:, None] * inv_freq[None, :]
            return jnp.concatenate([f, f], axis=-1)

        def _apply_rotary(pos, t):
            half = t.shape[-1] // 2
            rot = jnp.concatenate([-t[..., half:], t[..., :half]], axis=-1)
            return t * jnp.cos(pos) + rot * jnp.sin(pos)

        def _proj(inp, W, b):
            return jnp.einsum('oc,bct->bot', W, inp) + b[None, :, None]
        key = jax.random.key(seed)
        ks = jax.random.split(key, 10)
        B, C, T = (4, CHANNELS, 512)
        bound = math.sqrt(6.0 / (C + C))

        def w(k):
            return jax.random.uniform(k, (C, C), jnp.float32, -bound, bound)
        return {'x': jax.random.normal(ks[0], (B, C, T), jnp.float32), 'c': jax.random.normal(ks[1], (B, C, T), jnp.float32), 'Wq': w(ks[2]), 'bq': jnp.zeros((C,), jnp.float32), 'Wk': w(ks[3]), 'bk': jnp.zeros((C,), jnp.float32), 'Wv': w(ks[4]), 'bv': jnp.zeros((C,), jnp.float32), 'Wo': w(ks[5]), 'bo': jnp.zeros((C,), jnp.float32)}
    _L0_xattn_all = _L0_xattn_setup()
    _L0_xattn_in = {k: v for k, v in _L0_xattn_all.items() if k in ('Wq', 'bq', 'Wk', 'bk', 'Wv', 'bv', 'Wo', 'bo')}
    del _L0_xattn_all

    def _L0_ffn_setup():
        import jax, jax.numpy as jnp
        import numpy as np
        B_, S, D = (2, 512, 512)
        F_ = 2048
        R = 16
        H = 16
        HD = D // H
        MOD_SCALE = 0.1
        EPS = 1e-06

        def _rmsnorm(x, w):
            v = jnp.mean(x * x, axis=-1, keepdims=True)
            return x * jax.lax.rsqrt(v + EPS) * w

        def _attention(x, Wq, Wk, Wv, Wo):
            b, s, d = x.shape
            q = (x @ Wq.T).reshape(b, s, H, HD)
            k = (x @ Wk.T).reshape(b, s, H, HD)
            v = (x @ Wv.T).reshape(b, s, H, HD)
            scores = jnp.einsum('bqhd,bkhd->bhqk', q, k) / np.sqrt(HD).astype(np.float32)
            causal = jnp.tril(jnp.ones((s, s), bool))
            scores = jnp.where(causal, scores, jnp.finfo(scores.dtype).min)
            probs = jax.nn.softmax(scores, axis=-1)
            out = jnp.einsum('bhqk,bkhd->bqhd', probs, v).reshape(b, s, d)
            return out @ Wo.T
        key = jax.random.key(seed)
        ks = jax.random.split(key, 12)
        sd = 0.02
        return {'hidden_states': jax.random.normal(ks[0], (B_, S, D), jnp.float32), 'ln1_w': jnp.ones((D,), jnp.float32), 'ln2_w': jnp.ones((D,), jnp.float32), 'Wq': jax.random.normal(ks[1], (D, D), jnp.float32) * sd, 'Wk': jax.random.normal(ks[2], (D, D), jnp.float32) * sd, 'Wv': jax.random.normal(ks[3], (D, D), jnp.float32) * sd, 'Wo': jax.random.normal(ks[4], (D, D), jnp.float32) * sd, 'A': jax.random.normal(ks[5], (D, R), jnp.float32) * (0.01 / np.sqrt(D)), 'B': jax.random.normal(ks[6], (R, F_), jnp.float32) * (0.01 / np.sqrt(R)), 'W_in_base': jax.random.normal(ks[7], (F_, D), jnp.float32) * sd, 'W_up_base': jax.random.normal(ks[8], (F_, D), jnp.float32) * sd, 'W_down': jax.random.normal(ks[9], (D, F_), jnp.float32) * sd}
    _L0_ffn_all = _L0_ffn_setup()
    _L0_ffn_in = {k: v for k, v in _L0_ffn_all.items() if k in ('ln1_w', 'ln2_w', 'Wq', 'Wk', 'Wv', 'Wo', 'A', 'B', 'W_in_base', 'W_up_base', 'W_down')}
    del _L0_ffn_all

    def _L1_attn_setup():
        import jax, jax.numpy as jnp
        import numpy as np
        B, T, HID = (1, 512, 512)
        H = 16
        D = HID // H
        EPS = 1e-05

        def _layer_norm(x, eps=1e-05):
            mu = jnp.mean(x, axis=-1, keepdims=True)
            var = jnp.mean((x - mu) ** 2, axis=-1, keepdims=True)
            return (x - mu) * jax.lax.rsqrt(var + eps)

        def _feature_map(x, gamma, beta):
            return _layer_norm(x * gamma + beta)
        key = jax.random.key(seed)
        ks = jax.random.split(key, 8)
        s = HID ** (-0.5)
        return {'hidden_states': jax.random.normal(ks[0], (B, T, HID), jnp.float32), 'Wq': jax.random.normal(ks[1], (HID, HID), jnp.float32) * s, 'Wk': jax.random.normal(ks[2], (HID, HID), jnp.float32) * s, 'Wv': jax.random.normal(ks[3], (HID, HID), jnp.float32) * s, 'Wo': jax.random.normal(ks[4], (HID, HID), jnp.float32) * s, 'gamma': 1.0 + 0.1 * jax.random.normal(ks[5], (D,), jnp.float32), 'beta': 0.1 * jax.random.normal(ks[6], (D,), jnp.float32)}
    _L1_attn_all = _L1_attn_setup()
    _L1_attn_in = {k: v for k, v in _L1_attn_all.items() if k in ('Wq', 'Wk', 'Wv', 'Wo', 'gamma', 'beta')}
    del _L1_attn_all

    def _L1_xattn_setup():
        import math
        import jax, jax.numpy as jnp
        import numpy as np
        N_HEADS = 16
        key = jax.random.key(seed)
        k1, k2 = jax.random.split(key)
        qkv = jax.random.normal(k1, (2, 256, 512), dtype=jnp.float32)
        y = jax.random.normal(k2, (2, 256, 512), dtype=jnp.float32)
        return {'qkv': qkv, 'y': y}
    _L1_xattn_all = _L1_xattn_setup()
    _L1_xattn_in = {k: v for k, v in _L1_xattn_all.items() if k in ()}
    del _L1_xattn_all

    def _L1_ffn_setup():
        import jax, jax.numpy as jnp
        import numpy as np
        B, T, D = (1, 512, 512)
        E, K, F = (64, 4, 128)
        S, SF = (2, 128 * 4)
        CAP = 64

        def _moe_forward(x, router_w, router_bias, gate_w, up_w, down_w, sh_gate_w, sh_up_w, sh_down_w):
            b, t, d = x.shape
            flat = x.reshape(b * t, d)
            N = flat.shape[0]
            logits = flat @ router_w.T
            scores = jax.nn.softmax(logits, axis=-1)
            _, topk_idx = jax.lax.top_k(logits + router_bias, K)
            topk_w = jnp.take_along_axis(scores, topk_idx, axis=-1)
            topk_w = topk_w / topk_w.sum(axis=-1, keepdims=True)
            P = N * K
            e_flat = topk_idx.reshape(-1)
            t_flat = jnp.repeat(jnp.arange(N), K)
            w_flat = topk_w.reshape(-1)
            order = jnp.argsort(e_flat)
            e_s, t_s, w_s = (e_flat[order], t_flat[order], w_flat[order])
            counts = jnp.bincount(e_s, length=E)
            starts = jnp.concatenate([jnp.zeros((1,), counts.dtype), jnp.cumsum(counts)[:-1]])
            pos = jnp.arange(P) - starts[e_s]
            slot = jnp.where(pos < CAP, pos, CAP)
            tok_table = jnp.zeros((E, CAP + 1), jnp.int32).at[e_s, slot].set(t_s)[:, :CAP]
            w_table = jnp.zeros((E, CAP + 1), w_s.dtype).at[e_s, slot].set(w_s)[:, :CAP]
            xg = flat[tok_table]
            g = jnp.einsum('ecd,efd->ecf', xg, gate_w)
            u = jnp.einsum('ecd,efd->ecf', xg, up_w)
            y = jnp.einsum('ecf,edf->ecd', jax.nn.silu(g) * u, down_w)
            out = jnp.zeros_like(flat).at[tok_table.reshape(-1)].add((y * w_table[..., None]).reshape(-1, d))
            sg = jnp.einsum('nd,sfd->nsf', flat, sh_gate_w)
            su = jnp.einsum('nd,sfd->nsf', flat, sh_up_w)
            out = out + jnp.einsum('nsf,sdf->nd', jax.nn.silu(sg) * su, sh_down_w)
            return out.reshape(b, t, d)
        key = jax.random.key(seed)
        ks = jax.random.split(key, 9)
        s = 0.02
        return {'x': jax.random.normal(ks[0], (B, T, D), jnp.float32), 'router_w': jax.random.normal(ks[1], (E, D), jnp.float32) * s, 'router_bias': jnp.zeros((E,), jnp.float32), 'gate_w': jax.random.normal(ks[2], (E, F, D), jnp.float32) * s, 'up_w': jax.random.normal(ks[3], (E, F, D), jnp.float32) * s, 'down_w': jax.random.normal(ks[4], (E, D, F), jnp.float32) * s, 'sh_gate_w': jax.random.normal(ks[5], (S, SF, D), jnp.float32) * s, 'sh_up_w': jax.random.normal(ks[6], (S, SF, D), jnp.float32) * s, 'sh_down_w': jax.random.normal(ks[7], (S, D, SF), jnp.float32) * s}
    _L1_ffn_all = _L1_ffn_setup()
    _L1_ffn_in = {k: v for k, v in _L1_ffn_all.items() if k in ('router_w', 'router_bias', 'gate_w', 'up_w', 'down_w', 'sh_gate_w', 'sh_up_w', 'sh_down_w')}
    del _L1_ffn_all
    return {'x': x, 'ctx_2048': ctx_2048, 'L0_attn_Wq': _L0_attn_in['Wq'], 'L0_attn_Wk': _L0_attn_in['Wk'], 'L0_attn_Wv': _L0_attn_in['Wv'], 'L0_attn_Wo': _L0_attn_in['Wo'], 'L0_attn_b_out': _L0_attn_in['b_out'], 'L0_xattn_Wq': _L0_xattn_in['Wq'], 'L0_xattn_bq': _L0_xattn_in['bq'], 'L0_xattn_Wk': _L0_xattn_in['Wk'], 'L0_xattn_bk': _L0_xattn_in['bk'], 'L0_xattn_Wv': _L0_xattn_in['Wv'], 'L0_xattn_bv': _L0_xattn_in['bv'], 'L0_xattn_Wo': _L0_xattn_in['Wo'], 'L0_xattn_bo': _L0_xattn_in['bo'], 'L0_ffn_ln1_w': _L0_ffn_in['ln1_w'], 'L0_ffn_ln2_w': _L0_ffn_in['ln2_w'], 'L0_ffn_Wq': _L0_ffn_in['Wq'], 'L0_ffn_Wk': _L0_ffn_in['Wk'], 'L0_ffn_Wv': _L0_ffn_in['Wv'], 'L0_ffn_Wo': _L0_ffn_in['Wo'], 'L0_ffn_A': _L0_ffn_in['A'], 'L0_ffn_B': _L0_ffn_in['B'], 'L0_ffn_W_in_base': _L0_ffn_in['W_in_base'], 'L0_ffn_W_up_base': _L0_ffn_in['W_up_base'], 'L0_ffn_W_down': _L0_ffn_in['W_down'], 'L1_attn_Wq': _L1_attn_in['Wq'], 'L1_attn_Wk': _L1_attn_in['Wk'], 'L1_attn_Wv': _L1_attn_in['Wv'], 'L1_attn_Wo': _L1_attn_in['Wo'], 'L1_attn_gamma': _L1_attn_in['gamma'], 'L1_attn_beta': _L1_attn_in['beta'], 'L1_ffn_router_w': _L1_ffn_in['router_w'], 'L1_ffn_router_bias': _L1_ffn_in['router_bias'], 'L1_ffn_gate_w': _L1_ffn_in['gate_w'], 'L1_ffn_up_w': _L1_ffn_in['up_w'], 'L1_ffn_down_w': _L1_ffn_in['down_w'], 'L1_ffn_sh_gate_w': _L1_ffn_in['sh_gate_w'], 'L1_ffn_sh_up_w': _L1_ffn_in['sh_up_w'], 'L1_ffn_sh_down_w': _L1_ffn_in['sh_down_w']}

def reference(x, ctx_2048, L0_attn_Wq, L0_attn_Wk, L0_attn_Wv, L0_attn_Wo, L0_attn_b_out, L0_xattn_Wq, L0_xattn_bq, L0_xattn_Wk, L0_xattn_bk, L0_xattn_Wv, L0_xattn_bv, L0_xattn_Wo, L0_xattn_bo, L0_ffn_ln1_w, L0_ffn_ln2_w, L0_ffn_Wq, L0_ffn_Wk, L0_ffn_Wv, L0_ffn_Wo, L0_ffn_A, L0_ffn_B, L0_ffn_W_in_base, L0_ffn_W_up_base, L0_ffn_W_down, L1_attn_Wq, L1_attn_Wk, L1_attn_Wv, L1_attn_Wo, L1_attn_gamma, L1_attn_beta, L1_ffn_router_w, L1_ffn_router_bias, L1_ffn_gate_w, L1_ffn_up_w, L1_ffn_down_w, L1_ffn_sh_gate_w, L1_ffn_sh_up_w, L1_ffn_sh_down_w):
    import jax
    import jax.numpy as jnp

    def _L0_attn_ref(x, Wq, Wk, Wv, Wo, b_out):
        import jax, jax.numpy as jnp
        import numpy as np
        D_MODEL = 512
        N_HEADS = 32
        N_KV_HEADS = 8
        HEAD_DIM = D_MODEL // N_HEADS
        N_GROUPS = N_HEADS // N_KV_HEADS
        THETA = 10000.0

        def _rope_tables(T, dim):
            inv_freq = 1.0 / THETA ** (jnp.arange(0, dim, 2, dtype=jnp.float32) / dim)
            t = jnp.arange(T, dtype=jnp.float32)
            freqs = jnp.outer(t, inv_freq)
            return (jnp.cos(freqs), jnp.sin(freqs))

        def _apply_rope(x, cos, sin):
            half = x.shape[-1] // 2
            x1, x2 = (x[..., :half], x[..., half:])
            c = cos[None, None, :, :]
            s = sin[None, None, :, :]
            return jnp.concatenate([x1 * c - x2 * s, x2 * c + x1 * s], axis=-1)
        b, T, d = x.shape
        hd = HEAD_DIM
        q = (x @ Wq).reshape(b, T, N_HEADS, hd).transpose(0, 2, 1, 3)
        k = (x @ Wk).reshape(b, T, N_KV_HEADS, hd).transpose(0, 2, 1, 3)
        v = (x @ Wv).reshape(b, T, N_KV_HEADS, hd).transpose(0, 2, 1, 3)
        cos, sin = _rope_tables(T, hd)
        q = _apply_rope(q, cos, sin)
        k = _apply_rope(k, cos, sin)
        qg = q.reshape(b, N_KV_HEADS, N_GROUPS, T, hd)
        scores = jnp.einsum('bkgtd,bksd->bkgts', qg, k) / jnp.sqrt(jnp.asarray(hd, x.dtype))
        causal = jnp.tril(jnp.ones((T, T), dtype=bool))
        scores = jnp.where(causal[None, None, None, :, :], scores, jnp.asarray(-jnp.inf, x.dtype))
        attn = jax.nn.softmax(scores, axis=-1)
        ctx = jnp.einsum('bkgts,bksd->bkgtd', attn, v)
        ctx = ctx.reshape(b, N_HEADS, T, hd).transpose(0, 2, 1, 3).reshape(b, T, d)
        return ctx @ Wo + b_out

    def _L0_xattn_ref(x, c, Wq, bq, Wk, bk, Wv, bv, Wo, bo):
        import math
        import jax, jax.numpy as jnp
        import numpy as np
        N_HEADS = 8
        CHANNELS = 128
        K_CH = CHANNELS // N_HEADS
        THETA = 10000.0

        def _rope_freqs(length, dim):
            inv_freq = 1.0 / THETA ** (jnp.arange(0, dim, 2, dtype=jnp.float32) / dim)
            f = jnp.arange(length, dtype=jnp.float32)[:, None] * inv_freq[None, :]
            return jnp.concatenate([f, f], axis=-1)

        def _apply_rotary(pos, t):
            half = t.shape[-1] // 2
            rot = jnp.concatenate([-t[..., half:], t[..., :half]], axis=-1)
            return t * jnp.cos(pos) + rot * jnp.sin(pos)

        def _proj(inp, W, b):
            return jnp.einsum('oc,bct->bot', W, inp) + b[None, :, None]
        b, _, t_t = x.shape
        t_s = c.shape[2]
        q_emb = _rope_freqs(t_t, K_CH)
        k_emb = _rope_freqs(t_s, K_CH)

        def split_heads(t):
            return t.reshape(b, N_HEADS, K_CH, t.shape[2]).transpose(0, 1, 3, 2)
        q = split_heads(_proj(x, Wq, bq))
        k = split_heads(_proj(c, Wk, bk))
        v = split_heads(_proj(c, Wv, bv))
        q = _apply_rotary(q_emb, q)
        k = _apply_rotary(k_emb, k)
        scores = jnp.einsum('bhtc,bhsc->bhts', q, k) / math.sqrt(K_CH)
        p_attn = jax.nn.softmax(scores, axis=-1)
        out = jnp.einsum('bhts,bhsc->bhtc', p_attn, v)
        out = out.transpose(0, 1, 3, 2).reshape(b, N_HEADS * K_CH, t_t)
        return _proj(out, Wo, bo)

    def _L0_ffn_ref(hidden_states, ln1_w, ln2_w, Wq, Wk, Wv, Wo, A, B, W_in_base, W_up_base, W_down):
        import jax, jax.numpy as jnp
        import numpy as np
        B_, S, D = (2, 512, 512)
        F_ = 2048
        R = 16
        H = 16
        HD = D // H
        MOD_SCALE = 0.1
        EPS = 1e-06

        def _rmsnorm(x, w):
            v = jnp.mean(x * x, axis=-1, keepdims=True)
            return x * jax.lax.rsqrt(v + EPS) * w

        def _attention(x, Wq, Wk, Wv, Wo):
            b, s, d = x.shape
            q = (x @ Wq.T).reshape(b, s, H, HD)
            k = (x @ Wk.T).reshape(b, s, H, HD)
            v = (x @ Wv.T).reshape(b, s, H, HD)
            scores = jnp.einsum('bqhd,bkhd->bhqk', q, k) / np.sqrt(HD).astype(np.float32)
            causal = jnp.tril(jnp.ones((s, s), bool))
            scores = jnp.where(causal, scores, jnp.finfo(scores.dtype).min)
            probs = jax.nn.softmax(scores, axis=-1)
            out = jnp.einsum('bhqk,bkhd->bqhd', probs, v).reshape(b, s, d)
            return out @ Wo.T
        residual = hidden_states
        x = _rmsnorm(hidden_states, ln1_w)
        attn = _attention(x, Wq, Wk, Wv, Wo)
        mod = MOD_SCALE * jnp.tanh(attn @ A)
        h = _rmsnorm(residual, ln2_w)
        gate_pre = h @ W_in_base.T + mod * (h @ A) @ B
        gate = jax.nn.silu(gate_pre)
        up = h @ W_up_base.T
        mlp_out = gate * up @ W_down.T
        return residual + mlp_out

    def _L1_attn_ref(hidden_states, Wq, Wk, Wv, Wo, gamma, beta):
        import jax, jax.numpy as jnp
        import numpy as np
        B, T, HID = (1, 512, 512)
        H = 16
        D = HID // H
        EPS = 1e-05

        def _layer_norm(x, eps=1e-05):
            mu = jnp.mean(x, axis=-1, keepdims=True)
            var = jnp.mean((x - mu) ** 2, axis=-1, keepdims=True)
            return (x - mu) * jax.lax.rsqrt(var + eps)

        def _feature_map(x, gamma, beta):
            return _layer_norm(x * gamma + beta)
        b, t, _ = hidden_states.shape
        q = (hidden_states @ Wq.T).reshape(b, t, H, D)
        k = (hidden_states @ Wk.T).reshape(b, t, H, D)
        v = (hidden_states @ Wv.T).reshape(b, t, H, D)
        q = _feature_map(q, gamma, beta)
        k = _feature_map(k, gamma, beta)
        q = q * D ** (-0.5)
        attn = jnp.einsum('bqhd,bkhd->bhqk', q, k) ** 2
        mask = jnp.tril(jnp.ones((t, t), dtype=bool))
        attn = jnp.where(mask, attn, 0.0)
        o = jnp.einsum('bhqk,bkhd->bqhd', attn, v)
        z = jnp.sum(attn, axis=-1)
        o = o / (jnp.swapaxes(z, 1, 2)[..., None] + EPS)
        o = o.reshape(b, t, H * D)
        return o @ Wo.T

    def _L1_xattn_ref(qkv, y):
        import math
        import jax, jax.numpy as jnp
        import numpy as np
        N_HEADS = 16
        bs, width, length = qkv.shape
        ch = width // N_HEADS
        q = qkv.reshape(bs * N_HEADS, ch, length)
        k = v = y.reshape(bs * N_HEADS, ch, -1)
        scale = 1.0 / math.sqrt(math.sqrt(ch))
        weight = jnp.einsum('bct,bcs->bts', q * scale, k * scale)
        weight = jax.nn.softmax(weight.astype(jnp.float32), axis=-1).astype(weight.dtype)
        a = jnp.einsum('bts,bcs->bct', weight, v)
        return a.reshape(bs, -1, length)

    def _L1_ffn_ref(x, router_w, router_bias, gate_w, up_w, down_w, sh_gate_w, sh_up_w, sh_down_w):
        import jax, jax.numpy as jnp
        import numpy as np
        B, T, D = (1, 512, 512)
        E, K, F = (64, 4, 128)
        S, SF = (2, 128 * 4)
        CAP = 64

        def _moe_forward(x, router_w, router_bias, gate_w, up_w, down_w, sh_gate_w, sh_up_w, sh_down_w):
            b, t, d = x.shape
            flat = x.reshape(b * t, d)
            N = flat.shape[0]
            logits = flat @ router_w.T
            scores = jax.nn.softmax(logits, axis=-1)
            _, topk_idx = jax.lax.top_k(logits + router_bias, K)
            topk_w = jnp.take_along_axis(scores, topk_idx, axis=-1)
            topk_w = topk_w / topk_w.sum(axis=-1, keepdims=True)
            P = N * K
            e_flat = topk_idx.reshape(-1)
            t_flat = jnp.repeat(jnp.arange(N), K)
            w_flat = topk_w.reshape(-1)
            order = jnp.argsort(e_flat)
            e_s, t_s, w_s = (e_flat[order], t_flat[order], w_flat[order])
            counts = jnp.bincount(e_s, length=E)
            starts = jnp.concatenate([jnp.zeros((1,), counts.dtype), jnp.cumsum(counts)[:-1]])
            pos = jnp.arange(P) - starts[e_s]
            slot = jnp.where(pos < CAP, pos, CAP)
            tok_table = jnp.zeros((E, CAP + 1), jnp.int32).at[e_s, slot].set(t_s)[:, :CAP]
            w_table = jnp.zeros((E, CAP + 1), w_s.dtype).at[e_s, slot].set(w_s)[:, :CAP]
            xg = flat[tok_table]
            g = jnp.einsum('ecd,efd->ecf', xg, gate_w)
            u = jnp.einsum('ecd,efd->ecf', xg, up_w)
            y = jnp.einsum('ecf,edf->ecd', jax.nn.silu(g) * u, down_w)
            out = jnp.zeros_like(flat).at[tok_table.reshape(-1)].add((y * w_table[..., None]).reshape(-1, d))
            sg = jnp.einsum('nd,sfd->nsf', flat, sh_gate_w)
            su = jnp.einsum('nd,sfd->nsf', flat, sh_up_w)
            out = out + jnp.einsum('nsf,sdf->nd', jax.nn.silu(sg) * su, sh_down_w)
            return out.reshape(b, t, d)
        return _moe_forward(x, router_w, router_bias, gate_w, up_w, down_w, sh_gate_w, sh_up_w, sh_down_w)
    x = _layernorm(x + _L0_attn_ref(x, L0_attn_Wq, L0_attn_Wk, L0_attn_Wv, L0_attn_Wo, L0_attn_b_out), axis=-1)
    x = _layernorm(x + _L0_xattn_ref(x, ctx_2048, L0_xattn_Wq, L0_xattn_bq, L0_xattn_Wk, L0_xattn_bk, L0_xattn_Wv, L0_xattn_bv, L0_xattn_Wo, L0_xattn_bo), axis=-1)
    x = _layernorm(x + _L0_ffn_ref(x, L0_ffn_ln1_w, L0_ffn_ln2_w, L0_ffn_Wq, L0_ffn_Wk, L0_ffn_Wv, L0_ffn_Wo, L0_ffn_A, L0_ffn_B, L0_ffn_W_in_base, L0_ffn_W_up_base, L0_ffn_W_down), axis=-1)
    x = _layernorm(x + _L1_attn_ref(x, L1_attn_Wq, L1_attn_Wk, L1_attn_Wv, L1_attn_Wo, L1_attn_gamma, L1_attn_beta), axis=-1)
    x = _layernorm(x + _L1_xattn_ref(x, ctx_2048), axis=-1)
    x = _layernorm(x + _L1_ffn_ref(x, L1_ffn_router_w, L1_ffn_router_bias, L1_ffn_gate_w, L1_ffn_up_w, L1_ffn_down_w, L1_ffn_sh_gate_w, L1_ffn_sh_up_w, L1_ffn_sh_down_w), axis=-1)
    return x

_drawn_inputs = setup_inputs


def setup_inputs(seed=0):
    import zlib

    import numpy as np

    out = dict(_drawn_inputs(seed))
    spreads = {'L0_xattn_bq': (0.0, 0.506),
     'L0_xattn_bk': (0.0, 0.711),
     'L0_xattn_bv': (0.0, 2.0),
     'L0_xattn_bo': (0.0, 2.0),
     'L0_ffn_ln1_w': (1.0, 0.6),
     'L0_ffn_ln2_w': (1.0, 0.6),
     'L1_ffn_router_bias': (0.0, 0.8)}
    factors = {'L0_attn_b_out': 3.117,
     'L0_ffn_Wq': 35.845,
     'L0_ffn_Wk': 35.844,
     'L0_ffn_Wv': 35.851,
     'L0_ffn_Wo': 35.843,
     'L0_ffn_A': 64.0,
     'L0_ffn_B': 35.341,
     'L1_ffn_router_w': 6.284,
     'L1_ffn_gate_w': 6.026,
     'L1_ffn_up_w': 5.857,
     'L1_ffn_down_w': 5.891}
    for name, (base, spread) in spreads.items():
        noise = np.random.default_rng([zlib.crc32(name.encode()), seed]).standard_normal(out[name].shape)
        drawn = base * np.exp(spread * noise) if base else spread * noise
        out[name] = jnp.asarray(drawn.astype(out[name].dtype))
    for name, factor in factors.items():
        out[name] = (out[name] * factor).astype(out[name].dtype)
    return out
```

```python
import concourse.bass as bass
from concourse import mybir
from contextlib import ExitStack

F32 = mybir.dt.float32
BF16 = mybir.dt.bfloat16
U32 = mybir.dt.uint32
ACT = mybir.ActivationFunctionType
ALU = mybir.AluOpType
AX = mybir.AxisListType

P = 128
B = 16
D = 512
LN_EPS = 1e-5


class Phase:

    def __init__(self, nc):
        self.nc, self.ctx, self.sems = nc, ExitStack(), []

    def __enter__(self):
        self.ctx.__enter__()
        return self

    def __exit__(self, *exc):
        self.ctx.__exit__(*exc)
        if exc[0] is None:
            self.nc.clear_and_free_semaphores(self.sems)
            self.nc.all_engine_barrier()

    def sb(self, name, shape, dt=F32):
        return self.ctx.enter_context(self.nc.sbuf_tensor(name, shape, dt))

    def ps(self, name, shape, dt=F32):
        return self.ctx.enter_context(self.nc.psum_tensor(name, shape, dt))

    def sem(self, name):
        s = self.nc.alloc_semaphore(name)
        self.sems.append(s)
        return s


def begun(count):
    return not (isinstance(count, int) and count <= 0)


def cross_attention(nc, tag, H, x_in, q_parts, k_parts, v_rows, x_out, ident_d, sel_o_d, sel_s_d,
                    half_d, wo_d=None, bo_d=None):
    C = P // H
    L = 512
    G = 4
    NG = H // G
    UNITS = B * NG
    RING = 8
    NBS = RING // NG
    AHEAD = NG + 1
    KT = L // P
    ROWS, MROW, MPARTS = 6 * C, 96, 3
    PROJ = wo_d is not None

    with Phase(nc) as ph:
        sem, sb = ph.sem, ph.sb
        q_st = sb(f"{tag}_q_st", [P, RING, G, L], BF16)
        k_st = sb(f"{tag}_k_st", [P, RING, G, L], BF16)
        v_raw = sb(f"{tag}_v_raw", [P, 2, KT, P])
        v_aug = sb(f"{tag}_v_aug", [P, NBS, KT, H, 32])
        probs = sb(f"{tag}_probs", [P, 2, G, L])
        o_raw = sb(f"{tag}_o_raw", [P, 2, NG, L])
        maxes = sb(f"{tag}_maxes", [P, 2, H * KT])
        m_neg = sb(f"{tag}_m_neg", [H * KT, P])
        m_rest = sb(f"{tag}_m_rest", [H * KT, P])
        m_parts = sb(f"{tag}_m_parts", [H * KT, 2, MPARTS, P], BF16)
        recip = sb(f"{tag}_recip", [P, L])
        o_norm = sb(f"{tag}_o_norm", [P, L])
        x_res = sb(f"{tag}_x_res", [P, 2, L])
        y = sb(f"{tag}_y", [P, L])
        stats = sb(f"{tag}_stats", [P, 6])
        mv = sb(f"{tag}_mv", [P, 2])
        var_eps = sb(f"{tag}_var_eps", [P, 1])
        rstd = sb(f"{tag}_rstd", [P, 1])
        x_new = sb(f"{tag}_x_new", [P, 2, L])
        ident = sb(f"{tag}_ident", [P, P])
        sel_o = sb(f"{tag}_sel_o", [P, G * C])
        sel_s = sb(f"{tag}_sel_s", [P, G * C])
        minus_half = sb(f"{tag}_minus_half", [P, 1])
        if PROJ:
            wo = sb(f"{tag}_wo", [P, P])
            bo = sb(f"{tag}_bo", [P, 1])

        s1_ps = ph.ps(f"{tag}_s1", [P, 2, L])
        st_ps = ph.ps(f"{tag}_st", [P, 2, 2, L])
        o_ps = ph.ps(f"{tag}_o", [P, L])
        misc_ps = ph.ps(f"{tag}_misc", [P, L])

        const_ld = sem(f"{tag}_const_ld")
        passed_dve = sem(f"{tag}_passed_dve")
        passed_pe = sem(f"{tag}_passed_pe")
        passed_pool = sem(f"{tag}_passed_pool")
        memset_done = sem(f"{tag}_memset_done")
        ones_done = sem(f"{tag}_ones_done")
        stack_ld = [sem(f"{tag}_stack_ld{i}") for i in range(RING)]
        v_ld = [sem(f"{tag}_v_ld{i}") for i in range(2)]
        v_placed = sem(f"{tag}_v_placed")
        x_ld = [sem(f"{tag}_x_ld{i}") for i in range(2)]
        s1_full = sem(f"{tag}_s1_full")
        max_done = sem(f"{tag}_max_done")
        st_full = sem(f"{tag}_st_full")
        exp_done = sem(f"{tag}_exp_done")
        av_done = sem(f"{tag}_av_done")
        o_copied = sem(f"{tag}_o_copied")
        sums_full = sem(f"{tag}_sums_full")
        recip_done = sem(f"{tag}_recip_done")
        o_full = sem(f"{tag}_o_full")
        o_normed = sem(f"{tag}_o_normed")
        proj_full = sem(f"{tag}_proj_full")
        mT_full = sem(f"{tag}_mT_full")
        m_step = sem(f"{tag}_m_step")
        m_ld = sem(f"{tag}_m_ld")
        y_done = sem(f"{tag}_y_done")
        ln_step = sem(f"{tag}_ln_step")
        rstd_done = sem(f"{tag}_rstd_done")
        x_done = sem(f"{tag}_x_done")
        x_stored = [sem(f"{tag}_x_stored{i}") for i in range(2)]

        def rounds(eng, body):
            body(0, True, False)
            if UNITS // RING > 2:
                with eng.Fori(1, UNITS // RING - 1) as it:
                    body(it, False, False)
            body(UNITS // RING - 1, False, True)

        def unit_exists(u_off, last):
            return not (last and u_off >= RING)

        block = nc.Block()
        with block:
            @block.sync
            def _(sp):
                for dst, src in ([(ident, ident_d), (sel_o, sel_o_d), (sel_s, sel_s_d), (minus_half, half_d)]
                                 + ([(wo, wo_d), (bo, bo_d)] if PROJ else [])):
                    sp.dma_start(dst[:, :], src).then_inc(const_ld, 16)

                def load_stack(it, j):
                    b, g, s = it * NBS + j // NG, j % NG, j % RING
                    heads = slice(g * G * L, (g + 1) * G * L)

                    def parts(src, p, n):
                        a = src[bass.ds(b, 1), p * C:(p + n) * C, heads]
                        return a.rearrange("o c t -> (o c) t")

                    row = 0
                    for n in (3, 2, 1):
                        sp.dma_start(q_st[row:row + n * C, s, :, :].rearrange("p h t -> p (h t)"),
                                     parts(q_parts, 0, n)).then_inc(stack_ld[s], 16)
                        a = parts(k_parts, 3 - n, 1)
                        a = bass.AP(a.tensor, a.offset, [[0, n]] + [list(x) for x in a.ap])
                        sp.dma_start(k_st[row:row + n * C, s, :, :].rearrange("p h t -> p (h t)"),
                                     a).then_inc(stack_ld[s], 16)
                        row += n * C

                def load_v(b, i):
                    sp.dma_start(v_raw[:, i % 2, :, :],
                                 v_rows[bass.ds(b, 1), :, :].rearrange("o (k p) c -> p (o k) c", p=P)
                                 ).then_inc(v_ld[i % 2], 16)

                def load_x(b, i):
                    sp.dma_start(x_res[:, i % 2, :], x_in[bass.ds(b, 1), :, :].rearrange("o p t -> p (o t)")
                                 ).then_inc(x_ld[i % 2], 16)

                def send_max(b, j0):
                    sp.wait_ge(m_step, (b + 1) * 5)
                    s0 = j0 % RING
                    for p in range(MPARTS):
                        dst = q_st[MROW + p:MROW + p + 1, s0:s0 + NG, :, :].rearrange("p u h t -> p (u h t)")
                        sp.dma_start(dst, m_parts[:, (j0 // NG) % 2, p, :]).then_inc(m_ld, 16)

                sp.wait_ge(memset_done, 1)
                for j in range(RING - 1):
                    if j == 0:
                        load_stack(0, 0)
                        load_v(0, 0)
                    else:
                        load_stack(0, j)
                send_max(0, 0)

                def body(it, first, last):
                    for j in range(RING):
                        b, jb, g = it * NBS + j // NG, j // NG, j % NG
                        if unit_exists(j + RING - 1, last):
                            if begun((it * RING + j) * KT):
                                sp.wait_ge(av_done, (it * RING + j) * KT)
                            load_stack(it + (j + RING - 1) // RING, (j + RING - 1) % RING)
                        if g == 0 and unit_exists(j + NG, last):
                            if begun(b):
                                sp.wait_ge(v_placed, b)
                            load_v(b + 1, jb + 1)
                        if g == 0:
                            if begun(b - 1):
                                sp.wait_ge(y_done, b - 1)
                            load_x(b, jb)
                        if g == NG - 1 and unit_exists(j + 1, last):
                            send_max(b + 1, j + 1)

                rounds(sp, body)

            @block.tensor
            def _(pe):
                pe.wait_ge(const_ld, 16 * (4 + 2 * PROJ))

                def scores(it, j, tt, heads):
                    s = j % RING
                    u = (it + j // RING) * RING + j % RING
                    for h in heads:
                        if tt == 0 and h == 0:
                            pe.wait_ge(stack_ld[s], 96 * (it + j // RING + 1))
                        n = u * (G * KT) + tt * G + h
                        if begun(n - 1):
                            pe.wait_ge(max_done, n - 1)
                        nc.tensor.matmul(s1_ps[:, (tt * G + h) % 2, :],
                                         q_st[0:MROW, s, h, tt * P:(tt + 1) * P],
                                         k_st[0:MROW, s, h, :], start=True, stop=True).then_inc(s1_full, 1)

                def scores_t(it, j, st, pair):
                    s, u = j % RING, it * RING + j
                    if st == 0 and pair == 0:
                        pe.wait_ge(m_ld, 16 * MPARTS * (it * NBS + j // NG + 1))
                    if begun((u * KT + st) * 2 + pair - 1):
                        pe.wait_ge(exp_done, (u * KT + st) * 2 + pair - 1)
                    for i in range(2):
                        h = pair * 2 + i
                        mm = nc.tensor.matmul(st_ps[:, pair, i, :],
                                              k_st[0:MROW + MPARTS, s, h, st * P:(st + 1) * P],
                                              q_st[0:MROW + MPARTS, s, h, :], start=True, stop=True)
                    mm.then_inc(st_full, 1)

                def values(it, j, st):
                    u = it * RING + j
                    n = u * KT + st
                    if st == 0:
                        pe.wait_ge(v_placed, it * NBS + j // NG + 1)
                        if begun(u):
                            pe.wait_ge(o_copied, u)
                    pe.wait_ge(exp_done, 2 * (n + 1))
                    for h in range(G):
                        mm = nc.tensor.matmul(o_ps[32 * h:32 * h + 32, :],
                                              v_aug[:, (j // NG) % NBS, st, (j % NG) * G + h, :],
                                              probs[:, st % 2, h, :], start=(st == 0), stop=(st == KT - 1),
                                              skip_group_check=True)
                    mm.then_inc(av_done, 1)

                def transpose_max(b, i):
                    pe.wait_ge(max_done, (b + 1) * NG * G * KT)
                    if begun(b - 1):
                        pe.wait_ge(o_normed, b - 1)
                    pe.sem_inc(passed_pe, 1)
                    nc.tensor.transpose(misc_ps[0:H * KT, 0:P], maxes[:, i % 2, :], ident[:, :]
                                        ).then_inc(mT_full, 1)

                def select(b, i, sel, done):
                    for g in range(NG):
                        mm = nc.tensor.matmul(misc_ps[g * G * C:(g + 1) * G * C, :], sel[:, :],
                                              o_raw[:, i % 2, g, :], start=True, stop=True,
                                              skip_group_check=True)
                    mm.then_inc(done, 1)

                def select_sums(b, i, more):
                    pe.wait_ge(o_copied, (b + 1) * NG)
                    if begun(more):
                        pe.wait_ge(m_step, more)
                    if PROJ:
                        if begun(b):
                            pe.wait_ge(y_done, b)
                    else:
                        if begun(b):
                            pe.wait_ge(o_normed, b)
                    select(b, i, sel_s, sums_full)

                def select_o(b, i):
                    pe.wait_ge(recip_done, b + 1)
                    select(b, i, sel_o, o_full)

                def project(b, more):
                    pe.wait_ge(o_normed, b + 1)
                    if begun(more):
                        pe.wait_ge(m_step, more)
                    nc.tensor.matmul(misc_ps[:, :], wo[:, :], o_norm[:, :], start=True, stop=True
                                     ).then_inc(proj_full, 1)

                for j in range(AHEAD):
                    for tt in range(KT):
                        scores(0, j, tt, range(G))
                    if j == NG - 1:
                        transpose_max(0, 0)

                def body(it, first, last):
                    for j in range(RING):
                        b, jb, g = it * NBS + j // NG, j // NG, j % NG
                        finish = not (first and jb == 0)
                        more = unit_exists(j - g + NG, last)
                        for st in range(KT):
                            ahead = unit_exists(j + AHEAD, last)
                            for pair in range(2):
                                if ahead:
                                    scores(it, j + AHEAD, st, [pair])
                                scores_t(it, j, st, pair)
                            if ahead:
                                scores(it, j + AHEAD, st, [2])
                            if st > 0:
                                values(it, j, st - 1)
                            elif not (first and j == 0):
                                if j == 0:
                                    values(it - 1, RING - 1, KT - 1)
                                else:
                                    values(it, j - 1, KT - 1)
                            if ahead:
                                scores(it, j + AHEAD, st, [3])
                            if finish and g == 0 and st == 2:
                                select_sums(b - 1, jb + 1, 5 * (b + 1))
                            if finish and g == 1 and st == 0:
                                select_o(b - 1, jb + 1)
                            if more and g == NG - 1 and st == 1:
                                transpose_max(b + 1, jb + 1)
                            if PROJ and finish and g == NG - 1 and st == 3:
                                project(b - 1, 5 * (b + 2) if more else 0)

                rounds(pe, body)
                values(UNITS // RING - 1, RING - 1, KT - 1)
                select_sums(B - 1, B - 1, 0)
                select_o(B - 1, B - 1)
                if PROJ:
                    project(B - 1, 0)

            @block.scalar
            def _(act):
                def exps(it, j, st):
                    for pair in range(2):
                        n = (it * RING + j) * KT + st
                        act.wait_ge(st_full, 2 * n + pair + 1)
                        if begun(n - 1):
                            act.wait_ge(av_done, n - 1)
                        nc.scalar.activation(probs[:, st % 2, 2 * pair:2 * pair + 2, :],
                                             st_ps[:, pair, :, :], ACT.Exp).then_inc(exp_done, 1)

                def copy_o(it, j):
                    u, b = it * RING + j, it * NBS + j // NG
                    act.wait_ge(av_done, (u + 1) * KT)
                    if begun(b - 1):
                        act.wait_ge(o_full, b - 1)
                    nc.scalar.activation(o_raw[:, (j // NG) % 2, j % NG, :], o_ps[:, :], ACT.Copy
                                         ).then_inc(o_copied, 1)

                def body(it, first, last):
                    for j in range(RING):
                        for st in range(KT):
                            exps(it, j, st)
                            if st == 0 and not (first and j == 0):
                                if j == 0:
                                    copy_o(it - 1, RING - 1)
                                else:
                                    copy_o(it, j - 1)

                rounds(act, body)
                copy_o(UNITS // RING - 1, RING - 1)

            @block.vector
            def _(dve):
                op = nc.vector.memset(k_st[MROW:MROW + MPARTS, :, :, :].rearrange("p u h t -> p (u h t)"), 1.0)
                if ROWS < MROW:
                    for st in (q_st, k_st):
                        flat = st[:, :, :, :].rearrange("p u h t -> p (u h t)").bitcast(U32)
                        for r in range(ROWS // 32 * 32, MROW, 32):
                            op = nc.vector.memset(flat[r:r + 32, :], 0)
                op.then_inc(memset_done, 1)
                dve.wait_ge(const_ld, 16 * (4 + 2 * PROJ))

                def row_max(it, j, tt, h):
                    u = (it + j // RING) * RING + j % RING
                    n = u * (G * KT) + tt * G + h
                    jb, g = j // NG, j % NG
                    if tt == 0 and h == 0 and g == 0:
                        if begun((it * NBS + jb) - 1):
                            dve.wait_ge(mT_full, (it * NBS + jb) - 1)
                    dve.wait_ge(s1_full, n + 1)
                    c = (g * G + h) * KT + tt
                    nc.vector.reduce_max(maxes[:, jb % 2, c:c + 1], s1_ps[:, (tt * G + h) % 2, :], AX.X
                                         ).then_inc(max_done, 1)

                def split_max(b, i):
                    dve.wait_ge(mT_full, b + 1)
                    if begun(16 * MPARTS * (b - 1)):
                        dve.wait_ge(m_ld, 16 * MPARTS * (b - 1))
                    out = m_parts[:, i % 2, :, :]
                    nc.vector.tensor_scalar(m_neg[:, :], misc_ps[0:H * KT, 0:P], -1.0, None, ALU.mult
                                            ).then_inc(m_step, 1)
                    dve.wait_ge(m_step, b * 5 + 1)
                    nc.vector.tensor_copy(out[:, 0, :], m_neg[:, :]).then_inc(m_step, 1)
                    dve.wait_ge(m_step, b * 5 + 2)
                    nc.vector.tensor_tensor(m_rest[:, :], m_neg[:, :], out[:, 0, :], ALU.subtract
                                            ).then_inc(m_step, 1)
                    dve.wait_ge(m_step, b * 5 + 3)
                    nc.vector.tensor_copy(out[:, 1, :], m_rest[:, :]).then_inc(m_step, 1)
                    dve.wait_ge(m_step, b * 5 + 4)
                    nc.vector.tensor_tensor(out[:, 2, :], m_rest[:, :], out[:, 1, :], ALU.subtract
                                            ).then_inc(m_step, 1)

                def recip_chunk(b, c):
                    if c == 0:
                        dve.wait_ge(sums_full, b + 1)
                        if begun(b):
                            dve.wait_ge(o_normed, b)
                    r = nc.vector.reciprocal(recip[:, c * P:(c + 1) * P], misc_ps[:, c * P:(c + 1) * P])
                    if c == KT - 1:
                        r.then_inc(recip_done, 1)

                def norm_o(b):
                    dve.wait_ge(o_full, b + 1)
                    dve.wait_ge(recip_done, b + 1)
                    if PROJ:
                        if begun(b):
                            dve.wait_ge(proj_full, b)
                    nc.vector.tensor_tensor(o_norm[:, :], misc_ps[:, :], recip[:, :], ALU.mult
                                            ).then_inc(o_normed, 1)

                def layer_norm(b, i, rnd):
                    dve.wait_ge(x_ld[i % 2], 16 * (rnd + 1))
                    if begun(b):
                        dve.wait_ge(x_done, b)
                    if PROJ:
                        dve.wait_ge(proj_full, b + 1)
                        nc.vector.scalar_tensor_tensor(out=y[:, :], in0=misc_ps[:, :], scalar=bo[:, 0:1],
                                                       in1=x_res[:, i % 2, :], op0=ALU.add, op1=ALU.add
                                                       ).then_inc(y_done, 1)
                    else:
                        dve.wait_ge(o_normed, b + 1)
                        nc.vector.tensor_tensor(y[:, :], o_norm[:, :], x_res[:, i % 2, :], ALU.add
                                                ).then_inc(y_done, 1)
                    dve.wait_ge(y_done, b + 1)
                    nc.vector.bn_stats(stats[:, :], y[:, :]).then_inc(ln_step, 1)
                    dve.wait_ge(ln_step, b * 3 + 1)
                    dve.sem_inc(passed_dve, 1)
                    nc.vector.bn_aggr(mv[:, :], stats[:, :]).then_inc(ln_step, 1)
                    dve.wait_ge(ln_step, b * 3 + 2)
                    nc.vector.tensor_scalar(var_eps[:, :], mv[:, 1:2], LN_EPS, None, ALU.add).then_inc(ln_step, 1)

                def finish_norm(b, i, rnd):
                    dve.wait_ge(rstd_done, b + 1)
                    if begun(16 * rnd):
                        dve.wait_ge(x_stored[i % 2], 16 * rnd)
                    nc.vector.tensor_scalar(x_new[:, i % 2, :], y[:, :], mv[:, 0:1], rstd[:, 0:1],
                                            ALU.subtract, ALU.mult).then_inc(x_done, 1)

                for j in range(AHEAD):
                    for tt in range(KT):
                        for h in range(G):
                            row_max(0, j, tt, h)
                        if j == NG and tt == 0:
                            split_max(0, 0)

                def rnd_of(it, jb):
                    return it * (NBS // 2) + jb // 2

                def body(it, first, last):
                    for j in range(RING):
                        b, jb, g = it * NBS + j // NG, j // NG, j % NG
                        finish = not (first and jb == 0)
                        more = unit_exists(j - g + NG, last)
                        prev = (it, jb - 1) if jb else (it - 1, NBS - 1)
                        for tt in range(KT):
                            for h in range(G):
                                if unit_exists(j + AHEAD, last):
                                    row_max(it, j + AHEAD, tt, h)
                                if finish and g == 0 and tt >= 2 and h % 2 == 1:
                                    recip_chunk(b - 1, (tt - 2) * 2 + h // 2)
                            if finish and g == 1 and tt == 0:
                                norm_o(b - 1)
                                if not PROJ:
                                    layer_norm(b - 1, jb + 1, rnd_of(*prev))
                            if more and g == NG - 1 and tt == 1:
                                split_max(b + 1, jb + 1)
                            if finish and not PROJ and g == 1 and tt == 2:
                                finish_norm(b - 1, jb + 1, rnd_of(*prev))
                            if finish and PROJ and g == NG - 1 and tt == 3:
                                layer_norm(b - 1, jb + 1, rnd_of(*prev))
                                finish_norm(b - 1, jb + 1, rnd_of(*prev))

                rounds(dve, body)
                for c in range(KT):
                    recip_chunk(B - 1, c)
                norm_o(B - 1)
                layer_norm(B - 1, B - 1, B // 2 - 1)
                finish_norm(B - 1, B - 1, B // 2 - 1)

            @block.gpsimd
            def _(pool):
                for c in range(NBS):
                    op = nc.gpsimd.memset(v_aug[:, c, :, :, :], 1.0)
                op.then_inc(ones_done, 1)
                pool.wait_ge(ones_done, 1)
                pool.wait_ge(const_ld, 16 * (4 + 2 * PROJ))

                def place_v(it, jb):
                    b = it * NBS + jb
                    pool.wait_ge(v_ld[jb % 2], 16 * (it * (NBS // 2) + jb // 2 + 1))
                    if begun((b - NBS + 1) * NG * KT):
                        pool.wait_ge(av_done, (b - NBS + 1) * NG * KT)
                    pool.sem_inc(passed_pool, 1)
                    for kt in range(KT):
                        op = nc.gpsimd.tensor_copy(v_aug[:, jb % NBS, kt, :, 0:C],
                                                   v_raw[:, jb % 2, kt, :].rearrange("p (h c) -> p h c", c=C))
                    op.then_inc(v_placed, 1)

                def power(b, i, rnd):
                    pool.wait_ge(ln_step, (b + 1) * 3)
                    nc.gpsimd.tensor_tensor(rstd[:, :], var_eps[:, :], minus_half[:, :], ALU.pow
                                            ).then_inc(rstd_done, 1)
                    pool.wait_ge(x_done, b + 1)
                    pool.dma_start(x_out[bass.ds(b, 1), :, :].rearrange("o p t -> p (o t)"),
                                   x_new[:, i % 2, :]).then_inc(x_stored[i % 2], 16)

                place_v(0, 0)

                def body(it, first, last):
                    for jb in range(NBS):
                        if not (last and jb == NBS - 1):
                            if jb == NBS - 1:
                                place_v(it + 1, 0)
                            else:
                                place_v(it, jb + 1)
                        if not (first and jb == 0):
                            pit, pj = (it, jb - 1) if jb else (it - 1, NBS - 1)
                            power(it * NBS + jb - 1, jb + 1, pit)

                rounds(pool, body)
                power(B - 1, B - 1, 0)
                pool.wait_ge(x_stored[0], 16 * (B // 2))
                pool.wait_ge(x_stored[1], 16 * (B // 2))


def prepare(nc, tag, kind, H, q_parts, k_parts, x_in, ctx_in=None, v_out=None, w=None, perm_d=None,
            cos_d=None, sin_d=None, bias_d=None, v_bias_d=None, q_scale=None):
    L = 512
    C = P // H
    KC = P if kind == "gqa" else L
    W = L + KC
    ROPE = kind != "plain"
    DK = D // P
    with Phase(nc) as ph:
        sem, sb = ph.sem, ph.sb
        n_const = 0
        if ROPE:
            perm = sb(f"{tag}_perm", [P, P])
            cos = sb(f"{tag}_cos", [P, W])
            sin = sb(f"{tag}_sin", [P, W])
            consts = [(perm, perm_d), (cos, cos_d), (sin, sin_d)]
            raw = sb(f"{tag}_raw", [P, 2, W])
            times_cos = sb(f"{tag}_times_cos", [P, 2, W])
            times_sin = sb(f"{tag}_times_sin", [P, 2, W])
            v_sb = sb(f"{tag}_v_sb", [P, 2, KC])
        else:
            consts = []
        if kind == "gqa":
            wq = sb(f"{tag}_wq", [P, DK, D])
            wk = sb(f"{tag}_wk", [P, DK, P])
            wv = sb(f"{tag}_wv", [P, DK, P])
            consts += [(wq, w[0]), (wk, w[1]), (wv, w[2])]
            xin = sb(f"{tag}_xin", [P, 2, DK, P])
        else:
            xin = sb(f"{tag}_xin", [P, 2, L])
            cin = sb(f"{tag}_cin", [P, 2, L])
        if kind == "cross":
            wq = sb(f"{tag}_wq", [P, P])
            wk = sb(f"{tag}_wk", [P, P])
            wv = sb(f"{tag}_wv", [P, P])
            bias = sb(f"{tag}_bias", [P, 2])
            v_bias = sb(f"{tag}_v_bias", [P, L])
            consts += [(wq, w[0]), (wk, w[1]), (wv, w[2]), (bias, bias_d), (v_bias, v_bias_d)]
        whole = sb(f"{tag}_whole", [P, 2, W])
        rest = sb(f"{tag}_rest", [P, 2, W])
        part = sb(f"{tag}_part", [P, 2, 3, W], BF16)
        if ROPE:
            qk_ps = ph.ps(f"{tag}_qk_ps", [P, 2, L])
            v_ps = ph.ps(f"{tag}_v_ps", [P, L])
            sw_ps = ph.ps(f"{tag}_sw_ps", [P, 2, 2, L])

        const_ld = sem(f"{tag}_const_ld")
        x_ld = [sem(f"{tag}_x_ld{i}") for i in range(2)]
        stored = [sem(f"{tag}_stored{i}") for i in range(2)]
        v_stored = [sem(f"{tag}_v_stored{i}") for i in range(2)]
        qk_full = sem(f"{tag}_qk_full")
        v_full = sem(f"{tag}_v_full")
        raw_done = sem(f"{tag}_raw_done")
        v_done = sem(f"{tag}_v_done")
        swapped = sem(f"{tag}_swapped")
        cos_done = sem(f"{tag}_cos_done")
        sin_done = sem(f"{tag}_sin_done")
        whole_done = sem(f"{tag}_whole_done")
        part1 = sem(f"{tag}_part1")
        rest_done = sem(f"{tag}_rest_done")
        part2 = sem(f"{tag}_part2")
        part3 = sem(f"{tag}_part3")

        def pairs(eng, body):
            body(0, 0)
            body(1, 1)
            with eng.Fori(1, B // 2) as it:
                body(it * 2, 0)
                body(it * 2 + 1, 1)

        with nc.Block() as block:
            @block.sync
            def _(sp):
                for dst, src in consts:
                    if len(dst.shape) == 3:
                        sp.dma_start(dst[:, :, :], src).then_inc(const_ld, 16)
                    else:
                        sp.dma_start(dst[:, :], src).then_inc(const_ld, 16)

                def store(b, i):
                    if ROPE:
                        sp.wait_ge(v_done, b + 1)
                        if kind == "gqa":
                            sp.dma_start(v_out[bass.ds(b, 1), :, :].rearrange("o t c -> t (o c)"), v_sb[:, i, :]
                                         ).then_inc(v_stored[i], 16)
                        else:
                            sp.dma_start(v_out[bass.ds(b, 1), :, :].rearrange("o (k p) c -> p (o k) c", p=P),
                                         v_sb[:, i, :].rearrange("p (k c) -> p k c", c=P)
                                         ).then_inc(v_stored[i], 16)
                    sp.wait_ge(part3, b + 1)
                    for out, c0, n in ((q_parts, 0, L), (k_parts, L, KC)):
                        for p in range(3):
                            dst = out[bass.ds(b, 1), p * C:(p + 1) * C, :].rearrange("o c (h t) -> (o h) c t", t=n)
                            sp.dma_start(dst, part[:, i, p, c0:c0 + n]).then_inc(stored[i], 16)

                pairs(sp, store)
                for i in range(2):
                    sp.wait_ge(stored[i], 96 * (B // 2))
                    if ROPE:
                        sp.wait_ge(v_stored[i], 16 * (B // 2))

            def in_loaded(eng, b, i):
                n = 16 if kind == "gqa" else 32
                eng.wait_ge(x_ld[i], (b - i) * (n // 2) + n)

            if ROPE:
                @block.tensor
                def _(pe):
                    pe.wait_ge(const_ld, 16 * len(consts))

                    def project(b, i):
                        in_loaded(pe, b, i)
                        if begun(b):
                            pe.wait_ge(raw_done, b)
                        if kind == "gqa":
                            for f in range(5):
                                for dk in range(DK):
                                    lhs = wq[:, dk, f * P:(f + 1) * P] if f < 4 else wk[:, dk, :]
                                    dst = qk_ps[:, 0, f * P:(f + 1) * P] if f < 4 else qk_ps[:, 1, 0:P]
                                    mm = nc.tensor.matmul(dst, lhs, xin[:, i, dk, :], start=(dk == 0),
                                                          stop=(dk == DK - 1), skip_group_check=True)
                            mm.then_inc(qk_full, 1)
                            if begun(b):
                                pe.wait_ge(v_done, b)
                            for dk in range(DK):
                                mm = nc.tensor.matmul(v_ps[:, 0:P], xin[:, i, dk, :], wv[:, dk, :],
                                                      start=(dk == 0), stop=(dk == DK - 1))
                            mm.then_inc(v_full, 1)
                        else:
                            nc.tensor.matmul(qk_ps[:, 0, :], wq[:, :], xin[:, i, :], start=True, stop=True)
                            nc.tensor.matmul(qk_ps[:, 1, :], wk[:, :], cin[:, i, :], start=True, stop=True
                                             ).then_inc(qk_full, 1)
                            if begun(b):
                                pe.wait_ge(v_done, b)
                            for kt in range(L // P):
                                mm = nc.tensor.matmul(v_ps[:, kt * P:(kt + 1) * P], cin[:, i, kt * P:(kt + 1) * P],
                                                      wv[:, :], start=True, stop=True, skip_group_check=True)
                            mm.then_inc(v_full, 1)

                    def swap(b, i):
                        pe.wait_ge(raw_done, b + 1)
                        if begun(b - 1):
                            pe.wait_ge(sin_done, b - 1)
                        nc.tensor.matmul(sw_ps[:, i, 0, :], perm[:, :], raw[:, i, 0:L], start=True, stop=True)
                        nc.tensor.matmul(sw_ps[:, i, 1, 0:KC], perm[:, :], raw[:, i, L:W], start=True, stop=True
                                         ).then_inc(swapped, 1)

                    project(0, 0)

                    def body(b, i):
                        project(b + 1, 1 - i)
                        swap(b, i)

                    body(0, 0)
                    body(1, 1)
                    with pe.Fori(1, B // 2 - 1) as it:
                        body(it * 2, 0)
                        body(it * 2 + 1, 1)
                    body(B - 2, 0)
                    swap(B - 1, 1)

            @block.scalar
            def _(act):
                if begun(16 * len(consts)):
                    act.wait_ge(const_ld, 16 * len(consts))

                def load(b, i):
                    if begun(b - 1):
                        act.wait_ge(v_full if ROPE else whole_done, b - 1)
                    if kind == "gqa":
                        act.dma_start(xin[:, i, :, :], x_in[bass.ds(b, 1), :, :, :].rearrange("o p k t -> p (o k) t")
                                     ).then_inc(x_ld[i], 16)
                    else:
                        act.dma_start(xin[:, i, :], x_in[bass.ds(b, 1), :, :].rearrange("o p t -> p (o t)")
                                     ).then_inc(x_ld[i], 16)
                        act.dma_start(cin[:, i, :], ctx_in[bass.ds(b, 1), :, :].rearrange("o p t -> p (o t)")
                                     ).then_inc(x_ld[i], 16)

                def first(b, i):
                    if kind == "plain":
                        in_loaded(act, b, i)
                        if begun(b - 1):
                            act.wait_ge(part3, b - 1)
                        nc.scalar.activation(whole[:, i, 0:L], xin[:, i, :], ACT.Copy, scale=q_scale)
                        nc.scalar.activation(whole[:, i, L:W], cin[:, i, :], ACT.Copy).then_inc(whole_done, 1)
                        return
                    act.wait_ge(qk_full, b + 1)
                    if begun(b - 1):
                        act.wait_ge(swapped, b - 1)
                    if begun(b - 1):
                        act.wait_ge(cos_done, b - 1)
                    if kind == "gqa":
                        nc.scalar.activation(raw[:, i, :], qk_ps[:, :, :].rearrange("p a t -> p (a t)")[:, 0:W],
                                             ACT.Copy).then_inc(raw_done, 1)
                        act.wait_ge(v_full, b + 1)
                        if begun((b - i) * 8):
                            act.wait_ge(v_stored[i], (b - i) * 8)
                        nc.scalar.activation(v_sb[:, i, :], v_ps[:, 0:P], ACT.Copy).then_inc(v_done, 1)
                    else:
                        nc.scalar.activation(raw[:, i, 0:L], qk_ps[:, 0, :], ACT.Identity, bias=bias[:, 0:1])
                        nc.scalar.activation(raw[:, i, L:W], qk_ps[:, 1, :], ACT.Identity, bias=bias[:, 1:2]
                                             ).then_inc(raw_done, 1)

                def second(b, i):
                    act.wait_ge(whole_done, b + 1)
                    if begun((b - i) * 48):
                        act.wait_ge(stored[i], (b - i) * 48)
                    nc.scalar.activation(part[:, i, 0, :], whole[:, i, :], ACT.Copy).then_inc(part1, 1)
                    act.wait_ge(rest_done, b + 1)
                    nc.scalar.activation(part[:, i, 1, :], rest[:, i, :], ACT.Copy).then_inc(part2, 1)

                load(0, 0)
                load(1, 1)
                first(0, 0)

                def body(b, i):
                    load(b + 2, i)
                    first(b + 1, 1 - i)
                    second(b, i)

                body(0, 0)
                body(1, 1)
                with act.Fori(1, B // 2 - 1) as it:
                    body(it * 2, 0)
                    body(it * 2 + 1, 1)
                first(B - 1, 1)
                second(B - 2, 0)
                second(B - 1, 1)

            @block.vector
            def _(dve):
                if ROPE:
                    dve.wait_ge(const_ld, 16 * len(consts))

                def rope(b, i):
                    if kind == "cross":
                        dve.wait_ge(v_full, b + 1)
                        if begun((b - i) * 8):
                            dve.wait_ge(v_stored[i], (b - i) * 8)
                        nc.vector.tensor_tensor(v_sb[:, i, :], v_ps[:, :], v_bias[:, :], ALU.add).then_inc(v_done, 1)
                    dve.wait_ge(swapped, b + 1)
                    nc.vector.tensor_tensor(times_sin[:, i, :], sw_ps[:, i, :, :].rearrange("p a t -> p (a t)")[:, 0:W],
                                            sin[:, :], ALU.mult).then_inc(sin_done, 1)
                    dve.wait_ge(sin_done, b + 1)
                    dve.wait_ge(cos_done, b + 1)
                    if begun(b - 1):
                        dve.wait_ge(part3, b - 1)
                    nc.vector.tensor_tensor(whole[:, i, :], times_cos[:, i, :], times_sin[:, i, :], ALU.add
                                            ).then_inc(whole_done, 1)

                def subtract(b, i):
                    dve.wait_ge(part1, b + 1)
                    if not ROPE:
                        dve.wait_ge(whole_done, b + 1)
                    nc.vector.tensor_tensor(rest[:, i, :], whole[:, i, :], part[:, i, 0, :], ALU.subtract
                                            ).then_inc(rest_done, 1)

                def body(b, i):
                    if ROPE:
                        rope(b, i)
                    subtract(b, i)

                pairs(dve, body)

            @block.gpsimd
            def _(pool):
                if begun(16 * len(consts)):
                    pool.wait_ge(const_ld, 16 * len(consts))

                def cosines(b, i):
                    pool.wait_ge(raw_done, b + 1)
                    if begun(b - 1):
                        pool.wait_ge(whole_done, b - 1)
                    nc.gpsimd.tensor_tensor(times_cos[:, i, :], raw[:, i, :], cos[:, :], ALU.mult).then_inc(cos_done, 1)

                def last_part(b, i):
                    pool.wait_ge(part2, b + 1)
                    nc.gpsimd.tensor_tensor(part[:, i, 2, :], rest[:, i, :], part[:, i, 1, :], ALU.subtract
                                            ).then_inc(part3, 1)

                if ROPE:
                    cosines(0, 0)

                def body(b, i):
                    if ROPE:
                        cosines(b + 1, 1 - i)
                    last_part(b, i)

                body(0, 0)
                body(1, 1)
                with pool.Fori(1, B // 2 - 1) as it:
                    body(it * 2, 0)
                    body(it * 2 + 1, 1)
                body(B - 2, 0)
                last_part(B - 1, 1)


def causal_gqa(nc, tag, H, x_in, q_parts, k_parts, v_rows, x_out, ident_d, sel_o_d, sel_s_d,
               half_d, ident_bf_d, mask_d, mask_t_d, wo_d, bo_d):
    C = P // H
    I = 4
    L = I * P
    G = 4
    NG = H // G
    UNITS = B * NG
    RING = 8
    NBS = RING // NG
    AHEAD = NG + 1
    MROW, MPARTS = 96, 3
    NCONST = 9

    with Phase(nc) as ph:
        sem, sb = ph.sem, ph.sb
        q_st = sb(f"{tag}_q_st", [P, RING, G, L], BF16)
        k_st = sb(f"{tag}_k_st", [P, RING, G, P], BF16)
        v_raw = sb(f"{tag}_v_raw", [P, 2, P])
        v_aug = sb(f"{tag}_v_aug", [P, NBS, H, 32])
        probs = sb(f"{tag}_probs", [P, 2, G, L])
        o_raw = sb(f"{tag}_o_raw", [P, 2, NG, L])
        maxes = sb(f"{tag}_maxes", [P, 2, H * I])
        m_neg = sb(f"{tag}_m_neg", [H * I, P])
        m_rest = sb(f"{tag}_m_rest", [H * I, P])
        m_parts = sb(f"{tag}_m_parts", [H * I, 2, MPARTS, P], BF16)
        recip = sb(f"{tag}_recip", [P, L])
        o_norm = sb(f"{tag}_o_norm", [P, L])
        x_res = sb(f"{tag}_x_res", [P, 2, D])
        x_bias = sb(f"{tag}_x_bias", [P, D])
        y = sb(f"{tag}_y", [P, D])
        stats = sb(f"{tag}_stats", [P, 6])
        mv = sb(f"{tag}_mv", [P, 2])
        var_eps = sb(f"{tag}_var_eps", [P, 1])
        rstd = sb(f"{tag}_rstd", [P, 1])
        x_new = sb(f"{tag}_x_new", [P, 2, D])
        ident = sb(f"{tag}_ident", [P, P])
        ident_bf = sb(f"{tag}_ident_bf", [P, P], BF16)
        mask = sb(f"{tag}_mask", [P, P], BF16)
        mask_t = sb(f"{tag}_mask_t", [P, P], BF16)
        sel_o = sb(f"{tag}_sel_o", [P, G * C])
        sel_s = sb(f"{tag}_sel_s", [P, G * C])
        minus_half = sb(f"{tag}_minus_half", [P, 1])
        wo = sb(f"{tag}_wo", [P, I, D])
        bo = sb(f"{tag}_bo", [P, D])

        s1_ps = ph.ps(f"{tag}_s1", [P, 2, L])
        st_ps = ph.ps(f"{tag}_st", [P, 2, 2, L])
        o_ps = ph.ps(f"{tag}_o", [P, L])
        misc_ps = ph.ps(f"{tag}_misc", [P, L])

        const_ld = sem(f"{tag}_const_ld")
        passed_dve = sem(f"{tag}_passed_dve")
        passed_pool = sem(f"{tag}_passed_pool")
        memset_done = sem(f"{tag}_memset_done")
        ones_done = sem(f"{tag}_ones_done")
        stack_ld = [sem(f"{tag}_stack_ld{i}") for i in range(RING)]
        v_ld = [sem(f"{tag}_v_ld{i}") for i in range(2)]
        v_placed = sem(f"{tag}_v_placed")
        x_ld = [sem(f"{tag}_x_ld{i}") for i in range(2)]
        x_biased = sem(f"{tag}_x_biased")
        s1_full = sem(f"{tag}_s1_full")
        max_done = sem(f"{tag}_max_done")
        st_full = sem(f"{tag}_st_full")
        exp_done = sem(f"{tag}_exp_done")
        av_done = sem(f"{tag}_av_done")
        o_copied = sem(f"{tag}_o_copied")
        sums_full = sem(f"{tag}_sums_full")
        recip_done = sem(f"{tag}_recip_done")
        o_full = sem(f"{tag}_o_full")
        o_normed = sem(f"{tag}_o_normed")
        proj_full = sem(f"{tag}_proj_full")
        mT_full = sem(f"{tag}_mT_full")
        m_step = sem(f"{tag}_m_step")
        m_ld = sem(f"{tag}_m_ld")
        y_done = sem(f"{tag}_y_done")
        ln_step = sem(f"{tag}_ln_step")
        rstd_done = sem(f"{tag}_rstd_done")
        x_done = sem(f"{tag}_x_done")
        x_stored = [sem(f"{tag}_x_stored{i}") for i in range(2)]

        def rounds(eng, body):
            body(0, True, False)
            with eng.Fori(1, UNITS // RING - 1) as it:
                body(it, False, False)
            body(UNITS // RING - 1, False, True)

        def unit_exists(u_off, last):
            return not (last and u_off >= RING)

        with nc.Block() as block:
            @block.sync
            def _(sp):
                for dst, src in ((ident, ident_d), (sel_o, sel_o_d), (sel_s, sel_s_d), (minus_half, half_d),
                                 (ident_bf, ident_bf_d), (mask, mask_d), (mask_t, mask_t_d), (bo, bo_d)):
                    sp.dma_start(dst[:, :], src).then_inc(const_ld, 16)
                sp.dma_start(wo[:, :, :], wo_d).then_inc(const_ld, 16)

                def load_stack(it, j):
                    b, g, s = it * NBS + j // NG, j % NG, j % RING

                    def parts(src, p, n, width):
                        heads = slice(g * G * width, (g + 1) * G * width)
                        return src[bass.ds(b, 1), p * C:(p + n) * C, heads].rearrange("o c t -> (o c) t")

                    row = 0
                    for n in (3, 2, 1):
                        sp.dma_start(q_st[row:row + n * C, s, :, :].rearrange("p h t -> p (h t)"),
                                     parts(q_parts, 0, n, L)).then_inc(stack_ld[s], 16)
                        a = parts(k_parts, 3 - n, 1, P)
                        a = bass.AP(a.tensor, a.offset, [[0, n]] + [list(x) for x in a.ap])
                        sp.dma_start(k_st[row:row + n * C, s, :, :].rearrange("p h t -> p (h t)"),
                                     a).then_inc(stack_ld[s], 16)
                        row += n * C

                def load_v(b, i):
                    sp.dma_start(v_raw[:, i % 2, :], v_rows[bass.ds(b, 1), :, :].rearrange("o p c -> p (o c)")
                                 ).then_inc(v_ld[i % 2], 16)

                def load_x(b, i):
                    sp.dma_start(x_res[:, i % 2, :], x_in[bass.ds(b, 1), :, :].rearrange("o p t -> p (o t)")
                                 ).then_inc(x_ld[i % 2], 16)

                def send_max(b, j0):
                    sp.wait_ge(m_step, (b + 1) * 5)
                    s0 = j0 % RING
                    for p in range(MPARTS):
                        dst = q_st[MROW + p:MROW + p + 1, s0:s0 + NG, :, :].rearrange("p u h t -> p (u h t)")
                        sp.dma_start(dst, m_parts[:, (j0 // NG) % 2, p, :]).then_inc(m_ld, 16)

                sp.wait_ge(memset_done, 1)
                load_stack(0, 0)
                load_v(0, 0)
                for j in range(1, RING - 1):
                    load_stack(0, j)
                send_max(0, 0)

                def body(it, first, last):
                    for j in range(RING):
                        b, jb, g = it * NBS + j // NG, j // NG, j % NG
                        if unit_exists(j + RING - 1, last):
                            if begun(it * RING + j):
                                sp.wait_ge(av_done, it * RING + j)
                            load_stack(it + (j + RING - 1) // RING, (j + RING - 1) % RING)
                        if g == 0 and unit_exists(j + NG, last):
                            if begun(b):
                                sp.wait_ge(v_placed, b)
                            load_v(b + 1, jb + 1)
                        if g == 0:
                            if begun(b - 1):
                                sp.wait_ge(x_biased, b - 1)
                            load_x(b, jb)
                        if g == NG - 1 and unit_exists(j + 1, last):
                            send_max(b + 1, j + 1)

                rounds(sp, body)

            @block.tensor
            def _(pe):
                pe.wait_ge(const_ld, 16 * NCONST)

                def scores(it, j, h):
                    s = j % RING
                    n = ((it + j // RING) * RING + j % RING) * G + h
                    if h == 0:
                        pe.wait_ge(stack_ld[s], 96 * (it + j // RING + 1))
                    if begun(n - 1):
                        pe.wait_ge(max_done, n - 1)
                    nc.tensor.matmul(s1_ps[:, h % 2, :].rearrange("p (i s) -> p i s", i=I), ident_bf[:, :],
                                     mask[:, :].rearrange("p (o s) -> p o s", o=1).to_broadcast([P, I, P]),
                                     start=True, stop=False, skip_group_check=True)
                    for i in range(I):
                        mm = nc.tensor.matmul(s1_ps[:, h % 2, i * P:(i + 1) * P],
                                              q_st[0:MROW, s, h, i * P:(i + 1) * P],
                                              k_st[0:MROW, s, h, :], start=False, stop=(i == I - 1),
                                              skip_group_check=True)
                    mm.then_inc(s1_full, 1)

                def scores_t(it, j, pair):
                    s, u = j % RING, it * RING + j
                    if pair == 0:
                        pe.wait_ge(m_ld, 16 * MPARTS * (it * NBS + j // NG + 1))
                    if begun(u * 2 + pair - 1):
                        pe.wait_ge(exp_done, u * 2 + pair - 1)
                    for i in range(2):
                        h = pair * 2 + i
                        nc.tensor.matmul(st_ps[:, pair, i, :],
                                         k_st[0:MROW + MPARTS, s, h, :],
                                         q_st[0:MROW + MPARTS, s, h, :], start=True, stop=False)
                        mm = nc.tensor.matmul(st_ps[:, pair, i, :].rearrange("p (i t) -> p i t", i=I),
                                              ident_bf[:, :],
                                              mask_t[:, :].rearrange("p (o s) -> p o s", o=1).to_broadcast([P, I, P]),
                                              start=False, stop=True)
                    mm.then_inc(st_full, 1)

                def values(it, j):
                    u = it * RING + j
                    pe.wait_ge(v_placed, it * NBS + j // NG + 1)
                    if begun(u):
                        pe.wait_ge(o_copied, u)
                    pe.wait_ge(exp_done, 2 * (u + 1))
                    for h in range(G):
                        mm = nc.tensor.matmul(o_ps[32 * h:32 * h + 32, :],
                                              v_aug[:, (j // NG) % NBS, (j % NG) * G + h, :],
                                              probs[:, j % 2, h, :], start=True, stop=True,
                                              skip_group_check=True)
                    mm.then_inc(av_done, 1)

                def transpose_max(b, i):
                    pe.wait_ge(max_done, (b + 1) * NG * G)
                    if begun(b - 1):
                        pe.wait_ge(o_normed, b - 1)
                    nc.tensor.transpose(misc_ps[0:H * I, 0:P], maxes[:, i % 2, :], ident[:, :]
                                        ).then_inc(mT_full, 1)

                def select(b, i, sel, done):
                    for g in range(NG):
                        mm = nc.tensor.matmul(misc_ps[g * G * C:(g + 1) * G * C, :], sel[:, :],
                                              o_raw[:, i % 2, g, :], start=True, stop=True,
                                              skip_group_check=True)
                    mm.then_inc(done, 1)

                def select_sums(b, i, more):
                    pe.wait_ge(o_copied, (b + 1) * NG)
                    if begun(more):
                        pe.wait_ge(m_step, more)
                    if begun(b):
                        pe.wait_ge(y_done, b)
                    select(b, i, sel_s, sums_full)

                def select_o(b, i):
                    pe.wait_ge(recip_done, b + 1)
                    select(b, i, sel_o, o_full)

                def project(b, more):
                    pe.wait_ge(o_normed, b + 1)
                    if begun(more):
                        pe.wait_ge(m_step, more)
                    for i in range(I):
                        mm = nc.tensor.matmul(misc_ps[:, :], o_norm[:, i * P:(i + 1) * P], wo[:, i, :],
                                              start=(i == 0), stop=(i == I - 1))
                    mm.then_inc(proj_full, 1)

                for j in range(AHEAD):
                    for h in range(G):
                        scores(0, j, h)
                    if j == NG - 1:
                        transpose_max(0, 0)

                def body(it, first, last):
                    for j in range(RING):
                        b, jb, g = it * NBS + j // NG, j // NG, j % NG
                        finish = not (first and jb == 0)
                        more = unit_exists(j - g + NG, last)
                        ahead = unit_exists(j + AHEAD, last)
                        for pair in range(2):
                            if ahead:
                                scores(it, j + AHEAD, pair)
                            scores_t(it, j, pair)
                        if ahead:
                            scores(it, j + AHEAD, 2)
                        if finish and g == 1:
                            select_o(b - 1, jb + 1)
                        if j > 0:
                            values(it, j - 1)
                        elif not first:
                            values(it - 1, RING - 1)
                        if ahead:
                            scores(it, j + AHEAD, 3)
                        if finish and g == 0:
                            select_sums(b - 1, jb + 1, 5 * (b + 1))
                        if more and g == NG - 1:
                            transpose_max(b + 1, jb + 1)
                        if finish and g == NG - 1:
                            project(b - 1, 5 * (b + 2) if more else 0)

                rounds(pe, body)
                values(UNITS // RING - 1, RING - 1)
                select_sums(B - 1, B - 1, 0)
                select_o(B - 1, B - 1)
                project(B - 1, 0)

            @block.scalar
            def _(act):
                def exps(it, j):
                    u = it * RING + j
                    for pair in range(2):
                        act.wait_ge(st_full, 2 * u + pair + 1)
                        if begun(u - 1):
                            act.wait_ge(av_done, u - 1)
                        nc.scalar.activation(probs[:, j % 2, 2 * pair:2 * pair + 2, :],
                                             st_ps[:, pair, :, :], ACT.Exp).then_inc(exp_done, 1)

                def copy_o(it, j):
                    u, b = it * RING + j, it * NBS + j // NG
                    act.wait_ge(av_done, u + 1)
                    if begun(b - 1):
                        act.wait_ge(o_full, b - 1)
                    nc.scalar.activation(o_raw[:, (j // NG) % 2, j % NG, :], o_ps[:, :], ACT.Copy
                                         ).then_inc(o_copied, 1)

                def body(it, first, last):
                    for j in range(RING):
                        exps(it, j)
                        if j > 0:
                            copy_o(it, j - 1)
                        elif not first:
                            copy_o(it - 1, RING - 1)

                rounds(act, body)
                copy_o(UNITS // RING - 1, RING - 1)

            @block.vector
            def _(dve):
                nc.vector.memset(k_st[MROW:MROW + MPARTS, :, :, :].rearrange("p u h t -> p (u h t)"), 1.0
                                 ).then_inc(memset_done, 1)
                dve.wait_ge(const_ld, 16 * NCONST)

                def row_max(it, j, h):
                    n = ((it + j // RING) * RING + j % RING) * G + h
                    jb, g = j // NG, j % NG
                    if h == 0 and g == 0:
                        if begun((it * NBS + jb) - 1):
                            dve.wait_ge(mT_full, (it * NBS + jb) - 1)
                    dve.wait_ge(s1_full, n + 1)
                    c = (g * G + h) * I
                    nc.vector.tensor_reduce(maxes[:, jb % 2, c:c + I],
                                            s1_ps[:, h % 2, :].rearrange("p (i s) -> p i s", i=I), AX.X, ALU.max
                                            ).then_inc(max_done, 1)

                def split_max(b, i):
                    dve.wait_ge(mT_full, b + 1)
                    if begun(16 * MPARTS * (b - 1)):
                        dve.wait_ge(m_ld, 16 * MPARTS * (b - 1))
                    out = m_parts[:, i % 2, :, :]
                    nc.vector.tensor_scalar(m_neg[:, :], misc_ps[0:H * I, 0:P], -1.0, None, ALU.mult
                                            ).then_inc(m_step, 1)
                    dve.wait_ge(m_step, b * 5 + 1)
                    nc.vector.tensor_copy(out[:, 0, :], m_neg[:, :]).then_inc(m_step, 1)
                    dve.wait_ge(m_step, b * 5 + 2)
                    nc.vector.tensor_tensor(m_rest[:, :], m_neg[:, :], out[:, 0, :], ALU.subtract
                                            ).then_inc(m_step, 1)
                    dve.wait_ge(m_step, b * 5 + 3)
                    nc.vector.tensor_copy(out[:, 1, :], m_rest[:, :]).then_inc(m_step, 1)
                    dve.wait_ge(m_step, b * 5 + 4)
                    nc.vector.tensor_tensor(out[:, 2, :], m_rest[:, :], out[:, 1, :], ALU.subtract
                                            ).then_inc(m_step, 1)

                def recip_chunk(b, c):
                    if c == 0:
                        dve.wait_ge(sums_full, b + 1)
                        if begun(b):
                            dve.wait_ge(o_normed, b)
                    r = nc.vector.reciprocal(recip[:, c * P:(c + 1) * P], misc_ps[:, c * P:(c + 1) * P])
                    if c == I - 1:
                        r.then_inc(recip_done, 1)

                def norm_o(b):
                    dve.wait_ge(o_full, b + 1)
                    dve.wait_ge(recip_done, b + 1)
                    if begun(b):
                        dve.wait_ge(proj_full, b)
                    nc.vector.tensor_tensor(o_norm[:, :], misc_ps[:, :], recip[:, :], ALU.mult
                                            ).then_inc(o_normed, 1)

                def layer_norm(b):
                    dve.wait_ge(proj_full, b + 1)
                    dve.wait_ge(x_biased, b + 1)
                    if begun(b):
                        dve.wait_ge(x_done, b)
                    nc.vector.tensor_tensor(y[:, :], misc_ps[:, :], x_bias[:, :], ALU.add).then_inc(y_done, 1)
                    dve.wait_ge(y_done, b + 1)
                    nc.vector.bn_stats(stats[:, :], y[:, :]).then_inc(ln_step, 1)
                    dve.wait_ge(ln_step, b * 3 + 1)
                    dve.sem_inc(passed_dve, 1)
                    nc.vector.bn_aggr(mv[:, :], stats[:, :]).then_inc(ln_step, 1)
                    dve.wait_ge(ln_step, b * 3 + 2)
                    nc.vector.tensor_scalar(var_eps[:, :], mv[:, 1:2], LN_EPS, None, ALU.add).then_inc(ln_step, 1)

                def finish_norm(b, i, rnd):
                    dve.wait_ge(rstd_done, b + 1)
                    if begun(16 * rnd):
                        dve.wait_ge(x_stored[i % 2], 16 * rnd)
                    nc.vector.tensor_scalar(x_new[:, i % 2, :], y[:, :], mv[:, 0:1], rstd[:, 0:1],
                                            ALU.subtract, ALU.mult).then_inc(x_done, 1)

                for j in range(AHEAD):
                    for h in range(G):
                        row_max(0, j, h)
                    if j == NG:
                        split_max(0, 0)

                def rnd_of(it, jb):
                    return it * (NBS // 2) + jb // 2

                def body(it, first, last):
                    for j in range(RING):
                        b, jb, g = it * NBS + j // NG, j // NG, j % NG
                        finish = not (first and jb == 0)
                        more = unit_exists(j - g + NG, last)
                        prev = (it, jb - 1) if jb else (it - 1, NBS - 1)
                        if finish and g == 0 and not (first and jb == 1):
                            back = (it, jb - 2) if jb > 1 else (it - 1, NBS - 2 + jb)
                            finish_norm(b - 2, jb, rnd_of(*back))
                        for h in range(G):
                            if unit_exists(j + AHEAD, last):
                                row_max(it, j + AHEAD, h)
                            if finish and g == 1 and h < 2:
                                for c in range(2):
                                    recip_chunk(b - 1, 2 * h + c)
                        if finish and g == 1:
                            norm_o(b - 1)
                        if more and g == NG - 1:
                            split_max(b + 1, jb + 1)
                        if finish and g == NG - 1:
                            layer_norm(b - 1)

                rounds(dve, body)
                finish_norm(B - 2, 0, B // 2 - 1)
                for c in range(I):
                    recip_chunk(B - 1, c)
                norm_o(B - 1)
                layer_norm(B - 1)
                finish_norm(B - 1, 1, B // 2 - 1)

            @block.gpsimd
            def _(pool):
                nc.gpsimd.memset(v_aug[:, :, :, :], 1.0).then_inc(ones_done, 1)
                pool.wait_ge(ones_done, 1)
                pool.wait_ge(const_ld, 16 * NCONST)

                def place_v(it, jb):
                    b = it * NBS + jb
                    pool.wait_ge(v_ld[jb % 2], 16 * (it * (NBS // 2) + jb // 2 + 1))
                    if begun((b - NBS + 1) * NG):
                        pool.wait_ge(av_done, (b - NBS + 1) * NG)
                    pool.sem_inc(passed_pool, 1)
                    nc.gpsimd.tensor_copy(v_aug[:, jb % NBS, :, 0:C],
                                          v_raw[:, jb % 2, :].rearrange("p (h c) -> p h c", c=C)
                                          ).then_inc(v_placed, 1)

                def add_bias(b, i, rnd):
                    pool.wait_ge(x_ld[i % 2], 16 * (rnd + 1))
                    if begun(b):
                        pool.wait_ge(y_done, b)
                    nc.gpsimd.tensor_tensor(x_bias[:, :], x_res[:, i % 2, :], bo[:, :], ALU.add
                                            ).then_inc(x_biased, 1)

                def power(b, i):
                    pool.wait_ge(ln_step, (b + 1) * 3)
                    nc.gpsimd.tensor_tensor(rstd[:, :], var_eps[:, :], minus_half[:, :], ALU.pow
                                            ).then_inc(rstd_done, 1)
                    pool.wait_ge(x_done, b + 1)
                    pool.dma_start(x_out[bass.ds(b, 1), :, :].rearrange("o p t -> p (o t)"),
                                   x_new[:, i % 2, :]).then_inc(x_stored[i % 2], 16)

                place_v(0, 0)

                def rnd_of(it, jb):
                    return it * (NBS // 2) + jb // 2

                def body(it, first, last):
                    for jb in range(NBS):
                        if not (last and jb == NBS - 1):
                            if jb == NBS - 1:
                                place_v(it + 1, 0)
                            else:
                                place_v(it, jb + 1)
                        if not (first and jb == 0):
                            pit, pj = (it, jb - 1) if jb else (it - 1, NBS - 1)
                            add_bias(it * NBS + jb - 1, jb + 1, rnd_of(pit, pj))
                            power(it * NBS + jb - 1, jb + 1)

                rounds(pool, body)
                add_bias(B - 1, B - 1, B // 2 - 1)
                power(B - 1, B - 1)
                pool.wait_ge(x_stored[0], 16 * (B // 2))
                pool.wait_ge(x_stored[1], 16 * (B // 2))


RMS_EPS = 1e-6
HEADS, HD = 16, 32
DK = D // P
NJ = P // HD


def batches(eng, body):
    body(0, 0)
    body(1, 1)
    with eng.Fori(1, B // 2 - 1) as it:
        body(it * 2, 0)
        body(it * 2 + 1, 1)
    body(B - 2, 0)
    body(B - 1, 1)


def before(b, n):
    return not isinstance(b, int) or b + n < B


def gate_attention(nc, tag, x_in, h_t_out, mod_out, wq_d, wk_d, wv_d, wo_d, a_d, ln_d, ident_d, half_d,
                   ident_bf_d, mask_d, mask_t_d):
    R = 16
    SCALE = HD ** -0.5
    with Phase(nc) as ph:
        sem, sb = ph.sem, ph.sb
        wq = sb(f"{tag}_wq", [P, DK, D])
        wk = sb(f"{tag}_wk", [P, DK, D])
        wv = sb(f"{tag}_wv", [P, DK, D])
        wo = sb(f"{tag}_wo", [P, DK, D])
        a_w = sb(f"{tag}_a", [P, DK, R])
        ln_w = sb(f"{tag}_ln_w", [P, 2, DK])
        ident = sb(f"{tag}_ident", [P, P])
        minus_half = sb(f"{tag}_minus_half", [P, 1])
        ident_bf = sb(f"{tag}_ident_bf", [P, P], BF16)
        mask = sb(f"{tag}_mask", [P, P], BF16)
        mask_t = sb(f"{tag}_mask_t", [P, P], BF16)
        wo_a = sb(f"{tag}_wo_a", [P, DK, R])
        ones = sb(f"{tag}_ones", [P, HD])
        ones_bf = sb(f"{tag}_ones_bf", [3, P], BF16)
        x = sb(f"{tag}_x", [P, 2, D])
        squares = sb(f"{tag}_squares", [P, D])
        sumsq = sb(f"{tag}_sumsq", [P, 1])
        mean_eps = sb(f"{tag}_mean_eps", [P, 1])
        rstd = sb(f"{tag}_rstd", [P, 1])
        x_rms = sb(f"{tag}_x_rms", [P, 2, D])
        x1_t = sb(f"{tag}_x1_t", [P, 2, DK, P])
        h_t = sb(f"{tag}_h_t", [P, 2, DK, P])
        q_own = sb(f"{tag}_q_own", [P, 2, DK, NJ, P])
        k_t = sb(f"{tag}_k_t", [P, 2, DK, P])
        v = sb(f"{tag}_v", [P, 2, D])
        maxes = sb(f"{tag}_maxes", [P, 2, HEADS])
        m_neg = sb(f"{tag}_m_neg", [HEADS, P])
        m_rest = sb(f"{tag}_m_rest", [HEADS, P])
        m_parts = sb(f"{tag}_m_parts", [HEADS, 3, P], BF16)
        m_row = sb(f"{tag}_m_row", [3, 2, HEADS * P], BF16)
        probs = sb(f"{tag}_probs", [P, 2, DK, NJ, P])
        recip = sb(f"{tag}_recip", [P, D])
        o_norm = sb(f"{tag}_o_norm", [P, D])
        mod = sb(f"{tag}_mod", [R, 2, P])

        proj_ps = ph.ps(f"{tag}_proj", [P, 2, D])
        s1_ps = ph.ps(f"{tag}_s1", [P, 2, D])
        st_ps = ph.ps(f"{tag}_st", [P, 2, D])
        o_ps = ph.ps(f"{tag}_o", [P, D])
        misc_ps = ph.ps(f"{tag}_misc", [P, D])

        const_ld = sem(f"{tag}_const_ld")
        x_ld = [sem(f"{tag}_x_ld{i}") for i in range(2)]
        h_stored = [sem(f"{tag}_h_stored{i}") for i in range(2)]
        mod_stored = [sem(f"{tag}_mod_stored{i}") for i in range(2)]
        names = ("zeros wo_a_full wo_a_done sumsq_done mean_done rstd_done rms_done tr_full x1_done h_done q_full "
                 "q_done_act q_done_dve k_full k_done v_full v_done s1_full max_done mT_full m_step m_ld st_full "
                 "exp_done o_full sums_full recip_done o_normed mod_full mod_done").split()
        (zeros, wo_a_full, wo_a_done, sumsq_done, mean_done, rstd_done, rms_done, tr_full, x1_done, h_done, q_full,
         q_done_act, q_done_dve, k_full, k_done, v_full, v_done, s1_full, max_done, mT_full, m_step, m_ld, st_full,
         exp_done, o_full, sums_full, recip_done, o_normed, mod_full, mod_done) = [sem(f"{tag}_{n}") for n in names]
        NCONST = 11

        def bcast(m):
            return m[:, :].rearrange("p (o s) -> p o s", o=1).to_broadcast([P, NJ, P])

        with nc.Block() as block:
            @block.sync
            def _(sp):
                for dst, src in ((wq, wq_d), (wk, wk_d), (wv, wv_d), (wo, wo_d), (a_w, a_d), (ln_w, ln_d)):
                    sp.dma_start(dst[:, :, :], src).then_inc(const_ld, 16)
                for dst, src in ((ident, ident_d), (minus_half, half_d), (ident_bf, ident_bf_d), (mask, mask_d),
                                 (mask_t, mask_t_d)):
                    sp.dma_start(dst[:, :], src).then_inc(const_ld, 16)

                def load(b, i):
                    if begun(b - 1):
                        sp.wait_ge(rms_done, b - 1)
                    sp.dma_start(x[:, i, :], x_in[bass.ds(b, 1), :, :].rearrange("o p t -> p (o t)")
                                 ).then_inc(x_ld[i], 16)

                def store_h(b, i):
                    sp.wait_ge(h_done, b + 1)
                    sp.dma_start(h_t_out[bass.ds(b, 1), :, :, :].rearrange("o p k t -> p (o k) t"),
                                 h_t[:, i, :, :]).then_inc(h_stored[i], 16)

                def send_max(b, i):
                    sp.wait_ge(m_step, 5 * (b + 1))
                    for p in range(3):
                        sp.dma_start(m_row[p:p + 1, i, :], m_parts[:, p, :]).then_inc(m_ld, 16)

                def store_mod(b, i):
                    sp.wait_ge(mod_done, b + 1)
                    sp.dma_start(mod_out[bass.ds(b, 1), :, :].rearrange("o r t -> r (o t)"), mod[:, i, :]
                                 ).then_inc(mod_stored[i], 16)

                load(0, 0)
                load(1, 1)
                load(2, 0)
                store_h(0, 0)
                send_max(0, 0)

                def body(b, i):
                    if before(b, 1):
                        store_h(b + 1, 1 - i)
                    if before(b, 3):
                        load(b + 3, 1 - i)
                    store_mod(b, i)
                    if before(b, 1):
                        send_max(b + 1, 1 - i)

                body(0, 0)
                body(1, 1)
                with sp.Fori(1, B // 2 - 2) as it:
                    body(it * 2, 0)
                    body(it * 2 + 1, 1)
                for b in range(B - 4, B):
                    body(b, b % 2)
                for i in range(2):
                    sp.wait_ge(h_stored[i], 16 * (B // 2))
                    sp.wait_ge(mod_stored[i], 16 * (B // 2))

            @block.tensor
            def _(pe):
                pe.wait_ge(const_ld, 16 * NCONST)
                for f in range(DK):
                    for dk in range(DK):
                        mm = nc.tensor.matmul(misc_ps[:, f * R:(f + 1) * R], wo[:, dk, f * P:(f + 1) * P],
                                              a_w[:, dk, :], start=(dk == 0), stop=(dk == DK - 1),
                                              skip_group_check=True)
                mm.then_inc(wo_a_full, 1)
                pe.wait_ge(zeros, 2)

                def transposes(b, i):
                    pe.wait_ge(rms_done, b + 1)
                    if begun(b):
                        pe.wait_ge(k_done, b)
                    for dk in range(DK):
                        mm = nc.tensor.transpose(proj_ps[:, 0, dk * P:(dk + 1) * P], x_rms[:, i, dk * P:(dk + 1) * P],
                                                 ident[:, :])
                    mm.then_inc(tr_full, 1)

                def project_t(b, i, w, bank, done):
                    for f in range(DK):
                        for dk in range(DK):
                            mm = nc.tensor.matmul(proj_ps[:, bank, f * P:(f + 1) * P], w[:, dk, f * P:(f + 1) * P],
                                                  x1_t[:, i, dk, :], start=(dk == 0), stop=(dk == DK - 1),
                                                  skip_group_check=True)
                    mm.then_inc(done, 1)

                def project_q(b, i):
                    pe.wait_ge(x1_done, b + 1)
                    if begun(b):
                        pe.wait_ge(v_done, b)
                    project_t(b, i, wq, 1, q_full)

                def project_k(b, i):
                    pe.wait_ge(h_done, b + 1)
                    project_t(b, i, wk, 0, k_full)

                def project_v(b, i):
                    pe.wait_ge(q_done_act, b + 1)
                    pe.wait_ge(q_done_dve, b + 1)
                    for dk in range(DK):
                        mm = nc.tensor.matmul(proj_ps[:, 1, :], x1_t[:, i, dk, :], wv[:, dk, :], start=(dk == 0),
                                              stop=(dk == DK - 1))
                    mm.then_inc(v_full, 1)

                def scores(b, i):
                    pe.wait_ge(k_done, b + 1)
                    for f in range(DK):
                        if begun(b * DK + f - 1):
                            pe.wait_ge(max_done, b * DK + f - 1)
                        nc.tensor.matmul(s1_ps[:, f % 2, :].rearrange("p (i s) -> p i s", i=NJ), ident_bf[:, :],
                                         bcast(mask), start=True, stop=False, skip_group_check=True)
                        for j in range(NJ):
                            mm = nc.tensor.matmul(s1_ps[:, f % 2, j * P:(j + 1) * P], q_own[:, i, f, j, :],
                                                  k_t[:, i, f, :], start=False, stop=(j == NJ - 1),
                                                  skip_group_check=True)
                        mm.then_inc(s1_full, 1)

                def transpose_max(b, i):
                    pe.wait_ge(max_done, (b + 1) * DK)
                    if begun(b):
                        pe.wait_ge(mod_done, b)
                    nc.tensor.transpose(misc_ps[0:HEADS, 0:P], maxes[:, i, :], ident[:, :]).then_inc(mT_full, 1)

                def scores_t(b, i, f):
                    if f == 0:
                        pe.wait_ge(m_ld, 48 * (b + 1))
                    if begun(b * DK + f - 1):
                        pe.wait_ge(exp_done, b * DK + f - 1)
                    nc.tensor.matmul(st_ps[:, f % 2, :], k_t[:, i, f, :],
                                     q_own[:, i, f, :, :].rearrange("p j t -> p (j t)"), start=True, stop=False)
                    nc.tensor.matmul(st_ps[:, f % 2, :].rearrange("p (i s) -> p i s", i=NJ), ident_bf[:, :],
                                     bcast(mask_t), start=False, stop=False)
                    nc.tensor.matmul(st_ps[:, f % 2, :], ones_bf[:, :], m_row[:, i, f * D:(f + 1) * D],
                                     start=False, stop=True).then_inc(st_full, 1)

                def values(b, i):
                    pe.wait_ge(v_done, b + 1)
                    pe.wait_ge(exp_done, (b + 1) * DK)
                    if begun(b):
                        pe.wait_ge(o_normed, b)
                    for f in range(DK):
                        for j in range(NJ):
                            mm = nc.tensor.matmul(o_ps[HD * j:HD * j + HD, f * P:(f + 1) * P],
                                                  v[:, i, (f * NJ + j) * HD:(f * NJ + j + 1) * HD],
                                                  probs[:, i, f, j, :], start=True, stop=True, skip_group_check=True)
                    mm.then_inc(o_full, 1)
                    pe.wait_ge(m_step, 5 * (b + 1))
                    for j in range(NJ):
                        mm = nc.tensor.matmul(misc_ps[HD * j:HD * j + HD, :].rearrange("p (f t) -> p f t", f=DK),
                                              ones[:, :], probs[:, i, :, j, :], start=True, stop=True,
                                              skip_group_check=True)
                    mm.then_inc(sums_full, 1)

                def modulate(b, i):
                    pe.wait_ge(wo_a_done, 1)
                    pe.wait_ge(o_normed, b + 1)
                    for f in range(DK):
                        mm = nc.tensor.matmul(misc_ps[0:R, 0:P], wo_a[:, f, :], o_norm[:, f * P:(f + 1) * P],
                                              start=(f == 0), stop=(f == DK - 1))
                    mm.then_inc(mod_full, 1)

                transposes(0, 0)
                project_q(0, 0)
                project_k(0, 0)
                project_v(0, 0)
                scores(0, 0)
                pe.wait_ge(wo_a_done, 1)
                transpose_max(0, 0)

                def body(b, i):
                    more = before(b, 1)
                    if more:
                        transposes(b + 1, 1 - i)
                        project_q(b + 1, 1 - i)
                    scores_t(b, i, 0)
                    scores_t(b, i, 1)
                    if more:
                        project_k(b + 1, 1 - i)
                    scores_t(b, i, 2)
                    scores_t(b, i, 3)
                    if more:
                        project_v(b + 1, 1 - i)
                    values(b, i)
                    if more:
                        scores(b + 1, 1 - i)
                    modulate(b, i)
                    if more:
                        transpose_max(b + 1, 1 - i)

                batches(pe, body)

            @block.scalar
            def _(act):
                def norm(b, i):
                    act.wait_ge(x_ld[i], (b - i) * 8 + 16)
                    if begun(b):
                        act.wait_ge(mean_done, b)
                    nc.scalar.activation(squares[:, :], x[:, i, :], ACT.Square, accum_out=sumsq[:, :]
                                         ).then_inc(sumsq_done, 1)
                    act.wait_ge(rstd_done, b + 1)
                    if begun(b - 1):
                        act.wait_ge(tr_full, b - 1)
                    nc.scalar.activation(x_rms[:, i, :], x[:, i, :], ACT.Copy, scale=rstd[:, 0:1]
                                         ).then_inc(rms_done, 1)

                def take_q(b, i):
                    act.wait_ge(q_full, b + 1)
                    if begun((b - 1) * DK):
                        act.wait_ge(st_full, (b - 1) * DK)
                    for j in range(2):
                        op = nc.scalar.activation(q_own[HD * j:HD * j + HD, i, :, j, :],
                                                  proj_ps[HD * j:HD * j + HD, 1, :].rearrange("p (f t) -> p f t", f=DK),
                                                  ACT.Copy, scale=SCALE)
                    op.then_inc(q_done_act, 1)

                def take_k(b, i):
                    act.wait_ge(k_full, b + 1)
                    if begun((b - 1) * DK):
                        act.wait_ge(st_full, (b - 1) * DK)
                    nc.scalar.activation(k_t[:, i, :, :].rearrange("p f t -> p (f t)"), proj_ps[:, 0, :], ACT.Copy
                                         ).then_inc(k_done, 1)

                def take_v(b, i):
                    act.wait_ge(v_full, b + 1)
                    if begun(b - 1):
                        act.wait_ge(o_full, b - 1)
                    nc.scalar.activation(v[:, i, :], proj_ps[:, 1, :], ACT.Copy).then_inc(v_done, 1)

                def exps(b, i, f):
                    act.wait_ge(st_full, b * DK + f + 1)
                    if begun(b - 1):
                        act.wait_ge(sums_full, b - 1)
                    nc.scalar.activation(probs[:, i, f, :, :].rearrange("p j t -> p (j t)"), st_ps[:, f % 2, :],
                                         ACT.Exp).then_inc(exp_done, 1)

                def tanh(b, i):
                    act.wait_ge(mod_full, b + 1)
                    if begun((b - i) * 8):
                        act.wait_ge(mod_stored[i], (b - i) * 8)
                    nc.scalar.activation(mod[:, i, :], misc_ps[0:R, 0:P], ACT.Tanh).then_inc(mod_done, 1)

                act.wait_ge(wo_a_full, 1)
                nc.scalar.activation(wo_a[:, :, :].rearrange("p f r -> p (f r)"), misc_ps[:, 0:DK * R], ACT.Copy
                                     ).then_inc(wo_a_done, 1)
                act.wait_ge(zeros, 2)
                norm(0, 0)
                norm(1, 1)
                take_q(0, 0)
                take_k(0, 0)
                take_v(0, 0)

                def body(b, i):
                    more = before(b, 1)
                    if more:
                        take_q(b + 1, 1 - i)
                    exps(b, i, 0)
                    exps(b, i, 1)
                    if more:
                        take_k(b + 1, 1 - i)
                    exps(b, i, 2)
                    exps(b, i, 3)
                    if more:
                        take_v(b + 1, 1 - i)
                    if before(b, 2):
                        norm(b + 2, i)
                    tanh(b, i)

                batches(act, body)

            @block.vector
            def _(dve):
                nc.vector.memset(ones[:, :], 1.0)
                nc.vector.memset(ones_bf[:, :], 1.0)
                nc.vector.memset(q_own[:, 0, :, :, :], 0.0).then_inc(zeros, 1)
                dve.wait_ge(const_ld, 16 * NCONST)

                def mean(b):
                    dve.wait_ge(sumsq_done, b + 1)
                    if begun(b):
                        dve.wait_ge(rstd_done, b)
                    nc.vector.tensor_scalar(mean_eps[:, :], sumsq[:, :], 1.0 / D, RMS_EPS, ALU.mult, ALU.add
                                            ).then_inc(mean_done, 1)

                def take_x(b, i):
                    dve.wait_ge(tr_full, b + 1)
                    src = proj_ps[:, 0, :].rearrange("p (f t) -> p f t", f=DK)
                    if begun(b - 1):
                        dve.wait_ge(v_full, b - 1)
                    nc.vector.tensor_tensor(x1_t[:, i, :, :], src,
                                            ln_w[:, 0, :].rearrange("p (f o) -> p f o", o=1).to_broadcast([P, DK, P]),
                                            ALU.mult).then_inc(x1_done, 1)
                    if begun((b - i) * 8):
                        dve.wait_ge(h_stored[i], (b - i) * 8)
                    nc.vector.tensor_tensor(h_t[:, i, :, :], src,
                                            ln_w[:, 1, :].rearrange("p (f o) -> p f o", o=1).to_broadcast([P, DK, P]),
                                            ALU.mult).then_inc(h_done, 1)

                def take_q(b, i):
                    dve.wait_ge(q_full, b + 1)
                    if begun((b - 1) * DK):
                        dve.wait_ge(st_full, (b - 1) * DK)
                    for j in range(2, NJ):
                        op = nc.vector.tensor_scalar(q_own[HD * j:HD * j + HD, i, :, j, :],
                                                     proj_ps[HD * j:HD * j + HD, 1, :].rearrange("p (f t) -> p f t", f=DK),
                                                     SCALE, None, ALU.mult)
                    op.then_inc(q_done_dve, 1)

                def row_max(b, i):
                    if begun(b - 1):
                        dve.wait_ge(mT_full, b - 1)
                    for f in range(DK):
                        dve.wait_ge(s1_full, b * DK + f + 1)
                        nc.vector.tensor_reduce(maxes[:, i, f * NJ:(f + 1) * NJ],
                                                s1_ps[:, f % 2, :].rearrange("p (i s) -> p i s", i=NJ), AX.X, ALU.max
                                                ).then_inc(max_done, 1)

                def split_max(b):
                    dve.wait_ge(mT_full, b + 1)
                    if begun(48 * b):
                        dve.wait_ge(m_ld, 48 * b)
                    nc.vector.tensor_scalar(m_neg[:, :], misc_ps[0:HEADS, 0:P], -1.0, None, ALU.mult).then_inc(m_step, 1)
                    dve.wait_ge(m_step, b * 5 + 1)
                    nc.vector.tensor_copy(m_parts[:, 0, :], m_neg[:, :]).then_inc(m_step, 1)
                    dve.wait_ge(m_step, b * 5 + 2)
                    nc.vector.tensor_tensor(m_rest[:, :], m_neg[:, :], m_parts[:, 0, :], ALU.subtract).then_inc(m_step, 1)
                    dve.wait_ge(m_step, b * 5 + 3)
                    nc.vector.tensor_copy(m_parts[:, 1, :], m_rest[:, :]).then_inc(m_step, 1)
                    dve.wait_ge(m_step, b * 5 + 4)
                    nc.vector.tensor_tensor(m_parts[:, 2, :], m_rest[:, :], m_parts[:, 1, :], ALU.subtract
                                            ).then_inc(m_step, 1)

                def normalize(b):
                    dve.wait_ge(sums_full, b + 1)
                    if begun(b):
                        dve.wait_ge(o_normed, b)
                    nc.vector.reciprocal(recip[:, :], misc_ps[:, :]).then_inc(recip_done, 1)
                    dve.wait_ge(recip_done, b + 1)
                    if begun(b):
                        dve.wait_ge(mod_full, b)
                    nc.vector.tensor_tensor(o_norm[:, :], o_ps[:, :], recip[:, :], ALU.mult).then_inc(o_normed, 1)

                mean(0)
                mean(1)
                take_x(0, 0)
                take_q(0, 0)
                row_max(0, 0)
                split_max(0)

                def body(b, i):
                    more = before(b, 1)
                    if more:
                        take_x(b + 1, 1 - i)
                        take_q(b + 1, 1 - i)
                    if before(b, 2):
                        mean(b + 2)
                    normalize(b)
                    if more:
                        row_max(b + 1, 1 - i)
                        split_max(b + 1)

                batches(dve, body)

            @block.gpsimd
            def _(pool):
                nc.gpsimd.memset(q_own[:, 1, :, :, :], 0.0).then_inc(zeros, 1)
                pool.wait_ge(const_ld, 16 * NCONST)

                def body(b, i):
                    pool.wait_ge(mean_done, b + 1)
                    if begun(b):
                        pool.wait_ge(rms_done, b)
                    nc.gpsimd.tensor_tensor(rstd[:, :], mean_eps[:, :], minus_half[:, :], ALU.pow
                                            ).then_inc(rstd_done, 1)

                batches(pool, body)


def squared_attention(nc, tag, x_in, x_out, wq_d, wk_d, wv_d, wo_d, gamma_d, beta_d, ident_d, half_d, keep_t_d):
    NG = 2 * HEADS
    W = 2 * D
    SCALE = HD ** -0.5
    with Phase(nc) as ph:
        sem, sb = ph.sem, ph.sb
        wq = sb(f"{tag}_wq", [P, DK, D])
        wk = sb(f"{tag}_wk", [P, DK, D])
        wv = sb(f"{tag}_wv", [P, DK, D])
        wo = sb(f"{tag}_wo", [P, DK, D])
        gamma = sb(f"{tag}_gamma", [P, HD])
        beta = sb(f"{tag}_beta", [P, HD])
        ident = sb(f"{tag}_ident", [P, P])
        minus_half = sb(f"{tag}_minus_half", [P, NG])
        keep_t = sb(f"{tag}_keep_t", [P, P])
        ones = sb(f"{tag}_ones", [P, HD])
        x = sb(f"{tag}_x", [P, 2, D])
        x_res = sb(f"{tag}_x_res", [P, 2, D])
        x_t = sb(f"{tag}_x_t", [P, DK, P])
        scaled = sb(f"{tag}_scaled", [P, W])
        shifted = sb(f"{tag}_shifted", [P, W])
        group_sum = sb(f"{tag}_group_sum", [P, NG])
        group_mean = sb(f"{tag}_group_mean", [P, NG])
        centred = sb(f"{tag}_centred", [P, W])
        squares = sb(f"{tag}_squares", [P, W])
        group_sq = sb(f"{tag}_group_sq", [P, NG])
        group_var = sb(f"{tag}_group_var", [P, NG])
        group_rstd = sb(f"{tag}_group_rstd", [P, NG])
        qk = sb(f"{tag}_qk", [P, W])
        q_own = sb(f"{tag}_q_own", [P, 2, DK, NJ, P])
        k_t = sb(f"{tag}_k_t", [P, 2, DK, P])
        v = sb(f"{tag}_v", [P, 2, D])
        weights = sb(f"{tag}_weights", [P, DK, NJ, P])
        kept = sb(f"{tag}_kept", [P, 2, DK, NJ, P])
        z_eps = sb(f"{tag}_z_eps", [P, D])
        recip = sb(f"{tag}_recip", [P, D])
        o_norm = sb(f"{tag}_o_norm", [P, D])
        y = sb(f"{tag}_y", [P, D])
        stats = sb(f"{tag}_stats", [P, 6])
        mv = sb(f"{tag}_mv", [P, 2])
        var_eps = sb(f"{tag}_var_eps", [P, 1])
        rstd = sb(f"{tag}_rstd", [P, 1])
        x_new = sb(f"{tag}_x_new", [P, 2, D])

        tr_ps = ph.ps(f"{tag}_tr", [P, D])
        qk_ps = ph.ps(f"{tag}_qk_ps", [P, 2, D])
        v_ps = ph.ps(f"{tag}_v_ps", [P, D])
        st_ps = ph.ps(f"{tag}_st", [P, 2, D])
        o_ps = ph.ps(f"{tag}_o", [P, D])
        misc_ps = ph.ps(f"{tag}_misc", [P, D])

        const_ld = sem(f"{tag}_const_ld")
        passed_dve = sem(f"{tag}_passed_dve")
        x_ld = [sem(f"{tag}_x_ld{i}") for i in range(2)]
        res_ld = [sem(f"{tag}_res_ld{i}") for i in range(2)]
        x_stored = [sem(f"{tag}_x_stored{i}") for i in range(2)]
        names = ("zeros x_tr_full x_t_done qk_full v_full v_done scaled_done shifted_done stat_step sq_done grstd_done "
                 "qk_done q_tr_full q_done_act q_done_dve k_tr_full k_done st_full square_done kept_done o_full "
                 "sums_full z_done recip_done o_normed proj_full y_done ln_step rstd_done x_done").split()
        (zeros, x_tr_full, x_t_done, qk_full, v_full, v_done, scaled_done, shifted_done, stat_step, sq_done, grstd_done,
         qk_done, q_tr_full, q_done_act, q_done_dve, k_tr_full, k_done, st_full, square_done, kept_done, o_full,
         sums_full, z_done, recip_done, o_normed, proj_full, y_done, ln_step, rstd_done, x_done
         ) = [sem(f"{tag}_{n}") for n in names]
        NCONST = 9

        def groups(ap):
            return ap.rearrange("p (g c) -> p g c", c=HD)

        def by_channel(ap):
            return ap.rearrange("p (o c) -> p o c", o=1).to_broadcast([P, NG, HD])

        def by_group(ap):
            return ap.rearrange("p (g o) -> p g o", o=1).to_broadcast([P, NG, HD])

        with nc.Block() as block:
            @block.sync
            def _(sp):
                for dst, src in ((wq, wq_d), (wk, wk_d), (wv, wv_d), (wo, wo_d)):
                    sp.dma_start(dst[:, :, :], src).then_inc(const_ld, 16)
                for dst, src in ((gamma, gamma_d), (beta, beta_d), (ident, ident_d), (minus_half, half_d),
                                 (keep_t, keep_t_d)):
                    sp.dma_start(dst[:, :], src).then_inc(const_ld, 16)

                def load(b, i, dst, done):
                    sp.dma_start(dst[:, i, :], x_in[bass.ds(b, 1), :, :].rearrange("o p t -> p (o t)")
                                 ).then_inc(done[i], 16)

                def store(b, i):
                    sp.wait_ge(x_done, b + 1)
                    sp.dma_start(x_out[bass.ds(b, 1), :, :].rearrange("o p t -> p (o t)"), x_new[:, i, :]
                                 ).then_inc(x_stored[i], 16)

                load(0, 0, x, x_ld)
                load(1, 1, x, x_ld)

                def body(b, i):
                    if before(b, 2):
                        sp.wait_ge(x_tr_full, b + 1)
                        load(b + 2, i, x, x_ld)
                    if begun(b - 1):
                        sp.wait_ge(y_done, b - 1)
                    load(b, i, x_res, res_ld)
                    if not (isinstance(b, int) and b == 0):
                        store(b - 1, 1 - i)

                batches(sp, body)
                store(B - 1, 1)
                for i in range(2):
                    sp.wait_ge(x_stored[i], 16 * (B // 2))

            @block.tensor
            def _(pe):
                pe.wait_ge(const_ld, 16 * NCONST)
                pe.wait_ge(zeros, 2)

                def transpose_x(b, i):
                    pe.wait_ge(x_ld[i], (b - i) * 8 + 16)
                    if begun(b):
                        pe.wait_ge(k_done, b)
                    for dk in range(DK):
                        mm = nc.tensor.transpose(tr_ps[:, dk * P:(dk + 1) * P], x[:, i, dk * P:(dk + 1) * P], ident[:, :])
                    mm.then_inc(x_tr_full, 1)

                def project(dst, w):
                    for dk in range(DK):
                        mm = nc.tensor.matmul(dst, x_t[:, dk, :], w[:, dk, :], start=(dk == 0), stop=(dk == DK - 1))
                    return mm

                def project_qk(b):
                    pe.wait_ge(x_t_done, b + 1)
                    if begun(b):
                        pe.wait_ge(scaled_done, b)
                    project(qk_ps[:, 0, :], wq)
                    project(qk_ps[:, 1, :], wk).then_inc(qk_full, 1)

                def project_v(b):
                    if begun(b):
                        pe.wait_ge(v_done, b)
                    project(v_ps[:, :], wv).then_inc(v_full, 1)

                def transpose_qk(b):
                    pe.wait_ge(qk_done, b + 1)
                    pe.wait_ge(x_t_done, b + 1)
                    for f in range(DK):
                        mm = nc.tensor.transpose(tr_ps[:, f * P:(f + 1) * P], qk[:, f * P:(f + 1) * P], ident[:, :])
                    mm.then_inc(q_tr_full, 1)
                    pe.wait_ge(q_done_act, b + 1)
                    pe.wait_ge(q_done_dve, b + 1)
                    for f in range(DK):
                        mm = nc.tensor.transpose(tr_ps[:, f * P:(f + 1) * P], qk[:, D + f * P:D + (f + 1) * P],
                                                 ident[:, :])
                    mm.then_inc(k_tr_full, 1)

                def products(b, i, f):
                    if f == 0:
                        pe.wait_ge(k_done, b + 1)
                    if begun(b * DK + f - 1):
                        pe.wait_ge(square_done, b * DK + f - 1)
                    nc.tensor.matmul(st_ps[:, f % 2, :], k_t[:, i, f, :],
                                     q_own[:, i, f, :, :].rearrange("p j t -> p (j t)"), start=True, stop=True
                                     ).then_inc(st_full, 1)

                def values(b, i):
                    pe.wait_ge(v_done, b + 1)
                    pe.wait_ge(kept_done, (b + 1) * DK)
                    if begun(b):
                        pe.wait_ge(o_normed, b)
                    for f in range(DK):
                        for j in range(NJ):
                            mm = nc.tensor.matmul(o_ps[HD * j:HD * j + HD, f * P:(f + 1) * P],
                                                  v[:, i, (f * NJ + j) * HD:(f * NJ + j + 1) * HD],
                                                  kept[:, i, f, j, :], start=True, stop=True, skip_group_check=True)
                    mm.then_inc(o_full, 1)
                    if begun(b):
                        pe.wait_ge(y_done, b)
                    for j in range(NJ):
                        mm = nc.tensor.matmul(misc_ps[HD * j:HD * j + HD, :].rearrange("p (f t) -> p f t", f=DK),
                                              ones[:, :], kept[:, i, :, j, :], start=True, stop=True,
                                              skip_group_check=True)
                    mm.then_inc(sums_full, 1)

                def project_o(b):
                    pe.wait_ge(o_normed, b + 1)
                    pe.wait_ge(z_done, b + 1)
                    for f in range(DK):
                        mm = nc.tensor.matmul(misc_ps[:, :], o_norm[:, f * P:(f + 1) * P], wo[:, f, :],
                                              start=(f == 0), stop=(f == DK - 1))
                    mm.then_inc(proj_full, 1)

                transpose_x(0, 0)
                project_qk(0)
                project_v(0)
                transpose_qk(0)

                def body(b, i):
                    more = before(b, 1)
                    if more:
                        transpose_x(b + 1, 1 - i)
                    if not (isinstance(b, int) and b == 0):
                        project_o(b - 1)
                    products(b, i, 0)
                    products(b, i, 1)
                    if more:
                        project_qk(b + 1)
                    products(b, i, 2)
                    products(b, i, 3)
                    if more:
                        project_v(b + 1)
                    values(b, i)
                    if more:
                        transpose_qk(b + 1)

                batches(pe, body)
                project_o(B - 1)

            @block.scalar
            def _(act):
                act.wait_ge(zeros, 2)

                def take_x(b):
                    act.wait_ge(x_tr_full, b + 1)
                    if begun(b):
                        act.wait_ge(v_full, b)
                    nc.scalar.activation(x_t[:, :, :].rearrange("p k t -> p (k t)"), tr_ps[:, :], ACT.Copy
                                         ).then_inc(x_t_done, 1)

                def square(b):
                    act.wait_ge(stat_step, b * 5 + 3)
                    nc.scalar.activation(squares[:, :], centred[:, :], ACT.Square).then_inc(sq_done, 1)

                def take_v(b, i):
                    act.wait_ge(v_full, b + 1)
                    if begun(b - 1):
                        act.wait_ge(o_full, b - 1)
                    nc.scalar.activation(v[:, i, :], v_ps[:, :], ACT.Copy).then_inc(v_done, 1)

                def take_qk(b, i):
                    act.wait_ge(q_tr_full, b + 1)
                    for j in range(2):
                        op = nc.scalar.activation(q_own[HD * j:HD * j + HD, i, :, j, :],
                                                  tr_ps[HD * j:HD * j + HD, :].rearrange("p (f t) -> p f t", f=DK),
                                                  ACT.Copy, scale=SCALE)
                    op.then_inc(q_done_act, 1)
                    act.wait_ge(k_tr_full, b + 1)
                    nc.scalar.activation(k_t[:, i, :, :].rearrange("p f t -> p (f t)"), tr_ps[:, :], ACT.Copy
                                         ).then_inc(k_done, 1)

                def squared(b, f):
                    act.wait_ge(st_full, b * DK + f + 1)
                    if begun((b - 1) * DK + f + 1):
                        act.wait_ge(kept_done, (b - 1) * DK + f + 1)
                    nc.scalar.activation(weights[:, f, :, :].rearrange("p j t -> p (j t)"), st_ps[:, f % 2, :],
                                         ACT.Square).then_inc(square_done, 1)

                take_x(0)
                square(0)
                take_v(0, 0)
                take_qk(0, 0)

                def body(b, i):
                    more = before(b, 1)
                    if more:
                        take_x(b + 1)
                    squared(b, 0)
                    squared(b, 1)
                    squared(b, 2)
                    squared(b, 3)
                    if more:
                        square(b + 1)
                        take_v(b + 1, 1 - i)
                        take_qk(b + 1, 1 - i)

                batches(act, body)

            @block.vector
            def _(dve):
                nc.vector.memset(ones[:, :], 1.0)
                nc.vector.memset(q_own[:, 0, :, :, :], 0.0).then_inc(zeros, 1)
                dve.wait_ge(const_ld, 16 * NCONST)
                dve.wait_ge(zeros, 2)

                def feature_map(b):
                    s = b * 5
                    dve.wait_ge(qk_full, b + 1)
                    if begun(b):
                        dve.wait_ge(shifted_done, b)
                    nc.vector.tensor_tensor(groups(scaled[:, :]), groups(qk_ps[:, :, :].rearrange("p a c -> p (a c)")),
                                            by_channel(gamma[:, :]), ALU.mult).then_inc(scaled_done, 1)
                    dve.wait_ge(shifted_done, b + 1)
                    nc.vector.tensor_reduce(group_sum[:, :], groups(shifted[:, :]), AX.X, ALU.add).then_inc(stat_step, 1)
                    dve.wait_ge(stat_step, s + 1)
                    nc.vector.tensor_scalar(group_mean[:, :], group_sum[:, :], 1.0 / HD, None, ALU.mult
                                            ).then_inc(stat_step, 1)
                    dve.wait_ge(stat_step, s + 2)
                    nc.vector.tensor_tensor(groups(centred[:, :]), groups(shifted[:, :]), by_group(group_mean[:, :]),
                                            ALU.subtract).then_inc(stat_step, 1)
                    dve.wait_ge(sq_done, b + 1)
                    nc.vector.tensor_reduce(group_sq[:, :], groups(squares[:, :]), AX.X, ALU.add).then_inc(stat_step, 1)
                    dve.wait_ge(stat_step, s + 4)
                    nc.vector.tensor_scalar(group_var[:, :], group_sq[:, :], 1.0 / HD, LN_EPS, ALU.mult, ALU.add
                                            ).then_inc(stat_step, 1)
                    dve.wait_ge(grstd_done, b + 1)
                    if begun(b):
                        dve.wait_ge(k_tr_full, b)
                    nc.vector.tensor_tensor(groups(qk[:, :]), groups(centred[:, :]), by_group(group_rstd[:, :]),
                                            ALU.mult).then_inc(qk_done, 1)

                def take_q(b, i):
                    dve.wait_ge(q_tr_full, b + 1)
                    for j in range(2, NJ):
                        op = nc.vector.tensor_scalar(q_own[HD * j:HD * j + HD, i, :, j, :],
                                                     tr_ps[HD * j:HD * j + HD, :].rearrange("p (f t) -> p f t", f=DK),
                                                     SCALE, None, ALU.mult)
                    op.then_inc(q_done_dve, 1)

                def normalize(b):
                    dve.wait_ge(sums_full, b + 1)
                    if begun(b):
                        dve.wait_ge(recip_done, b)
                    nc.vector.tensor_scalar(z_eps[:, :], misc_ps[:, :], LN_EPS, None, ALU.add).then_inc(z_done, 1)
                    dve.wait_ge(z_done, b + 1)
                    if begun(b):
                        dve.wait_ge(o_normed, b)
                    nc.vector.reciprocal(recip[:, :], z_eps[:, :]).then_inc(recip_done, 1)
                    dve.wait_ge(recip_done, b + 1)
                    if begun(b):
                        dve.wait_ge(proj_full, b)
                    nc.vector.tensor_tensor(o_norm[:, :], o_ps[:, :], recip[:, :], ALU.mult).then_inc(o_normed, 1)

                def layer_norm(b, i):
                    dve.wait_ge(proj_full, b + 1)
                    dve.wait_ge(res_ld[i], (b - i) * 8 + 16)
                    if begun(b):
                        dve.wait_ge(x_done, b)
                    nc.vector.tensor_tensor(y[:, :], misc_ps[:, :], x_res[:, i, :], ALU.add).then_inc(y_done, 1)
                    dve.wait_ge(y_done, b + 1)
                    nc.vector.bn_stats(stats[:, :], y[:, :]).then_inc(ln_step, 1)
                    dve.wait_ge(ln_step, b * 3 + 1)
                    dve.sem_inc(passed_dve, 1)
                    nc.vector.bn_aggr(mv[:, :], stats[:, :]).then_inc(ln_step, 1)
                    dve.wait_ge(ln_step, b * 3 + 2)
                    nc.vector.tensor_scalar(var_eps[:, :], mv[:, 1:2], LN_EPS, None, ALU.add).then_inc(ln_step, 1)
                    dve.wait_ge(rstd_done, b + 1)
                    if begun((b - i) * 8):
                        dve.wait_ge(x_stored[i], (b - i) * 8)
                    nc.vector.tensor_scalar(x_new[:, i, :], y[:, :], mv[:, 0:1], rstd[:, 0:1],
                                            ALU.subtract, ALU.mult).then_inc(x_done, 1)

                feature_map(0)
                take_q(0, 0)

                def body(b, i):
                    if not (isinstance(b, int) and b == 0):
                        layer_norm(b - 1, 1 - i)
                    if before(b, 1):
                        feature_map(b + 1)
                    normalize(b)
                    if before(b, 1):
                        take_q(b + 1, 1 - i)

                batches(dve, body)
                layer_norm(B - 1, 1)

            @block.gpsimd
            def _(pool):
                nc.gpsimd.memset(q_own[:, 1, :, :, :], 0.0).then_inc(zeros, 1)
                pool.wait_ge(const_ld, 16 * NCONST)

                def shift(b):
                    pool.wait_ge(scaled_done, b + 1)
                    if begun(b * 5):
                        pool.wait_ge(stat_step, b * 5)
                    nc.gpsimd.tensor_tensor(groups(shifted[:, :]), groups(scaled[:, :]), by_channel(beta[:, :]), ALU.add
                                            ).then_inc(shifted_done, 1)

                def powers(b):
                    pool.wait_ge(stat_step, (b + 1) * 5)
                    if begun(b):
                        pool.wait_ge(qk_done, b)
                    nc.gpsimd.tensor_tensor(group_rstd[:, :], group_var[:, :], minus_half[:, :], ALU.pow
                                            ).then_inc(grstd_done, 1)

                def mask(b, i, f):
                    pool.wait_ge(square_done, b * DK + f + 1)
                    if begun(b - 1):
                        pool.wait_ge(sums_full, b - 1)
                    nc.gpsimd.tensor_tensor(kept[:, i, f, :, :], weights[:, f, :, :],
                                            keep_t[:, :].rearrange("p (o s) -> p o s", o=1).to_broadcast([P, NJ, P]),
                                            ALU.mult).then_inc(kept_done, 1)

                def rsqrt(b):
                    pool.wait_ge(ln_step, (b + 1) * 3)
                    nc.gpsimd.tensor_tensor(rstd[:, :], var_eps[:, :], minus_half[:, 0:1], ALU.pow).then_inc(rstd_done, 1)

                shift(0)
                powers(0)

                def body(b, i):
                    if not (isinstance(b, int) and b == 0):
                        rsqrt(b - 1)
                    mask(b, i, 0)
                    mask(b, i, 1)
                    if before(b, 1):
                        shift(b + 1)
                    mask(b, i, 2)
                    if before(b, 1):
                        powers(b + 1)
                    mask(b, i, 3)

                batches(pool, body)
                rsqrt(B - 1)


TOK = 4
GROUPS = B // TOK
TOPK = 4


def feed_forward(nc, tag, NF, h_t_in, x_in, x_out, w_in_d, w_up_d, w_down_d, half_d, mod_in=None, a_d=None,
                 b_d=None, expert_rows=None, sel_w_d=None, sel_slot_d=None):
    R = 16
    MOD = mod_in is not None
    MOE = expert_rows is not None
    N = TOK * P
    with Phase(nc) as ph:
        sem, sb = ph.sem, ph.sb
        w_in = sb(f"{tag}_w_in", [P, DK, NF * P])
        w_up = sb(f"{tag}_w_up", [P, DK, NF * P])
        w_down = sb(f"{tag}_w_down", [P, NF, D])
        h_t = sb(f"{tag}_h_t", [P, 2, TOK, DK, P])
        x = sb(f"{tag}_x", [P, 2, D])
        gate = sb(f"{tag}_gate", [P, 2, N])
        hidden = sb(f"{tag}_hidden", [P, 2, N])
        y = sb(f"{tag}_y", [P, 2, D])
        minus_half = sb(f"{tag}_minus_half", [P, 1])
        stats = sb(f"{tag}_stats", [P, 6])
        mv = sb(f"{tag}_mv", [P, 2])
        var_eps = sb(f"{tag}_var_eps", [P, 1])
        rstd = sb(f"{tag}_rstd", [P, 1])
        x_new = sb(f"{tag}_x_new", [P, 2, D])
        if MOD:
            a_w = sb(f"{tag}_a_w", [P, DK, R])
            b_w = sb(f"{tag}_b_w", [R, NF * P])
            mod = sb(f"{tag}_mod", [R, 2, N])
            mod_h = sb(f"{tag}_mod_h", [R, N])
        if MOE:
            sel_w = sb(f"{tag}_sel_w", [P, B, TOPK])
            sel_slot = sb(f"{tag}_sel_slot", [P, B * TOPK], U32)
            rows = sb(f"{tag}_rows", [P, 2, TOPK, D])
        gate_ps = ph.ps(f"{tag}_gate_ps", [P, 2, N])
        up_ps = ph.ps(f"{tag}_up_ps", [P, 2, N])
        out_ps = ph.ps(f"{tag}_out_ps", [P, TOK, D])

        w_ld = [sem(f"{tag}_w_ld{i}") for i in range(4)]
        const_ld = sem(f"{tag}_const_ld")
        passed_dve = sem(f"{tag}_passed_dve")
        consts = [(minus_half[:, :], half_d)]
        if MOD:
            consts += [(a_w[:, :, :], a_d), (b_w[:, :], b_d)]
        if MOE:
            consts += [(sel_w[:, :, :], sel_w_d), (sel_slot[:, :], sel_slot_d)]
        CONSTS = 16 * len(consts)
        h_ld = [sem(f"{tag}_h_ld{i}") for i in range(2)]
        x_ld = [sem(f"{tag}_x_ld{i}") for i in range(2)]
        stored = [sem(f"{tag}_stored{i}") for i in range(2)]
        rows_ld = [sem(f"{tag}_rows_ld{i}") for i in range(2)]
        (ha_full, ha_done, gate_full, up_full, silu_done, hidden_done, down_done, out_full, y_done, ln_step, rstd_done,
         x_done, rows_done) = [sem(f"{tag}_{n}") for n in ("ha_full ha_done gate_full up_full silu_done hidden_done down_done "
                                                "out_full y_done ln_step rstd_done x_done rows_done").split()]
        FQ = NF // 4

        def groups(eng, body):
            body(0, 0)
            body(1, 1)
            with eng.Fori(1, GROUPS // 2) as it:
                body(it * 2, 0)
                body(it * 2 + 1, 1)

        with nc.Block() as block:
            @block.sync
            def _(sp):
                def load_h(g, i):
                    for t in range(TOK):
                        sp.dma_start(h_t[:, i, t, :, :],
                                     h_t_in[bass.ds(g * TOK + t, 1), :, :, :].rearrange("o p k t -> p (o k) t")
                                     ).then_inc(h_ld[i], 16)
                        if MOD:
                            sp.dma_start(mod[:, i, t * P:(t + 1) * P],
                                         mod_in[bass.ds(g * TOK + t, 1), :, :].rearrange("o r t -> r (o t)")
                                         ).then_inc(h_ld[i], 16)

                for dst, src in consts:
                    sp.dma_start(dst, src).then_inc(const_ld, 16)
                load_h(0, 0)
                for q in range(4):
                    cols = slice(q * FQ * P, (q + 1) * FQ * P)
                    sp.dma_start(w_in[:, :, cols], w_in_d[:, :, cols]).then_inc(w_ld[q], 16)
                    sp.dma_start(w_up[:, :, cols], w_up_d[:, :, cols]).then_inc(w_ld[q], 16)
                    sp.dma_start(w_down[:, q * FQ:(q + 1) * FQ, :], w_down_d[:, q * FQ:(q + 1) * FQ, :]
                                 ).then_inc(w_ld[q], 16)
                load_h(1, 1)

                def body(g, i):
                    for t in range(TOK):
                        if begun(g * TOK + t - 1):
                            sp.wait_ge(y_done, g * TOK + t - 1)
                        sp.dma_start(x[:, t % 2, :], x_in[bass.ds(g * TOK + t, 1), :, :].rearrange("o p t -> p (o t)")
                                     ).then_inc(x_ld[t % 2], 16)
                    for t in range(TOK):
                        sp.wait_ge(x_done, g * TOK + t + 1)
                        sp.dma_start(x_out[bass.ds(g * TOK + t, 1), :, :].rearrange("o p t -> p (o t)"),
                                     x_new[:, t % 2, :]).then_inc(stored[t % 2], 16)

                body(0, 0)
                load_h(2, 0)
                body(1, 1)
                load_h(3, 1)
                body(2, 0)
                body(3, 1)
                for i in range(2):
                    sp.wait_ge(stored[i], 16 * (B // 2))

            @block.tensor
            def _(pe):
                HL = 16 * TOK * (1 + MOD)
                if MOD:
                    pe.wait_ge(const_ld, CONSTS)

                def low_rank(g, i):
                    if begun(g * NF - 1):
                        pe.wait_ge(silu_done, g * NF - 1)
                    for dk in range(DK):
                        mm = nc.tensor.matmul(gate_ps[0:R, 0, :], a_w[:, dk, :], h_t[:, i, :, dk, :],
                                              start=(dk == 0), stop=(dk == DK - 1))
                    mm.then_inc(ha_full, 1)

                def project(bank, w, g, i, f, more):
                    for dk in range(DK):
                        mm = nc.tensor.matmul(bank, w[:, dk, f * P:(f + 1) * P], h_t[:, i, :, dk, :],
                                              start=(dk == 0), stop=(dk == DK - 1 and not more))
                    return mm

                def gate_up(g, i, f):
                    n = g * NF + f
                    if isinstance(g, int) and g == 0 and f % FQ == 0:
                        pe.wait_ge(w_ld[f // FQ], 48)
                    if begun(n - 1):
                        pe.wait_ge(silu_done, n - 1)
                    if MOD and f == 0:
                        pe.wait_ge(ha_done, g + 1)
                    mm = project(gate_ps[:, f % 2, :], w_in, g, i, f, MOD)
                    if MOD:
                        mm = nc.tensor.matmul(gate_ps[:, f % 2, :], b_w[:, f * P:(f + 1) * P], mod_h[:, :],
                                              start=False, stop=True)
                    mm.then_inc(gate_full, 1)
                    if begun(n - 1):
                        pe.wait_ge(hidden_done, n - 1)
                    project(up_ps[:, f % 2, :], w_up, g, i, f, False).then_inc(up_full, 1)

                def down(g, f):
                    n = g * NF + f
                    pe.wait_ge(hidden_done, n + 1)
                    for t in range(TOK):
                        if f == 0:
                            if begun((g - 1) * TOK + t + 1):
                                pe.wait_ge(y_done, (g - 1) * TOK + t + 1)
                        mm = nc.tensor.matmul(out_ps[:, t, :], hidden[:, f % 2, t * P:(t + 1) * P], w_down[:, f, :],
                                              start=(f == 0), stop=(f == NF - 1))
                        if f == NF - 1:
                            mm.then_inc(out_full, 1)
                        elif t == TOK - 1:
                            mm.then_inc(down_done, 1)

                def body(g, i):
                    pe.wait_ge(h_ld[i], (g - i) * (HL // 2) + HL)
                    if MOD:
                        low_rank(g, i)
                    gate_up(g, i, 0)
                    for f in range(1, NF):
                        gate_up(g, i, f)
                        down(g, f - 1)
                    down(g, NF - 1)

                groups(pe, body)

            @block.scalar
            def _(act):
                def body(g, i):
                    for f in range(NF):
                        n = g * NF + f
                        act.wait_ge(gate_full, n + 1)
                        if begun(n - 1):
                            act.wait_ge(hidden_done, n - 1)
                        nc.scalar.activation(gate[:, f % 2, :], gate_ps[:, f % 2, :], ACT.Silu).then_inc(silu_done, 1)

                groups(act, body)

            @block.vector
            def _(dve):
                def output(g, t):
                    n = g * TOK + t
                    dve.wait_ge(out_full, n + 1)
                    dve.wait_ge(x_ld[t % 2], g * (TOK // 2) * 16 + 16 * (t // 2 + 1))
                    if MOE:
                        nc.vector.tensor_tensor(y[:, t % 2, :], out_ps[:, t, :], x[:, t % 2, :], ALU.add
                                                ).then_inc(y_done, 1)
                        dve.wait_ge(y_done, n + 1)
                        dve.wait_ge(rows_ld[t % 2], (g * (TOK // 2) + t // 2 + 1) * 16 * TOPK)
                        for k in range(TOPK):
                            nc.vector.scalar_tensor_tensor(
                                out=y[:, t % 2, :], in0=rows[:, t % 2, k, :], in1=y[:, t % 2, :],
                                scalar=sel_w[:, bass.ds(n, 1), k:k + 1].rearrange("p o k -> p (o k)"),
                                op0=ALU.mult, op1=ALU.add).then_inc(rows_done, 1)
                            dve.wait_ge(rows_done, n * TOPK + k + 1)
                    else:
                        nc.vector.scalar_tensor_tensor(out=y[:, t % 2, :], in0=x[:, t % 2, :], scalar=2.0,
                                                       in1=out_ps[:, t, :], op0=ALU.mult, op1=ALU.add
                                                       ).then_inc(y_done, 1)
                        dve.wait_ge(y_done, n + 1)
                    nc.vector.bn_stats(stats[:, :], y[:, t % 2, :]).then_inc(ln_step, 1)
                    dve.wait_ge(ln_step, n * 3 + 1)
                    dve.sem_inc(passed_dve, 1)
                    nc.vector.bn_aggr(mv[:, :], stats[:, :]).then_inc(ln_step, 1)
                    dve.wait_ge(ln_step, n * 3 + 2)
                    nc.vector.tensor_scalar(var_eps[:, :], mv[:, 1:2], LN_EPS, None, ALU.add).then_inc(ln_step, 1)
                    dve.wait_ge(rstd_done, n + 1)
                    if begun(g * (TOK // 2) * 16 + 16 * (t // 2)):
                        dve.wait_ge(stored[t % 2], g * (TOK // 2) * 16 + 16 * (t // 2))
                    nc.vector.tensor_scalar(x_new[:, t % 2, :], y[:, t % 2, :], mv[:, 0:1], rstd[:, 0:1],
                                            ALU.subtract, ALU.mult).then_inc(x_done, 1)

                if MOE:
                    dve.wait_ge(const_ld, CONSTS)

                def body(g, i):
                    if MOD:
                        dve.wait_ge(ha_full, g + 1)
                        if begun(g * NF):
                            dve.wait_ge(gate_full, g * NF)
                        nc.vector.scalar_tensor_tensor(out=mod_h[:, :], in0=mod[:, i, :], scalar=0.1,
                                                       in1=gate_ps[0:R, 0, :], op0=ALU.mult, op1=ALU.mult
                                                       ).then_inc(ha_done, 1)
                    for f in range(NF):
                        n = g * NF + f
                        dve.wait_ge(silu_done, n + 1)
                        dve.wait_ge(up_full, n + 1)
                        if f >= 2:
                            dve.wait_ge(down_done, g * (NF - 1) + f - 1)
                        elif f == 1:
                            if begun(g * TOK):
                                dve.wait_ge(out_full, g * TOK)
                        else:
                            if begun(g * (NF - 1)):
                                dve.wait_ge(down_done, g * (NF - 1))
                        nc.vector.tensor_tensor(hidden[:, f % 2, :], gate[:, f % 2, :], up_ps[:, f % 2, :], ALU.mult
                                                ).then_inc(hidden_done, 1)
                    for t in range(TOK):
                        output(g, t)

                groups(dve, body)

            @block.gpsimd
            def _(pool):
                pool.wait_ge(const_ld, CONSTS)

                def gather(n):
                    if begun((n - 1) * TOPK):
                        pool.wait_ge(rows_done, (n - 1) * TOPK)
                    for k in range(TOPK):
                        col = n * TOPK + k
                        nc.gpsimd.indirect_dma_start(
                            rows[:, n % 2, k, :], None, expert_rows,
                            bass.IndirectOffsetOnAxis(ap=sel_slot[:, col:col + 1], axis=0)
                        ).then_inc(rows_ld[n % 2], 16)

                def power(n):
                    pool.wait_ge(ln_step, n * 3 + 3)
                    nc.gpsimd.tensor_tensor(rstd[:, :], var_eps[:, :], minus_half[:, :], ALU.pow
                                            ).then_inc(rstd_done, 1)

                if MOE:
                    gather(0)
                    gather(1)
                    for n in range(B):
                        power(n)
                        if n + 2 < B:
                            gather(n + 2)
                else:
                    with pool.Fori(0, B) as n:
                        power(n)


E = 64
CAP = 64
SLOTS = E * CAP
NSEL = B * TOPK
TABLE = SLOTS + NSEL * P


def router(nc, tag, x_in, h_t_out, table_out, sel_w_out, sel_slot_out, rw_d, rbias_d, ident_d, before_d, ones_d,
           iota_d, trash_d, token_d, zero_d):
    with Phase(nc) as ph:
        sem, sb = ph.sem, ph.sb
        rw = sb(f"{tag}_rw", [P, DK, E])
        rbias = sb(f"{tag}_rbias", [P, E])
        ident = sb(f"{tag}_ident", [P, P])
        earlier = sb(f"{tag}_earlier", [P, P], BF16)
        ones = sb(f"{tag}_ones", [P, P], BF16)
        iota = sb(f"{tag}_iota", [P, E])
        trash = sb(f"{tag}_trash", [P, NSEL])
        token = sb(f"{tag}_token", [P, B], U32)
        x = sb(f"{tag}_x", [P, 2, D])
        x_t = sb(f"{tag}_x_t", [P, 2, DK, P])
        logits = sb(f"{tag}_logits", [P, B, E])
        biased = sb(f"{tag}_biased", [P, B, E])
        top = sb(f"{tag}_top", [P, B, 8])
        top_i = sb(f"{tag}_top_i", [P, B, 8], U32)
        expert = sb(f"{tag}_expert", [P, B, TOPK])
        row_max = sb(f"{tag}_row_max", [P, B])
        row_sum = sb(f"{tag}_row_sum", [P, B])
        row_inv = sb(f"{tag}_row_inv", [P, B])
        shifted = sb(f"{tag}_shifted", [P, B, E])
        probs = sb(f"{tag}_probs", [P, B, E])
        onehot = sb(f"{tag}_onehot", [P, TOPK, B, E], BF16)
        chosen = sb(f"{tag}_chosen", [P, B, E], BF16)
        pair = sb(f"{tag}_pair", [P, 2, B, E], BF16)
        prefix = sb(f"{tag}_prefix", [P, 2, B, E], BF16)
        picked = sb(f"{tag}_picked", [P, 2, B, E])
        sel_p = sb(f"{tag}_sel_p", [P, B, TOPK])
        sel_sum = sb(f"{tag}_sel_sum", [P, B])
        sel_inv = sb(f"{tag}_sel_inv", [P, B])
        sel_w = sb(f"{tag}_sel_w", [P, B, TOPK])
        place = sb(f"{tag}_place", [P, B, TOPK])
        kept = sb(f"{tag}_kept", [P, B, TOPK])
        slot = sb(f"{tag}_slot", [P, B, TOPK])
        slot_i = sb(f"{tag}_slot_i", [P, NSEL], U32)
        read_slot = sb(f"{tag}_read_slot", [P, B, TOPK], U32)
        t_ps = ph.ps(f"{tag}_t_ps", [P, 2, DK, P])
        logit_ps = ph.ps(f"{tag}_logit_ps", [P, 2, D])
        count_ps = ph.ps(f"{tag}_count_ps", [P, B, E])

        const_ld = sem(f"{tag}_const_ld")
        x_ld = [sem(f"{tag}_x_ld{i}") for i in range(2)]
        h_stored = [sem(f"{tag}_h_stored{i}") for i in range(2)]
        (table_zero, sel_stored, scattered, t_full, x_t_done, logit_full, logit_done, counted, probs_ready, exp_done,
         step, slots_ready, weights_ready, chosen_ready) = [sem(f"{tag}_{n}") for n in (
             "table_zero sel_stored scattered t_full x_t_done logit_full logit_done counted probs_ready exp_done "
             "step slots_ready weights_ready chosen_ready").split()]
        CONSTS = ((rw[:, :, :], rw_d), (rbias[:, :], rbias_d), (ident[:, :], ident_d), (earlier[:, :], before_d),
                  (ones[:, :], ones_d), (iota[:, :], iota_d), (trash[:, :], trash_d), (token[:, :], token_d))

        def tiles(eng, body):
            body(0, 0)
            body(1, 1)
            with eng.Fori(1, B // 2) as it:
                body(it * 2, 0)
                body(it * 2 + 1, 1)

        with nc.Block() as block:
            @block.sync
            def _(sp):
                for dst, src in CONSTS:
                    sp.dma_start(dst, src).then_inc(const_ld, 16)
                sp.dma_start(table_out.rearrange("(p n) o -> p (n o)", p=P), zero_d).then_inc(table_zero, 16)

                def load(b, i):
                    sp.dma_start(x[:, i, :], x_in[bass.ds(b, 1), :, :].rearrange("o p t -> p (o t)")
                                 ).then_inc(x_ld[i], 16)

                def store(b, i):
                    sp.wait_ge(x_t_done, b + 1)
                    sp.dma_start(h_t_out[bass.ds(b, 1), :, :, :].rearrange("o p k t -> p (o k) t"), x_t[:, i, :, :]
                                 ).then_inc(h_stored[i], 16)

                load(0, 0)
                load(1, 1)

                def body(b, i):
                    sp.wait_ge(t_full, b + 1)
                    if not (isinstance(b, int) and b >= B - 2):
                        load(b + 2, i)
                    store(b, i)

                body(0, 0)
                body(1, 1)
                with sp.Fori(1, B // 2 - 1) as it:
                    body(it * 2, 0)
                    body(it * 2 + 1, 1)
                body(B - 2, 0)
                body(B - 1, 1)
                sp.wait_ge(weights_ready, 1)
                sp.dma_start(sel_w_out, sel_w[:, :, :].rearrange("p b k -> p (b k)")).then_inc(sel_stored, 16)
                sp.wait_ge(slots_ready, 1)
                sp.dma_start(sel_slot_out, read_slot[:, :, :].rearrange("p b k -> p (b k)")).then_inc(sel_stored, 16)
                for i in range(2):
                    sp.wait_ge(h_stored[i], 16 * (B // 2))
                sp.wait_ge(sel_stored, 32)

            @block.tensor
            def _(pe):
                pe.wait_ge(const_ld, 16 * len(CONSTS))

                def transpose(b, i):
                    pe.wait_ge(x_ld[i], (b - i) * 8 + 16)
                    if begun(b - 1):
                        pe.wait_ge(x_t_done, b - 1)
                    for dk in range(DK):
                        mm = nc.tensor.transpose(t_ps[:, i, dk, :], x[:, i, dk * P:(dk + 1) * P], ident[:, :])
                    mm.then_inc(t_full, 1)

                def product(b, i):
                    pe.wait_ge(x_t_done, b + 1)
                    if begun(b - 1):
                        pe.wait_ge(logit_done, b - 1)
                    for dk in range(DK):
                        mm = nc.tensor.matmul(logit_ps[:, i, 0:E], x_t[:, i, dk, :], rw[:, dk, :], start=(dk == 0),
                                              stop=(dk == DK - 1))
                    mm.then_inc(logit_full, 1)

                transpose(0, 0)
                transpose(1, 1)
                product(0, 0)
                with pe.Fori(0, B // 2 - 1) as it:
                    transpose(it * 2 + 2, 0)
                    product(it * 2 + 1, 1)
                    transpose(it * 2 + 3, 1)
                    product(it * 2 + 2, 0)
                product(B - 1, 1)

                pe.wait_ge(chosen_ready, 2)
                for h in range(2):
                    half = slice(h * (B // 2), (h + 1) * (B // 2))
                    nc.tensor.matmul(count_ps[:, half, :], earlier[:, :], chosen[:, half, :], start=True, stop=False)
                    mm = nc.tensor.matmul(count_ps[:, half, :], ones[:, :], prefix[:, 0, half, :], start=False,
                                          stop=True)
                mm.then_inc(counted, 1)

            @block.scalar
            def _(act):
                def body(b, i):
                    act.wait_ge(t_full, b + 1)
                    if begun((b - i) * 8):
                        act.wait_ge(h_stored[i], (b - i) * 8)
                    if begun(b - 1):
                        act.wait_ge(logit_full, b - 1)
                    nc.scalar.activation(x_t[:, i, :, :], t_ps[:, i, :, :], ACT.Copy).then_inc(x_t_done, 1)

                tiles(act, body)
                act.wait_ge(probs_ready, 1)
                nc.scalar.activation(probs[:, :, :], shifted[:, :, :], ACT.Exp).then_inc(exp_done, 1)

            @block.vector
            def _(dve):
                done = 0

                def chain(op):
                    nonlocal done
                    op.then_inc(step, 1)
                    done += 1
                    dve.wait_ge(step, done)

                def per_tile(a):
                    return a.rearrange("p (b o) -> p b o", o=1).to_broadcast([P, B, E])

                def per_expert(a):
                    return a.rearrange("p (o e) -> p o e", o=1).to_broadcast([P, B, E])

                dve.wait_ge(const_ld, 16 * len(CONSTS))

                def take(b, i):
                    dve.wait_ge(logit_full, b + 1)
                    nc.vector.tensor_copy(logits[:, bass.ds(b, 1), :].rearrange("p o e -> p (o e)"),
                                          logit_ps[:, i, 0:E]).then_inc(logit_done, 1)

                tiles(dve, take)
                dve.wait_ge(logit_done, B)
                chain(nc.vector.tensor_reduce(row_max[:, :], logits[:, :, :], AX.X, ALU.max))
                nc.vector.tensor_tensor(shifted[:, :, :], logits[:, :, :], per_tile(row_max[:, :]), ALU.subtract
                                        ).then_inc(probs_ready, 1)
                chain(nc.vector.tensor_tensor(biased[:, :, :], logits[:, :, :], per_expert(rbias[:, :]), ALU.add))
                for b in range(B):
                    nc.vector.max(top[:, b, :], biased[:, b, :]).then_inc(step, 1)
                done += B
                dve.wait_ge(step, done)
                for b in range(B):
                    nc.vector.max_index(top_i[:, b, :], top[:, b, :], biased[:, b, :]).then_inc(step, 1)
                done += B
                dve.wait_ge(step, done)
                chain(nc.vector.tensor_copy(expert[:, :, :], top_i[:, :, 0:TOPK]))
                for k in range(TOPK):
                    nc.vector.tensor_tensor(onehot[:, k, :, :], per_expert(iota[:, :]),
                                            expert[:, :, k:k + 1].to_broadcast([P, B, E]), ALU.is_equal
                                            ).then_inc(step, 1)
                done += TOPK
                dve.wait_ge(step, done)
                nc.vector.tensor_tensor(pair[:, 0, :, :], onehot[:, 0, :, :], onehot[:, 1, :, :], ALU.add
                                        ).then_inc(step, 1)
                nc.vector.tensor_tensor(pair[:, 1, :, :], onehot[:, 2, :, :], onehot[:, 3, :, :], ALU.add
                                        ).then_inc(step, 1)
                done += 2
                dve.wait_ge(step, done)
                chain(nc.vector.tensor_tensor(chosen[:, :, :], pair[:, 0, :, :], pair[:, 1, :, :], ALU.add))
                nc.vector.memset(prefix[:, 0, 0:1, :], 0.0).then_inc(step, 1)
                nc.vector.tensor_copy(prefix[:, 0, 1:B, :], chosen[:, 0:B - 1, :]).then_inc(step, 1)
                done += 2
                dve.wait_ge(step, done)
                cur, reach = 0, 1
                while reach < B:
                    last = reach * 2 >= B
                    signal = chosen_ready if last else step
                    nc.vector.tensor_copy(prefix[:, 1 - cur, 0:reach, :], prefix[:, cur, 0:reach, :]
                                          ).then_inc(signal, 1)
                    nc.vector.tensor_tensor(prefix[:, 1 - cur, reach:B, :], prefix[:, cur, reach:B, :],
                                            prefix[:, cur, 0:B - reach, :], ALU.add).then_inc(signal, 1)
                    if not last:
                        done += 2
                        dve.wait_ge(step, done)
                    cur, reach = 1 - cur, reach * 2
                assert cur == 0

                dve.wait_ge(exp_done, 1)
                chain(nc.vector.tensor_reduce(row_sum[:, :], probs[:, :, :], AX.X, ALU.add))
                chain(nc.vector.reciprocal(row_inv[:, :], row_sum[:, :]))
                for k in range(TOPK):
                    chain(nc.vector.tensor_tensor(picked[:, 0, :, :], probs[:, :, :], onehot[:, k, :, :], ALU.mult))
                    chain(nc.vector.tensor_reduce(sel_w[:, :, k], picked[:, 0, :, :], AX.X, ALU.add))
                chain(nc.vector.tensor_tensor(sel_p[:, :, :], sel_w[:, :, :], row_inv[:, :].rearrange(
                    "p (b o) -> p b o", o=1).to_broadcast([P, B, TOPK]), ALU.mult))
                chain(nc.vector.tensor_reduce(sel_sum[:, :], sel_p[:, :, :], AX.X, ALU.add))
                chain(nc.vector.reciprocal(sel_inv[:, :], sel_sum[:, :]))
                nc.vector.tensor_tensor(sel_w[:, :, :], sel_p[:, :, :], sel_inv[:, :].rearrange(
                    "p (b o) -> p b o", o=1).to_broadcast([P, B, TOPK]), ALU.mult).then_inc(weights_ready, 1)

                dve.wait_ge(counted, 1)
                for k in range(TOPK):
                    chain(nc.vector.tensor_tensor(picked[:, 1, :, :], count_ps[:, :, :], onehot[:, k, :, :],
                                                  ALU.mult))
                    chain(nc.vector.tensor_reduce(place[:, :, k], picked[:, 1, :, :], AX.X, ALU.add))
                chain(nc.vector.tensor_scalar(kept[:, :, :], place[:, :, :], float(CAP), None, ALU.is_lt))
                chain(nc.vector.scalar_tensor_tensor(out=slot[:, :, :], in0=expert[:, :, :], scalar=float(CAP),
                                                     in1=place[:, :, :], op0=ALU.mult, op1=ALU.add))
                flat = "p b k -> p (b k)"
                chain(nc.vector.tensor_tensor(slot[:, :, :].rearrange(flat), slot[:, :, :].rearrange(flat),
                                              trash[:, :], ALU.subtract))
                chain(nc.vector.tensor_tensor(slot[:, :, :], slot[:, :, :], kept[:, :, :], ALU.mult))
                chain(nc.vector.tensor_tensor(slot[:, :, :].rearrange(flat), slot[:, :, :].rearrange(flat),
                                              trash[:, :], ALU.add))
                chain(nc.vector.tensor_copy(slot_i[:, :], slot[:, :, :].rearrange(flat)))
                nc.vector.tensor_scalar(read_slot[:, :, :], slot[:, :, :], float(SLOTS), None, ALU.min
                                        ).then_inc(slots_ready, 1)

            @block.gpsimd
            def _(pool):
                pool.wait_ge(const_ld, 16 * len(CONSTS))
                pool.wait_ge(table_zero, 16)
                pool.wait_ge(slots_ready, 1)
                for n in range(NSEL):
                    nc.gpsimd.indirect_dma_start(
                        table_out, bass.IndirectOffsetOnAxis(ap=slot_i[:, n:n + 1], axis=0),
                        token[:, n // TOPK:n // TOPK + 1], None).then_inc(scattered, 16)
                pool.wait_ge(scattered, 16 * NSEL)


def experts(nc, tag, x_rows, table, y_out, gate_d, up_d, down_d, ident_d):
    PAIRS = E // 2
    RING = 4
    with Phase(nc) as ph:
        sem, sb = ph.sem, ph.sb
        token = sb(f"{tag}_token", [P, PAIRS], U32)
        ident = sb(f"{tag}_ident", [P, P])
        zero_row = sb(f"{tag}_zero_row", [1, D])
        w_gate = sb(f"{tag}_w_gate", [P, RING, 2, DK, P])
        w_up = sb(f"{tag}_w_up", [P, RING, 2, DK, P])
        w_down = sb(f"{tag}_w_down", [P, RING, 2, D])
        x = sb(f"{tag}_x", [P, RING, D])
        x_t = sb(f"{tag}_x_t", [P, 2, DK, P])
        gate = sb(f"{tag}_gate", [P, 2, P])
        hidden = sb(f"{tag}_hidden", [P, 2, P])
        y = sb(f"{tag}_y", [P, 2, D])
        t_ps = ph.ps(f"{tag}_t_ps", [P, 2, DK, P])
        gate_ps = ph.ps(f"{tag}_gate_ps", [P, 2, D])
        up_ps = ph.ps(f"{tag}_up_ps", [P, 2, D])
        y_ps = ph.ps(f"{tag}_y_ps", [P, 2, D])

        w_ld = [sem(f"{tag}_w_ld{i}") for i in range(RING)]
        x_ld = [sem(f"{tag}_x_ld{i}") for i in range(RING)]
        stored = [sem(f"{tag}_stored{i}") for i in range(2)]
        (table_ld, ident_ld, zeros, zero_stored, t_full, x_t_done, gate_full, up_full, silu_done, hidden_done, y_full,
         y_done) = [sem(f"{tag}_{n}") for n in ("table_ld ident_ld zeros zero_stored t_full x_t_done gate_full "
                                                "up_full silu_done hidden_done y_full y_done").split()]

        def pairs(eng, body):
            for i in range(RING):
                body(i, i)
            with eng.Fori(1, PAIRS // RING) as it:
                for i in range(RING):
                    body(it * RING + i, i)

        with nc.Block() as block:
            @block.sync
            def _(sp):
                sp.dma_start(token[:, :], table[0:SLOTS, :].rearrange("(n p) o -> p (n o)", p=P),
                             allow_slow_non_contiguous=True
                             ).then_inc(table_ld, 16)
                sp.dma_start(ident[:, :], ident_d).then_inc(ident_ld, 16)

                def body(n, i):
                    if begun(n - RING + 1):
                        sp.wait_ge(y_full, n - RING + 1)
                    for dst, src in ((w_gate[:, i, :, :, :], gate_d), (w_up[:, i, :, :, :], up_d)):
                        for e in range(2):
                            sp.dma_start(dst[:, e, :, :], src[bass.ds(n * 2 + e, 1), :, :, :].rearrange(
                                "o p k f -> p (o k) f")).then_inc(w_ld[i], 16)
                    sp.dma_start(w_down[:, i, :, :], down_d[bass.ds(n * 2, 2), :, :].rearrange("e p f -> p e f")
                                 ).then_inc(w_ld[i], 16)

                pairs(sp, body)

            @block.scalar
            def _(act):
                act.wait_ge(zeros, 1)
                act.dma_start(y_out[SLOTS:SLOTS + 1, :], zero_row[:, :]).then_inc(zero_stored, 16)

                def store(n, i):
                    act.wait_ge(y_done, n + 1)
                    act.dma_start(y_out[bass.ds(n * P, P), :], y[:, i % 2, :]).then_inc(stored[i % 2], 16)

                def body(n, i):
                    act.wait_ge(t_full, n + 1)
                    if begun(n - 1):
                        act.wait_ge(up_full, n - 1)
                    nc.scalar.activation(x_t[:, i % 2, :, :], t_ps[:, i % 2, :, :], ACT.Copy).then_inc(x_t_done, 1)
                    act.wait_ge(gate_full, n + 1)
                    if begun(n - 1):
                        act.wait_ge(hidden_done, n - 1)
                    nc.scalar.activation(gate[:, i % 2, :], gate_ps[:, i % 2, 0:P], ACT.Silu).then_inc(silu_done, 1)
                    if isinstance(n, int) and n == 0:
                        return
                    store(n - 1, i - 1 + RING)

                pairs(act, body)
                store(PAIRS - 1, RING - 1)
                for i in range(2):
                    act.wait_ge(stored[i], 16 * (PAIRS // 2))
                act.wait_ge(zero_stored, 16)

            @block.tensor
            def _(pe):
                pe.wait_ge(ident_ld, 16)

                def transpose(n, i):
                    pe.wait_ge(x_ld[i], (n - i) * (16 // RING) + 16)
                    if begun(n - 1):
                        pe.wait_ge(x_t_done, n - 1)
                    for dk in range(DK):
                        mm = nc.tensor.transpose(t_ps[:, i % 2, dk, :], x[:, i, dk * P:(dk + 1) * P], ident[:, :])
                    mm.then_inc(t_full, 1)

                def gate_up(n, i):
                    pe.wait_ge(w_ld[i], (n - i) * (80 // RING) + 80)
                    pe.wait_ge(x_t_done, n + 1)
                    for bank, w, taken, full in ((gate_ps, w_gate, silu_done, gate_full),
                                                 (up_ps, w_up, hidden_done, up_full)):
                        if begun(n - 1):
                            pe.wait_ge(taken, n - 1)
                        for e in range(2):
                            tokens = slice(e * CAP, (e + 1) * CAP)
                            for dk in range(DK):
                                mm = nc.tensor.matmul(bank[:, i % 2, tokens], w[:, i, e, dk, :],
                                                      x_t[:, i % 2, dk, tokens], start=(dk == 0), stop=(dk == DK - 1))
                        mm.then_inc(full, 1)

                def down(n, i):
                    pe.wait_ge(hidden_done, n + 1)
                    if begun(n - 1):
                        pe.wait_ge(y_done, n - 1)
                    for e in range(2):
                        tokens = slice(e * CAP, (e + 1) * CAP)
                        mm = nc.tensor.matmul(y_ps[tokens, i % 2, :], hidden[:, i % 2, tokens], w_down[:, i, e, :],
                                              start=True, stop=True)
                    mm.then_inc(y_full, 1)

                transpose(0, 0)

                def step(n, i):
                    gate_up(n, i)
                    transpose(n + 1, (i + 1) % RING) if not (isinstance(n, int) and n == PAIRS - 1) else None
                    down(n, i)

                for i in range(RING - 1):
                    step(i, i)
                with pe.Fori(0, PAIRS // RING - 1) as it:
                    for i in range(RING):
                        step(it * RING + (RING - 1 + i), (RING - 1 + i) % RING)
                step(PAIRS - 1, RING - 1)

            @block.vector
            def _(dve):
                def body(n, i):
                    dve.wait_ge(silu_done, n + 1)
                    dve.wait_ge(up_full, n + 1)
                    if begun(n - 1):
                        dve.wait_ge(y_full, n - 1)
                    nc.vector.tensor_tensor(hidden[:, i % 2, :], gate[:, i % 2, :], up_ps[:, i % 2, 0:P], ALU.mult
                                            ).then_inc(hidden_done, 1)
                    dve.wait_ge(y_full, n + 1)
                    if begun((n - i % 2) * 8):
                        dve.wait_ge(stored[i % 2], (n - i % 2) * 8)
                    nc.vector.tensor_copy(y[:, i % 2, :], y_ps[:, i % 2, :]).then_inc(y_done, 1)

                pairs(dve, body)

            @block.gpsimd
            def _(pool):
                nc.gpsimd.memset(zero_row[:, :], 0.0).then_inc(zeros, 1)
                pool.wait_ge(table_ld, 16)

                for n in range(PAIRS):
                    i = n % RING
                    if begun(n - RING + 1):
                        pool.wait_ge(t_full, n - RING + 1)
                    nc.gpsimd.indirect_dma_start(x[:, i, :], None, x_rows,
                                                 bass.IndirectOffsetOnAxis(ap=token[:, n:n + 1], axis=0)
                                                 ).then_inc(x_ld[i], 16)


def decoder(nc, i, out):
    def dram(name, shape, dt=F32):
        return nc.dram_tensor(f"{name}_dram", shape, dt).ap()

    x1, x2, x3, x4, x5 = [dram(f"x{n}", (B, P, D)) for n in range(1, 6)]

    q, k = dram("a0_q", (B, 48, 8 * D), BF16), dram("a0_k", (B, 48, 8 * P), BF16)
    v = dram("a0_v", (B, P, P))
    prepare(nc, "a0p", "gqa", 8, q, k, i["x_t"], None, v, [i["a0_wq"], i["a0_wk"], i["a0_wv"]], i["rope_perm"],
            i["a0_cos"], i["a0_sin"])
    causal_gqa(nc, "a0", 8, i["x"], q, k, v, x1, i["ident"], i["sel_o16"], i["sel_s16"], i["half"],
               i["ident_bf"], i["mask"], i["mask_t"], i["a0_wo"], i["a0_bo"])

    q, k = dram("c0_q", (B, 48, 8 * D), BF16), dram("c0_k", (B, 48, 8 * D), BF16)
    v = dram("c0_v", (B, D, P))
    prepare(nc, "c0p", "cross", 8, q, k, x1, i["ctx"], v, [i["c0_wq"], i["c0_wk"], i["c0_wv"]], i["rope_perm"],
            i["c0_cos"], i["c0_sin"], i["c0_bqk"], i["c0_bv"])
    cross_attention(nc, "c0", 8, x1, q, k, v, x2, i["ident"], i["sel_o16"], i["sel_s16"], i["half"],
                    i["c0_wo"], i["c0_bo"])

    h_t, mod = dram("f0_h_t", (B, P, DK, P)), dram("f0_mod", (B, 16, P))
    gate_attention(nc, "g0", x2, h_t, mod, i["f0_wq"], i["f0_wk"], i["f0_wv"], i["f0_wo"], i["f0_a"], i["f0_ln"],
                   i["ident"], i["half"], i["ident_bf"], i["mask"], i["mask_t"])
    feed_forward(nc, "f0", 16, h_t, x2, x3, i["f0_win"], i["f0_wup"], i["f0_wdown"], i["half"], mod,
                 i["f0_a"], i["f0_b"])

    squared_attention(nc, "a1", x3, x4, i["a1_wq"], i["a1_wk"], i["a1_wv"], i["a1_wo"], i["a1_gamma"], i["a1_beta"],
                      i["ident"], i["half32"], i["keep_t"])

    q, k = dram("c1_q", (B, 24, 16 * D), BF16), dram("c1_k", (B, 24, 16 * D), BF16)
    prepare(nc, "c1p", "plain", 16, q, k, x4, i["ctx"], q_scale=8 ** -0.5)
    cross_attention(nc, "c1", 16, x4, q, k, i["ctx_t"], x5, i["ident"], i["sel_o8"], i["sel_s8"],
                    i["half"])

    h_t1, table = dram("f1_h_t", (B, P, DK, P)), dram("f1_table", (TABLE, 1), U32)
    sel_w, sel_slot = dram("f1_sel_w", (P, NSEL)), dram("f1_sel_slot", (P, NSEL), U32)
    rows = dram("f1_rows", (SLOTS + 1, D))
    router(nc, "r1", x5, h_t1, table, sel_w, sel_slot, i["f1_rw"], i["f1_rbias"], i["ident"], i["earlier"],
           i["ones_bf"], i["iota"], i["trash"], i["token"], i["zero_table"])
    experts(nc, "e1", x5.rearrange("b t d -> (b t) d"), table, rows, i["f1_gate"], i["f1_up"], i["f1_down"],
            i["ident"])
    feed_forward(nc, "f1", 8, h_t1, x5, out, i["f1_win"], i["f1_wup"], i["f1_wdown"], i["half"],
                 expert_rows=rows, sel_w_d=sel_w.rearrange("p (b k) -> p b k", k=TOPK), sel_slot_d=sel_slot)


def kernel(**inputs):
    import numpy as np
    import ml_dtypes
    import concourse.bacc as _bacc
    from concourse import mybir as _mybir
    from concourse.bass_utils import run_bass_kernel_spmd as _run

    w = {name: np.asarray(a) for name, a in inputs.items()}
    a = {}

    def rows(m):
        return m.reshape(m.shape[0] // P, P, -1).transpose(1, 0, 2)

    a["x"] = w["x"]
    a["x_t"] = w["x"].reshape(B, P, D // P, P).transpose(0, 3, 2, 1)
    a["ctx"] = w["ctx_2048"]
    a["ctx_t"] = w["ctx_2048"].transpose(0, 2, 1)
    a["a0_wq"] = w["L0_attn_Wq"].reshape(4, P, 8, 4, 16).transpose(1, 0, 3, 2, 4).reshape(P, 4, D)
    a["a0_wk"] = rows(w["L0_attn_Wk"])
    a["a0_wv"] = rows(w["L0_attn_Wv"])
    a["a0_wo"] = w["L0_attn_Wo"].reshape(8, 4, 16, D).transpose(0, 2, 1, 3).reshape(P, 4, D)
    a["a0_bo"] = np.broadcast_to(w["L0_attn_b_out"], (P, D))
    for n in "qkvo":
        a[f"c0_w{n}"] = w[f"L0_xattn_W{n}"].T
        a[f"a1_w{n}"] = rows(w[f"L1_attn_W{n}"].T)
    a["c0_bqk"] = np.stack([w["L0_xattn_bq"], w["L0_xattn_bk"]], 1)
    a["c0_bv"] = np.broadcast_to(np.tile(w["L0_xattn_bv"], 4), (P, D))
    a["c0_bo"] = w["L0_xattn_bo"].reshape(P, 1)
    for n in "qkv":
        a[f"f0_w{n}"] = rows(w[f"L0_ffn_W{n}"].T)
    a["f0_wo"] = rows(w["L0_ffn_Wo"])
    a["f0_a"] = rows(w["L0_ffn_A"])
    a["f0_b"] = w["L0_ffn_B"]
    a["f0_ln"] = np.stack([w[f"L0_ffn_ln{n}_w"].reshape(4, P).T for n in (1, 2)], 1)
    a["f0_win"] = rows(w["L0_ffn_W_in_base"].T)
    a["f0_wup"] = rows(w["L0_ffn_W_up_base"].T)
    a["f0_wdown"] = rows(w["L0_ffn_W_down"].T)
    a["a1_gamma"] = np.broadcast_to(w["L1_attn_gamma"], (P, 32))
    a["a1_beta"] = np.broadcast_to(w["L1_attn_beta"], (P, 32))
    a["f1_rw"] = rows(w["L1_ffn_router_w"].T)
    a["f1_rbias"] = np.broadcast_to(w["L1_ffn_router_bias"], (P, E))
    for n in ("gate", "up"):
        a[f"f1_{n}"] = w[f"L1_ffn_{n}_w"].transpose(0, 2, 1).reshape(E, 4, P, P).transpose(0, 2, 1, 3)
    a["f1_down"] = w["L1_ffn_down_w"].transpose(0, 2, 1)
    a["f1_win"] = rows(w["L1_ffn_sh_gate_w"].reshape(-1, D).T)
    a["f1_wup"] = rows(w["L1_ffn_sh_up_w"].reshape(-1, D).T)
    a["f1_wdown"] = rows(w["L1_ffn_sh_down_w"].transpose(0, 2, 1).reshape(-1, D))

    c = np.arange(P)
    a["ident"] = np.eye(P, dtype=np.float32)
    a["ident_bf"] = a["ident"].astype(ml_dtypes.bfloat16)
    a["half"] = np.full((P, 1), -0.5, np.float32)
    a["half32"] = np.full((P, 32), -0.5, np.float32)
    a["mask"] = np.where(c[None, :] > c[:, None], -1e30, 0.0).astype(ml_dtypes.bfloat16)
    a["mask_t"] = a["mask"].T
    a["keep_t"] = np.triu(np.ones((P, P), np.float32))
    a["earlier"] = (c[:, None] < c[None, :]).astype(ml_dtypes.bfloat16)
    a["ones_bf"] = np.ones((P, P), ml_dtypes.bfloat16)
    a["iota"] = np.broadcast_to(np.arange(E, dtype=np.float32), (P, E))
    a["trash"] = (SLOTS + np.arange(NSEL)[None, :] * P + c[:, None]).astype(np.float32)
    a["token"] = (np.arange(B)[None, :] * P + c[:, None]).astype(np.uint32)
    a["zero_table"] = np.zeros((P, TABLE // P), np.uint32)
    for ch in (16, 8):
        sel_o, sel_s = np.zeros((P, 4 * ch), np.float32), np.zeros((P, 4 * ch), np.float32)
        for r in range(4 * ch):
            sel_o[32 * (r // ch) + r % ch, r] = 1
            sel_s[32 * (r // ch) + ch + r % ch, r] = 1
        a[f"sel_o{ch}"], a[f"sel_s{ch}"] = sel_o, sel_s
    inv_freq = (1.0 / 10000.0 ** (np.arange(0, 16, 2, dtype=np.float32) / np.float32(16))).astype(np.float32)
    angle = np.arange(D, dtype=np.float32)[None, :] * inv_freq[:, None]
    cos = np.tile(np.concatenate([np.cos(angle), np.cos(angle)]), (8, 1)).astype(np.float32)
    sin = np.tile(np.concatenate([-np.sin(angle), np.sin(angle)]), (8, 1)).astype(np.float32)
    for name, t in (("cos", cos), ("sin", sin)):
        a[f"a0_{name}"] = np.concatenate([np.tile(t[:, :P] / 4, (1, 4)), t[:, :P]], 1)
        a[f"c0_{name}"] = np.concatenate([t / 4, t], 1)
    a["rope_perm"] = np.zeros((P, P), np.float32)
    a["rope_perm"][c - c % 16 + (c % 16 + 8) % 16, c] = 1

    nc = _bacc.Bacc("TRN2", target_bir_lowering=False, num_devices=1)
    arrays, aps = {}, {}
    for name, value in a.items():
        value = np.ascontiguousarray(value)
        arrays[f"in_{name}"] = value
        aps[name] = nc.dram_tensor(f"in_{name}", value.shape, _mybir.dt.from_np(value.dtype),
                                   kind="ExternalInput").ap()
    out = nc.dram_tensor("out_0", (B, P, D), F32, kind="ExternalOutput").ap()
    decoder(nc, aps, out)
    return _run(nc, [arrays], core_ids=[0]).results[0]["out_0"]
```

```python
import concourse.bass as bass
from concourse import mybir
from contextlib import ExitStack

F32 = mybir.dt.float32
BF16 = mybir.dt.bfloat16
F32R = mybir.dt.float32r
U32 = mybir.dt.uint32
ACT = mybir.ActivationFunctionType
ALU = mybir.AluOpType
AX = mybir.AxisListType

P = 128
B = 16
D = 512
LN_EPS = 1e-5
TWO_ONES = 1.0 + 2.0 ** -9 - 2.0 ** -16


class Phase:

    def __init__(self, nc):
        self.nc, self.ctx, self.sems = nc, ExitStack(), []

    def __enter__(self):
        self.ctx.__enter__()
        return self

    def __exit__(self, *exc):
        self.ctx.__exit__(*exc)
        if exc[0] is None:
            self.nc.clear_and_free_semaphores(self.sems)
            self.nc.all_engine_barrier()

    def sb(self, name, shape, dt=F32):
        return self.ctx.enter_context(self.nc.sbuf_tensor(name, shape, dt))

    def ps(self, name, shape, dt=F32):
        return self.ctx.enter_context(self.nc.psum_tensor(name, shape, dt))

    def sem(self, name):
        s = self.nc.alloc_semaphore(name)
        self.sems.append(s)
        return s


def begun(count):
    return not (isinstance(count, int) and count <= 0)


def cross_attention(nc, tag, H, x_in, q_parts, k_parts, v_rows, x_out, ident_d, sel_o_d, sel_s_d,
                    half_d, wo_d=None, bo_d=None):
    C = P // H
    L = 512
    G = 4
    NG = H // G
    UNITS = B * NG
    RING = 8
    NBS = RING // NG
    AHEAD = NG + 1
    KT = L // P
    ROWS, MROW, MPARTS = 6 * C, 96, 3
    PROJ = wo_d is not None

    SUMS_AT = ((0, 2), (0, 3), (1, 0), (1, 1))
    EXPAND_AT, COPY_AT, SELECT_AT, NORM_AT = (((0, 3), (0, 3), (1, 0), (1, 1)) if NG == 2 else
                                              ((1, 3), (2, 0), (2, 1), (2, 2)))
    with Phase(nc) as ph:
        sem, sb = ph.sem, ph.sb
        q_st = sb(f"{tag}_q_st", [P, RING, G, L], BF16)
        k_st = sb(f"{tag}_k_st", [P, RING, G, L], BF16)
        v_raw = sb(f"{tag}_v_raw", [P, 2, KT, P])
        v_aug = sb(f"{tag}_v_aug", [P, NBS, KT, H, 32])
        probs = sb(f"{tag}_probs", [P, 2, G, L])
        o_raw = sb(f"{tag}_o_raw", [P, 2, NG, L])
        maxes = sb(f"{tag}_maxes", [P, 2, H * KT])
        m_neg = sb(f"{tag}_m_neg", [H * KT, P])
        m_rest = sb(f"{tag}_m_rest", [H * KT, P])
        m_parts = sb(f"{tag}_m_parts", [H * KT, 2, MPARTS, P], BF16)
        recip_small = sb(f"{tag}_recip_small", [P, KT * H])
        recip_q = sb(f"{tag}_recip_q", [P, KT * P])
        recip = sb(f"{tag}_recip", [P, L])
        o_norm = sb(f"{tag}_o_norm", [P, L])
        x_res = sb(f"{tag}_x_res", [P, 2, L])
        y = sb(f"{tag}_y", [P, L])
        stats = sb(f"{tag}_stats", [P, 6])
        mv = sb(f"{tag}_mv", [P, 2])
        var_eps = sb(f"{tag}_var_eps", [P, 1])
        rstd = sb(f"{tag}_rstd", [P, 1])
        x_new = sb(f"{tag}_x_new", [P, 2, L])
        ident = sb(f"{tag}_ident", [P, P])
        sel_o = sb(f"{tag}_sel_o", [P, G * C])
        sel_s = sb(f"{tag}_sel_s", [P, G * C])
        minus_half = sb(f"{tag}_minus_half", [P, 1])
        if PROJ:
            wo = sb(f"{tag}_wo", [P, P])
            bo = sb(f"{tag}_bo", [P, 1])

        s1_ps = ph.ps(f"{tag}_s1", [P, 2, L])
        st_ps = ph.ps(f"{tag}_st", [P, 2, 2, L])
        o_ps = ph.ps(f"{tag}_o", [P, L])
        misc_ps = ph.ps(f"{tag}_misc", [P, L])

        const_ld = sem(f"{tag}_const_ld")
        passed_dve = sem(f"{tag}_passed_dve")
        passed_pe = sem(f"{tag}_passed_pe")
        passed_pool = sem(f"{tag}_passed_pool")
        expand_full, recip_copied, small_done = [sem(f"{tag}_{n}") for n in "expand_full recip_copied small_done".split()]
        memset_done = sem(f"{tag}_memset_done")
        ones_done = sem(f"{tag}_ones_done")
        stack_ld = [sem(f"{tag}_stack_ld{i}") for i in range(RING)]
        v_ld = [sem(f"{tag}_v_ld{i}") for i in range(2)]
        v_placed = sem(f"{tag}_v_placed")
        x_ld = [sem(f"{tag}_x_ld{i}") for i in range(2)]
        s1_full = sem(f"{tag}_s1_full")
        max_done = sem(f"{tag}_max_done")
        st_full = sem(f"{tag}_st_full")
        exp_done = sem(f"{tag}_exp_done")
        av_done = sem(f"{tag}_av_done")
        o_copied = sem(f"{tag}_o_copied")
        sums_full = sem(f"{tag}_sums_full")
        recip_done = sem(f"{tag}_recip_done")
        o_full = sem(f"{tag}_o_full")
        o_normed = sem(f"{tag}_o_normed")
        proj_full = sem(f"{tag}_proj_full")
        mT_full = sem(f"{tag}_mT_full")
        m_step = sem(f"{tag}_m_step")
        m_ld = sem(f"{tag}_m_ld")
        y_done = sem(f"{tag}_y_done")
        ln_step = sem(f"{tag}_ln_step")
        rstd_done = sem(f"{tag}_rstd_done")
        x_done = sem(f"{tag}_x_done")
        x_stored = sem(f"{tag}_x_stored")

        def rounds(eng, body):
            body(0, True, False)
            if UNITS // RING > 2:
                with eng.Fori(1, UNITS // RING - 1) as it:
                    body(it, False, False)
            body(UNITS // RING - 1, False, True)

        def unit_exists(u_off, last):
            return not (last and u_off >= RING)

        block = nc.Block()
        with block:
            @block.sync
            def _(sp):
                for dst, src in ([(ident, ident_d), (sel_o, sel_o_d), (sel_s, sel_s_d), (minus_half, half_d)]
                                 + ([(wo, wo_d), (bo, bo_d)] if PROJ else [])):
                    sp.dma_start(dst[:, :], src).then_inc(const_ld, 16)

                def load_stack(it, j):
                    b, g, s = it * NBS + j // NG, j % NG, j % RING
                    heads = slice(g * G * L, (g + 1) * G * L)

                    def parts(src, p, n):
                        a = src[bass.ds(b, 1), p * C:(p + n) * C, heads]
                        return a.rearrange("o c t -> (o c) t")

                    row = 0
                    for n in (3, 2, 1):
                        sp.dma_start(q_st[row:row + n * C, s, :, :].rearrange("p h t -> p (h t)"),
                                     parts(q_parts, 0, n)).then_inc(stack_ld[s], 16)
                        a = parts(k_parts, 3 - n, 1)
                        a = bass.AP(a.tensor, a.offset, [[0, n]] + [list(x) for x in a.ap])
                        sp.dma_start(k_st[row:row + n * C, s, :, :].rearrange("p h t -> p (h t)"),
                                     a).then_inc(stack_ld[s], 16)
                        row += n * C

                def load_v(b, i):
                    sp.dma_start(v_raw[:, i % 2, :, :],
                                 v_rows[bass.ds(b, 1), :, :].rearrange("o (k p) c -> p (o k) c", p=P)
                                 ).then_inc(v_ld[i % 2], 16)

                def load_x(b, i):
                    sp.dma_start(x_res[:, i % 2, :], x_in[bass.ds(b, 1), :, :].rearrange("o p t -> p (o t)")
                                 ).then_inc(x_ld[i % 2], 16)

                def send_max(b, j0):
                    sp.wait_ge(m_step, (b + 1) * 5)
                    s0 = j0 % RING
                    for p in range(MPARTS):
                        dst = q_st[MROW + p:MROW + p + 1, s0:s0 + NG, :, :].rearrange("p u h t -> p (u h t)")
                        sp.dma_start(dst, m_parts[:, (j0 // NG) % 2, p, :]).then_inc(m_ld, 16)

                sp.wait_ge(memset_done, 3 if ROWS < MROW else 1)
                for j in range(RING - 1):
                    if j == 0:
                        load_stack(0, 0)
                        load_v(0, 0)
                    else:
                        load_stack(0, j)
                send_max(0, 0)

                def body(it, first, last):
                    for j in range(RING):
                        b, jb, g = it * NBS + j // NG, j // NG, j % NG
                        if unit_exists(j + RING - 1, last):
                            if begun((it * RING + j) * KT):
                                sp.wait_ge(av_done, (it * RING + j) * KT)
                            load_stack(it + (j + RING - 1) // RING, (j + RING - 1) % RING)
                        if g == 0 and unit_exists(j + NG, last):
                            if begun(b):
                                sp.wait_ge(v_placed, b)
                            load_v(b + 1, jb + 1)
                        if g == 0:
                            if begun(b - 1):
                                sp.wait_ge(y_done, b - 1)
                            load_x(b, jb)
                        if g == NG - 1 and unit_exists(j + 1, last):
                            send_max(b + 1, j + 1)

                rounds(sp, body)

            @block.tensor
            def _(pe):
                pe.wait_ge(const_ld, 16 * (4 + 2 * PROJ))

                def scores(it, j, tt, heads):
                    s = j % RING
                    u = (it + j // RING) * RING + j % RING
                    for h in heads:
                        if tt == 0 and h == 0:
                            pe.wait_ge(stack_ld[s], 96 * (it + j // RING + 1))
                        n = u * (G * KT) + tt * G + h
                        if begun(n - 1):
                            pe.wait_ge(max_done, n - 1)
                        nc.tensor.matmul(s1_ps[:, (tt * G + h) % 2, :],
                                         q_st[0:MROW, s, h, tt * P:(tt + 1) * P],
                                         k_st[0:MROW, s, h, :], start=True, stop=True).then_inc(s1_full, 1)

                def scores_t(it, j, st, pair):
                    s, u = j % RING, it * RING + j
                    if st == 0 and pair == 0:
                        pe.wait_ge(m_ld, 16 * MPARTS * (it * NBS + j // NG + 1))
                    if begun((u * KT + st) * 2 + pair - 1):
                        pe.wait_ge(exp_done, (u * KT + st) * 2 + pair - 1)
                    for i in range(2):
                        h = pair * 2 + i
                        mm = nc.tensor.matmul(st_ps[:, pair, i, :],
                                              k_st[0:MROW + MPARTS, s, h, st * P:(st + 1) * P],
                                              q_st[0:MROW + MPARTS, s, h, :], start=True, stop=True)
                    mm.then_inc(st_full, 1)

                def values(it, j, st, half):
                    queries = slice(half * L // 2, (half + 1) * L // 2)
                    u = it * RING + j
                    n = u * KT + st
                    if st == 0 and half == 0:
                        pe.wait_ge(v_placed, it * NBS + j // NG + 1)
                        if begun(u):
                            pe.wait_ge(o_copied, u)
                    if half == 0:
                        pe.wait_ge(exp_done, 2 * (n + 1))
                    for h in range(G):
                        mm = nc.tensor.matmul(o_ps[32 * h:32 * h + 32, queries],
                                              v_aug[:, (j // NG) % NBS, st, (j % NG) * G + h, :],
                                              probs[:, st % 2, h, queries], start=(st == 0 and half == 0), stop=(st == KT - 1),
                                              skip_group_check=True)
                    if half == 1:
                        mm.then_inc(av_done, 1)

                def transpose_max(b, i):
                    pe.wait_ge(max_done, (b + 1) * NG * G * KT)
                    if begun(b - 1):
                        pe.wait_ge(o_normed, b - 1)
                    pe.sem_inc(passed_pe, 1)
                    nc.tensor.transpose(misc_ps[0:H * KT, 0:P], maxes[:, i % 2, :], ident[:, :]
                                        ).then_inc(mT_full, 1)

                def select(b, i, sel, done):
                    for g in range(NG):
                        mm = nc.tensor.matmul(misc_ps[g * G * C:(g + 1) * G * C, :], sel[:, :],
                                              o_raw[:, i % 2, g, :], start=True, stop=True,
                                              skip_group_check=True)
                    mm.then_inc(done, 1)

                def select_sums(b, i, more, tiles):
                    if 0 in tiles:
                        pe.wait_ge(o_copied, (b + 1) * NG)
                        if begun(more):
                            pe.wait_ge(m_step, more)
                        if PROJ:
                            if begun(b):
                                pe.wait_ge(y_done, b)
                        else:
                            if begun(b):
                                pe.wait_ge(o_normed, b)
                    for kt in tiles:
                        for g in range(NG):
                            c = kt * H + g * G
                            mm = nc.tensor.matmul(misc_ps[:, c:c + G], o_raw[:, i % 2, g, kt * P:(kt + 1) * P],
                                                  sel_s[:, :].rearrange("p (h c) -> p h c", c=C)[:, :, 0],
                                                  start=True, stop=True, skip_group_check=True)
                    if KT - 1 in tiles:
                        mm.then_inc(sums_full, 1)

                def expand(b):
                    pe.wait_ge(recip_done, b + 1)
                    for kt in range(KT):
                        mm = nc.tensor.matmul(misc_ps[:, kt * P:(kt + 1) * P], recip_q[:, kt * P:(kt + 1) * P],
                                              ident[:, :], start=True, stop=True, skip_group_check=True)
                    mm.then_inc(expand_full, 1)

                def select_o(b, i):
                    pe.wait_ge(recip_copied, b + 1)
                    select(b, i, sel_o, o_full)

                def project(b, more):
                    pe.wait_ge(o_normed, b + 1)
                    if begun(more):
                        pe.wait_ge(m_step, more)
                    nc.tensor.matmul(misc_ps[:, :], wo[:, :], o_norm[:, :], start=True, stop=True
                                     ).then_inc(proj_full, 1)

                for j in range(AHEAD):
                    for tt in range(KT):
                        scores(0, j, tt, range(G))
                    if j == NG - 1:
                        transpose_max(0, 0)

                def body(it, first, last):
                    for j in range(RING):
                        b, jb, g = it * NBS + j // NG, j // NG, j % NG
                        finish = not (first and jb == 0)
                        more = unit_exists(j - g + NG, last)
                        for st in range(KT):
                            ahead = unit_exists(j + AHEAD, last)
                            for pair in range(2):
                                if ahead:
                                    scores(it, j + AHEAD, st, [2 * pair])
                                scores_t(it, j, st, pair)
                                if ahead:
                                    scores(it, j + AHEAD, st, [2 * pair + 1])
                                if st > 0:
                                    values(it, j, st - 1, pair)
                                elif not (first and j == 0):
                                    if j == 0:
                                        values(it - 1, RING - 1, KT - 1, pair)
                                    else:
                                        values(it, j - 1, KT - 1, pair)
                            if finish and NG == 2 and g == 0 and st == 2:
                                select_sums(b - 1, jb + 1, 5 * (b + 1), range(KT))
                            if finish and NG == 4 and (g, st) in SUMS_AT:
                                select_sums(b - 1, jb + 1, 5 * (b + 1), [SUMS_AT.index((g, st))])
                            if finish and (g, st) == EXPAND_AT:
                                expand(b - 1)
                            if finish and (g, st) == SELECT_AT:
                                select_o(b - 1, jb + 1)
                            if more and g == NG - 1 and st == 1:
                                transpose_max(b + 1, jb + 1)
                            if PROJ and finish and g == NG - 1 and st == 2:
                                project(b - 1, 5 * (b + 1) + 1 if more else 0)

                rounds(pe, body)
                values(UNITS // RING - 1, RING - 1, KT - 1, 0)
                values(UNITS // RING - 1, RING - 1, KT - 1, 1)
                select_sums(B - 1, B - 1, 0, range(KT))
                expand(B - 1)
                select_o(B - 1, B - 1)
                if PROJ:
                    project(B - 1, 0)

            @block.scalar
            def _(act):
                def exps(it, j, st):
                    for pair in range(2):
                        n = (it * RING + j) * KT + st
                        act.wait_ge(st_full, 2 * n + pair + 1)
                        if begun(n - 1):
                            act.wait_ge(av_done, n - 1)
                        nc.scalar.activation(probs[:, st % 2, 2 * pair:2 * pair + 2, :],
                                             st_ps[:, pair, :, :], ACT.Exp).then_inc(exp_done, 1)

                def copy_o(it, j):
                    u, b = it * RING + j, it * NBS + j // NG
                    act.wait_ge(av_done, (u + 1) * KT)
                    if j % NG == 0:
                        if begun(b - 1):
                            act.wait_ge(o_full, b - 1)
                    nc.scalar.activation(o_raw[:, (j // NG) % 2, j % NG, :], o_ps[:, :], ACT.Copy
                                         ).then_inc(o_copied, 1)

                def copy_recip(b):
                    act.wait_ge(expand_full, b + 1)
                    if begun(b):
                        act.wait_ge(o_normed, b)
                    nc.scalar.activation(recip[:, :], misc_ps[:, :], ACT.Copy).then_inc(recip_copied, 1)

                def body(it, first, last):
                    for j in range(RING):
                        b, g = it * NBS + j // NG, j % NG
                        for st in range(KT):
                            exps(it, j, st)
                            if (g, st) == COPY_AT and not (first and j < NG):
                                copy_recip(b - 1)
                            if st == 0 and not (first and j == 0):
                                if j == 0:
                                    copy_o(it - 1, RING - 1)
                                else:
                                    copy_o(it, j - 1)

                rounds(act, body)
                copy_o(UNITS // RING - 1, RING - 1)
                copy_recip(B - 1)

            @block.vector
            def _(dve):
                k_flat = k_st[:, :, :, :].rearrange("p u h t -> p (u h t)")
                nc.vector.memset(k_flat[MROW:MROW + MPARTS, :].bitcast(F32), TWO_ONES).then_inc(memset_done, 1)
                if ROWS < MROW:
                    nc.vector.memset(k_flat[0:MROW, :].bitcast(U32), 0).then_inc(memset_done, 1)
                dve.wait_ge(const_ld, 16 * (4 + 2 * PROJ))

                def row_max(it, j, tt, h):
                    u = (it + j // RING) * RING + j % RING
                    n = u * (G * KT) + tt * G + h
                    jb, g = j // NG, j % NG
                    if tt == 0 and h == 0 and g == 0:
                        if begun((it * NBS + jb) - 1):
                            dve.wait_ge(mT_full, (it * NBS + jb) - 1)
                    dve.wait_ge(s1_full, n + 1)
                    c = (g * G + h) * KT + tt
                    nc.vector.reduce_max(maxes[:, jb % 2, c:c + 1], s1_ps[:, (tt * G + h) % 2, :], AX.X
                                         ).then_inc(max_done, 1)

                def split_max(b, i, steps):
                    out = m_parts[:, i % 2, :, :]
                    if 0 in steps:
                        dve.wait_ge(mT_full, b + 1)
                        if begun(16 * MPARTS * (b - 1)):
                            dve.wait_ge(m_ld, 16 * MPARTS * (b - 1))
                        nc.vector.tensor_scalar(m_neg[:, :], misc_ps[0:H * KT, 0:P], -1.0, None, ALU.mult
                                                ).then_inc(m_step, 1)
                    if 1 in steps:
                        dve.wait_ge(m_step, b * 5 + 1)
                        nc.vector.tensor_copy(out[:, 0, :], m_neg[:, :]).then_inc(m_step, 1)
                    if 2 in steps:
                        dve.wait_ge(m_step, b * 5 + 2)
                        nc.vector.tensor_tensor(m_rest[:, :], m_neg[:, :], out[:, 0, :], ALU.subtract
                                                ).then_inc(m_step, 1)
                    if 3 in steps:
                        dve.wait_ge(m_step, b * 5 + 3)
                        nc.vector.tensor_copy(out[:, 1, :], m_rest[:, :]).then_inc(m_step, 1)
                    if 4 in steps:
                        dve.wait_ge(m_step, b * 5 + 4)
                        nc.vector.tensor_tensor(out[:, 2, :], m_rest[:, :], out[:, 1, :], ALU.subtract
                                                ).then_inc(m_step, 1)

                def reciprocals(b):
                    dve.wait_ge(sums_full, b + 1)
                    nc.vector.reciprocal(recip_small[:, :], misc_ps[:, 0:KT * H]).then_inc(small_done, 1)
                    dve.wait_ge(small_done, b + 1)
                    if begun(b):
                        dve.wait_ge(expand_full, b)
                    nc.vector.tensor_copy(recip_q[:, :].rearrange("p (h c) -> p h c", c=C),
                                          recip_small[:, :].rearrange("p (h o) -> p h o", o=1)
                                          .to_broadcast([P, KT * H, C])).then_inc(recip_done, 1)

                def norm_o(b):
                    dve.wait_ge(o_full, b + 1)
                    dve.wait_ge(recip_copied, b + 1)
                    if PROJ:
                        if begun(b):
                            dve.wait_ge(proj_full, b)
                    nc.vector.tensor_tensor(o_norm[:, :], misc_ps[:, :], recip[:, :], ALU.mult
                                            ).then_inc(o_normed, 1)

                def layer_norm(b, i, rnd, steps):
                    if 0 in steps:
                        dve.wait_ge(x_ld[i % 2], 16 * (rnd + 1))
                        if begun(b):
                            dve.wait_ge(x_done, b)
                        if PROJ:
                            dve.wait_ge(proj_full, b + 1)
                            nc.vector.scalar_tensor_tensor(out=y[:, :], in0=misc_ps[:, :], scalar=bo[:, 0:1],
                                                           in1=x_res[:, i % 2, :], op0=ALU.add, op1=ALU.add
                                                           ).then_inc(y_done, 1)
                        else:
                            dve.wait_ge(o_normed, b + 1)
                            nc.vector.tensor_tensor(y[:, :], o_norm[:, :], x_res[:, i % 2, :], ALU.add
                                                    ).then_inc(y_done, 1)
                    if 1 in steps:
                        dve.wait_ge(y_done, b + 1)
                        nc.vector.bn_stats(stats[:, :], y[:, :]).then_inc(ln_step, 1)
                    if 2 in steps:
                        dve.wait_ge(ln_step, b * 3 + 1)
                        dve.sem_inc(passed_dve, 1)
                        nc.vector.bn_aggr(mv[:, :], stats[:, :]).then_inc(ln_step, 1)
                    if 3 in steps:
                        dve.wait_ge(ln_step, b * 3 + 2)
                        nc.vector.tensor_scalar(var_eps[:, :], mv[:, 1:2], LN_EPS, None, ALU.add).then_inc(ln_step, 1)

                def finish_norm(b, i, rnd):
                    dve.wait_ge(rstd_done, b + 1)
                    if begun(16 * b):
                        dve.wait_ge(x_stored, 16 * b)
                    nc.vector.tensor_scalar(x_new[:, i % 2, :], y[:, :], mv[:, 0:1], rstd[:, 0:1],
                                            ALU.subtract, ALU.mult).then_inc(x_done, 1)

                for j in range(AHEAD):
                    for tt in range(KT):
                        for h in range(G):
                            row_max(0, j, tt, h)
                        if j == NG and tt == 0:
                            split_max(0, 0, range(5))

                def rnd_of(it, jb):
                    return it * (NBS // 2) + jb // 2

                def body(it, first, last):
                    for j in range(RING):
                        b, jb, g = it * NBS + j // NG, j // NG, j % NG
                        finish = not (first and jb == 0)
                        more = unit_exists(j - g + NG, last)
                        prev = (it, jb - 1) if jb else (it - 1, NBS - 1)
                        lng, lnt = (NG - 1, 3) if PROJ else (2, 3)
                        for tt in range(KT):
                            for h in range(G):
                                if unit_exists(j + AHEAD, last):
                                    row_max(it, j + AHEAD, tt, h)
                                if finish and (g, tt, h) == ((0, 3, 0) if NG == 2 else (1, 2, 0)):
                                    reciprocals(b - 1)
                                if finish and (g, tt) == NORM_AT and h == 0:
                                    norm_o(b - 1)
                                if more and g == NG - 1 and tt == 1 and h == G - 1:
                                    split_max(b + 1, jb + 1, [0])
                                if more and g == NG - 1 and tt == 2:
                                    split_max(b + 1, jb + 1, [h + 1])
                                if finish and g == lng and tt == lnt and h < 3:
                                    layer_norm(b - 1, jb + 1, rnd_of(*prev), [h] if h < 2 else [2, 3])
                                if finish and g == lng and tt == lnt and h == 3:
                                    finish_norm(b - 1, jb + 1, rnd_of(*prev))

                rounds(dve, body)
                reciprocals(B - 1)
                norm_o(B - 1)
                layer_norm(B - 1, B - 1, B // 2 - 1, range(4))
                finish_norm(B - 1, B - 1, B // 2 - 1)

            @block.gpsimd
            def _(pool):
                if ROWS < MROW:
                    q_flat = q_st[:, :, :, :].rearrange("p u h t -> p (u h t)")
                    nc.gpsimd.memset(q_flat[0:MROW, :].bitcast(U32), 0).then_inc(memset_done, 1)
                for c in range(NBS):
                    op = nc.gpsimd.memset(v_aug[:, c, :, :, :], 1.0)
                op.then_inc(ones_done, 1)
                pool.wait_ge(ones_done, 1)
                pool.wait_ge(const_ld, 16 * (4 + 2 * PROJ))

                def place_v(it, jb):
                    b = it * NBS + jb
                    pool.wait_ge(v_ld[jb % 2], 16 * (it * (NBS // 2) + jb // 2 + 1))
                    if begun((b - NBS + 1) * NG * KT):
                        pool.wait_ge(av_done, (b - NBS + 1) * NG * KT)
                    pool.sem_inc(passed_pool, 1)
                    for kt in range(KT):
                        op = nc.gpsimd.tensor_copy(v_aug[:, jb % NBS, kt, :, 0:C],
                                                   v_raw[:, jb % 2, kt, :].rearrange("p (h c) -> p h c", c=C))
                    op.then_inc(v_placed, 1)

                def power(b, i, rnd):
                    pool.wait_ge(ln_step, (b + 1) * 3)
                    nc.gpsimd.tensor_tensor(rstd[:, :], var_eps[:, :], minus_half[:, :], ALU.pow
                                            ).then_inc(rstd_done, 1)
                    pool.wait_ge(x_done, b + 1)
                    pool.dma_start(x_out[bass.ds(b, 1), :, :].rearrange("o p t -> p (o t)"),
                                   x_new[:, i % 2, :]).then_inc(x_stored, 16)

                place_v(0, 0)

                def body(it, first, last):
                    for jb in range(NBS):
                        if not (last and jb == NBS - 1):
                            if jb == NBS - 1:
                                place_v(it + 1, 0)
                            else:
                                place_v(it, jb + 1)
                        if not (first and jb == 0):
                            pit, pj = (it, jb - 1) if jb else (it - 1, NBS - 1)
                            power(it * NBS + jb - 1, jb + 1, pit)

                rounds(pool, body)
                power(B - 1, B - 1, 0)
                pool.wait_ge(x_stored, 16 * B)


def prepare(nc, tag, kind, H, q_parts, k_parts, x_in, ctx_in=None, v_out=None, w=None, perm_d=None,
            cos_d=None, sin_d=None, bias_d=None, v_bias_d=None):
    L = 512
    C = P // H
    KC = P if kind == "gqa" else L
    W = L + KC
    DK = D // P
    with Phase(nc) as ph:
        sem, sb = ph.sem, ph.sb
        perm = sb(f"{tag}_perm", [P, P])
        cos = sb(f"{tag}_cos", [P, W])
        sin = sb(f"{tag}_sin", [P, W])
        consts = [(perm, perm_d), (cos, cos_d), (sin, sin_d)]
        raw = sb(f"{tag}_raw", [P, 2, W])
        times_cos = sb(f"{tag}_times_cos", [P, 2, W])
        times_sin = sb(f"{tag}_times_sin", [P, 2, W])
        v_sb = sb(f"{tag}_v_sb", [P, 2, KC])
        if kind == "gqa":
            wq = sb(f"{tag}_wq", [P, DK, D])
            wk = sb(f"{tag}_wk", [P, DK, P])
            wv = sb(f"{tag}_wv", [P, DK, P])
            consts += [(wq, w[0]), (wk, w[1]), (wv, w[2])]
            xin = sb(f"{tag}_xin", [P, 2, DK, P])
        else:
            xin = sb(f"{tag}_xin", [P, 2, L])
            cin = sb(f"{tag}_cin", [P, 2, L])
        if kind == "cross":
            wq = sb(f"{tag}_wq", [P, P])
            wk = sb(f"{tag}_wk", [P, P])
            wv = sb(f"{tag}_wv", [P, P])
            bias = sb(f"{tag}_bias", [P, 2])
            v_bias = sb(f"{tag}_v_bias", [P, L])
            consts += [(wq, w[0]), (wk, w[1]), (wv, w[2]), (bias, bias_d), (v_bias, v_bias_d)]
        whole = sb(f"{tag}_whole", [P, 2, W])
        rest = sb(f"{tag}_rest", [P, 2, W])
        part = sb(f"{tag}_part", [P, 2, 3, W], BF16)
        qk_ps = ph.ps(f"{tag}_qk_ps", [P, 2, L])
        v_ps = ph.ps(f"{tag}_v_ps", [P, L])
        sw_ps = ph.ps(f"{tag}_sw_ps", [P, 2, 2, L])

        const_ld = sem(f"{tag}_const_ld")
        x_ld = [sem(f"{tag}_x_ld{i}") for i in range(2)]
        stored = [sem(f"{tag}_stored{i}") for i in range(2)]
        v_stored = [sem(f"{tag}_v_stored{i}") for i in range(2)]
        qk_full = sem(f"{tag}_qk_full")
        v_full = sem(f"{tag}_v_full")
        raw_done = sem(f"{tag}_raw_done")
        v_done = sem(f"{tag}_v_done")
        swapped = sem(f"{tag}_swapped")
        cos_done = sem(f"{tag}_cos_done")
        sin_done = sem(f"{tag}_sin_done")
        whole_done = sem(f"{tag}_whole_done")
        part1 = sem(f"{tag}_part1")
        rest_done = sem(f"{tag}_rest_done")
        part2 = sem(f"{tag}_part2")
        part3 = sem(f"{tag}_part3")

        def pairs(eng, body):
            body(0, 0)
            body(1, 1)
            with eng.Fori(1, B // 2) as it:
                body(it * 2, 0)
                body(it * 2 + 1, 1)

        with nc.Block() as block:
            @block.sync
            def _(sp):
                for dst, src in consts:
                    if len(dst.shape) == 3:
                        sp.dma_start(dst[:, :, :], src).then_inc(const_ld, 16)
                    else:
                        sp.dma_start(dst[:, :], src).then_inc(const_ld, 16)

                def store(b, i):
                    sp.wait_ge(v_done, b + 1)
                    if kind == "gqa":
                        sp.dma_start(v_out[bass.ds(b, 1), :, :].rearrange("o t c -> t (o c)"), v_sb[:, i, :]
                                     ).then_inc(v_stored[i], 16)
                    else:
                        sp.dma_start(v_out[bass.ds(b, 1), :, :].rearrange("o (k p) c -> p (o k) c", p=P),
                                     v_sb[:, i, :].rearrange("p (k c) -> p k c", c=P)
                                     ).then_inc(v_stored[i], 16)
                    sp.wait_ge(part3, b + 1)
                    for out, c0, n in ((q_parts, 0, L), (k_parts, L, KC)):
                        for p in range(3):
                            dst = out[bass.ds(b, 1), p * C:(p + 1) * C, :].rearrange("o c (h t) -> (o h) c t", t=n)
                            sp.dma_start(dst, part[:, i, p, c0:c0 + n]).then_inc(stored[i], 16)

                pairs(sp, store)
                for i in range(2):
                    sp.wait_ge(stored[i], 96 * (B // 2))
                    sp.wait_ge(v_stored[i], 16 * (B // 2))

            def in_loaded(eng, b, i):
                n = 16 if kind == "gqa" else 32
                eng.wait_ge(x_ld[i], (b - i) * (n // 2) + n)

            @block.tensor
            def _(pe):
                pe.wait_ge(const_ld, 16 * len(consts))

                def project(b, i):
                    in_loaded(pe, b, i)
                    if begun(b):
                        pe.wait_ge(raw_done, b)
                    if kind == "gqa":
                        for f in range(5):
                            for dk in range(DK):
                                lhs = wq[:, dk, f * P:(f + 1) * P] if f < 4 else wk[:, dk, :]
                                dst = qk_ps[:, 0, f * P:(f + 1) * P] if f < 4 else qk_ps[:, 1, 0:P]
                                mm = nc.tensor.matmul(dst, lhs, xin[:, i, dk, :], start=(dk == 0),
                                                      stop=(dk == DK - 1), skip_group_check=True)
                        mm.then_inc(qk_full, 1)
                        if begun(b):
                            pe.wait_ge(v_done, b)
                        for dk in range(DK):
                            mm = nc.tensor.matmul(v_ps[:, 0:P], xin[:, i, dk, :], wv[:, dk, :],
                                                  start=(dk == 0), stop=(dk == DK - 1))
                        mm.then_inc(v_full, 1)
                    else:
                        nc.tensor.matmul(qk_ps[:, 0, :], wq[:, :], xin[:, i, :], start=True, stop=True)
                        nc.tensor.matmul(qk_ps[:, 1, :], wk[:, :], cin[:, i, :], start=True, stop=True
                                         ).then_inc(qk_full, 1)
                        if begun(b):
                            pe.wait_ge(v_done, b)
                        for kt in range(L // P):
                            mm = nc.tensor.matmul(v_ps[:, kt * P:(kt + 1) * P], cin[:, i, kt * P:(kt + 1) * P],
                                                  wv[:, :], start=True, stop=True, skip_group_check=True)
                        mm.then_inc(v_full, 1)

                def swap(b, i):
                    pe.wait_ge(raw_done, b + 1)
                    if begun(b - 1):
                        pe.wait_ge(sin_done, b - 1)
                    nc.tensor.matmul(sw_ps[:, i, 0, :], perm[:, :], raw[:, i, 0:L], start=True, stop=True)
                    nc.tensor.matmul(sw_ps[:, i, 1, 0:KC], perm[:, :], raw[:, i, L:W], start=True, stop=True
                                     ).then_inc(swapped, 1)

                project(0, 0)

                def body(b, i):
                    swap(b, i)
                    project(b + 1, 1 - i)

                body(0, 0)
                body(1, 1)
                with pe.Fori(1, B // 2 - 1) as it:
                    body(it * 2, 0)
                    body(it * 2 + 1, 1)
                body(B - 2, 0)
                swap(B - 1, 1)

            @block.scalar
            def _(act):
                act.wait_ge(const_ld, 16 * len(consts))

                def load(b, i):
                    if begun(b - 1):
                        act.wait_ge(v_full, b - 1)
                    if kind == "gqa":
                        act.dma_start(xin[:, i, :, :], x_in[bass.ds(b, 1), :, :, :].rearrange("o p k t -> p (o k) t")
                                     ).then_inc(x_ld[i], 16)
                    else:
                        act.dma_start(xin[:, i, :], x_in[bass.ds(b, 1), :, :].rearrange("o p t -> p (o t)")
                                     ).then_inc(x_ld[i], 16)
                        act.dma_start(cin[:, i, :], ctx_in[bass.ds(b, 1), :, :].rearrange("o p t -> p (o t)")
                                     ).then_inc(x_ld[i], 16)

                def first(b, i):
                    act.wait_ge(qk_full, b + 1)
                    if begun(b - 1):
                        act.wait_ge(swapped, b - 1)
                    if begun(b - 1):
                        act.wait_ge(cos_done, b - 1)
                    if kind == "gqa":
                        nc.scalar.activation(raw[:, i, :], qk_ps[:, :, :].rearrange("p a t -> p (a t)")[:, 0:W],
                                             ACT.Copy).then_inc(raw_done, 1)
                        act.wait_ge(v_full, b + 1)
                        if begun((b - i) * 8):
                            act.wait_ge(v_stored[i], (b - i) * 8)
                        nc.scalar.activation(v_sb[:, i, :], v_ps[:, 0:P], ACT.Copy).then_inc(v_done, 1)
                    else:
                        nc.scalar.activation(raw[:, i, 0:L], qk_ps[:, 0, :], ACT.Identity, bias=bias[:, 0:1])
                        nc.scalar.activation(raw[:, i, L:W], qk_ps[:, 1, :], ACT.Identity, bias=bias[:, 1:2]
                                             ).then_inc(raw_done, 1)

                def second(b, i):
                    act.wait_ge(whole_done, b + 1)
                    if begun((b - i) * 48):
                        act.wait_ge(stored[i], (b - i) * 48)
                    nc.scalar.activation(part[:, i, 0, :], whole[:, i, :], ACT.Copy).then_inc(part1, 1)
                    act.wait_ge(rest_done, b + 1)
                    nc.scalar.activation(part[:, i, 1, :], rest[:, i, :], ACT.Copy).then_inc(part2, 1)

                load(0, 0)
                load(1, 1)
                first(0, 0)

                def body(b, i):
                    load(b + 2, i)
                    first(b + 1, 1 - i)
                    second(b, i)

                body(0, 0)
                body(1, 1)
                with act.Fori(1, B // 2 - 1) as it:
                    body(it * 2, 0)
                    body(it * 2 + 1, 1)
                first(B - 1, 1)
                second(B - 2, 0)
                second(B - 1, 1)

            @block.vector
            def _(dve):
                dve.wait_ge(const_ld, 16 * len(consts))

                def take_v(b, i):
                    dve.wait_ge(v_full, b + 1)
                    if begun((b - i) * 8):
                        dve.wait_ge(v_stored[i], (b - i) * 8)
                    nc.vector.tensor_tensor(v_sb[:, i, :], v_ps[:, :], v_bias[:, :], ALU.add).then_inc(v_done, 1)

                def rope(b, i):
                    dve.wait_ge(swapped, b + 1)
                    nc.vector.tensor_tensor(times_sin[:, i, :], sw_ps[:, i, :, :].rearrange("p a t -> p (a t)")[:, 0:W],
                                            sin[:, :], ALU.mult).then_inc(sin_done, 1)
                    dve.wait_ge(sin_done, b + 1)
                    dve.wait_ge(cos_done, b + 1)
                    if begun(b - 1):
                        dve.wait_ge(part3, b - 1)
                    nc.vector.tensor_tensor(whole[:, i, :], times_cos[:, i, :], times_sin[:, i, :], ALU.add
                                            ).then_inc(whole_done, 1)

                def subtract(b, i):
                    dve.wait_ge(part1, b + 1)
                    nc.vector.tensor_tensor(rest[:, i, :], whole[:, i, :], part[:, i, 0, :], ALU.subtract
                                            ).then_inc(rest_done, 1)

                if kind == "cross":
                    take_v(0, 0)

                def body(b, i):
                    rope(b, i)
                    if kind == "cross" and not (isinstance(b, int) and b == B - 1):
                        take_v(b + 1, 1 - i)
                    subtract(b, i)

                body(0, 0)
                body(1, 1)
                with dve.Fori(1, B // 2 - 1) as it:
                    body(it * 2, 0)
                    body(it * 2 + 1, 1)
                body(B - 2, 0)
                body(B - 1, 1)

            @block.gpsimd
            def _(pool):
                pool.wait_ge(const_ld, 16 * len(consts))

                def cosines(b, i):
                    pool.wait_ge(raw_done, b + 1)
                    if begun(b - 1):
                        pool.wait_ge(whole_done, b - 1)
                    nc.gpsimd.tensor_tensor(times_cos[:, i, :], raw[:, i, :], cos[:, :], ALU.mult).then_inc(cos_done, 1)

                def last_part(b, i):
                    pool.wait_ge(part2, b + 1)
                    nc.gpsimd.tensor_tensor(part[:, i, 2, :], rest[:, i, :], part[:, i, 1, :], ALU.subtract
                                            ).then_inc(part3, 1)

                cosines(0, 0)

                def body(b, i):
                    cosines(b + 1, 1 - i)
                    last_part(b, i)

                body(0, 0)
                body(1, 1)
                with pool.Fori(1, B // 2 - 1) as it:
                    body(it * 2, 0)
                    body(it * 2 + 1, 1)
                body(B - 2, 0)
                last_part(B - 1, 1)


def causal_gqa(nc, tag, H, x_in, q_parts, k_parts, v_rows, x_out, ident_d, sel_o_d, sel_s_d,
               half_d, ident_bf_d, mask_d, mask_t_d, wo_d, bo_d):
    C = P // H
    I = 4
    L = I * P
    G = 4
    NG = H // G
    UNITS = B * NG
    RING = 8
    NBS = RING // NG
    AHEAD = NG + 1
    MROW, MPARTS = 96, 3
    NCONST = 9

    with Phase(nc) as ph:
        sem, sb = ph.sem, ph.sb
        q_st = sb(f"{tag}_q_st", [P, RING, G, L], BF16)
        k_st = sb(f"{tag}_k_st", [P, RING, G, P], BF16)
        v_raw = sb(f"{tag}_v_raw", [P, 2, P])
        v_aug = sb(f"{tag}_v_aug", [P, NBS, H, 32])
        probs = sb(f"{tag}_probs", [P, 2, G, L])
        o_raw = sb(f"{tag}_o_raw", [P, 2, NG, L])
        maxes = sb(f"{tag}_maxes", [P, 2, H * I])
        m_neg = sb(f"{tag}_m_neg", [H * I, P])
        m_rest = sb(f"{tag}_m_rest", [H * I, P])
        m_parts = sb(f"{tag}_m_parts", [H * I, 2, MPARTS, P], BF16)
        recip = sb(f"{tag}_recip", [P, L])
        o_norm = sb(f"{tag}_o_norm", [P, L])
        x_res = sb(f"{tag}_x_res", [P, 2, D])
        x_bias = sb(f"{tag}_x_bias", [P, D])
        y = sb(f"{tag}_y", [P, D])
        stats = sb(f"{tag}_stats", [P, 6])
        mv = sb(f"{tag}_mv", [P, 2])
        var_eps = sb(f"{tag}_var_eps", [P, 1])
        rstd = sb(f"{tag}_rstd", [P, 1])
        x_new = sb(f"{tag}_x_new", [P, 2, D])
        ident = sb(f"{tag}_ident", [P, P])
        ident_bf = sb(f"{tag}_ident_bf", [P, P], BF16)
        mask = sb(f"{tag}_mask", [P, P], BF16)
        mask_t = sb(f"{tag}_mask_t", [P, P], BF16)
        sel_o = sb(f"{tag}_sel_o", [P, G * C])
        sel_s = sb(f"{tag}_sel_s", [P, G * C])
        minus_half = sb(f"{tag}_minus_half", [P, 1])
        wo = sb(f"{tag}_wo", [P, I, D])
        bo = sb(f"{tag}_bo", [P, D])

        s1_ps = ph.ps(f"{tag}_s1", [P, 2, L])
        st_ps = ph.ps(f"{tag}_st", [P, 2, 2, L])
        o_ps = ph.ps(f"{tag}_o", [P, L])
        misc_ps = ph.ps(f"{tag}_misc", [P, L])

        const_ld = sem(f"{tag}_const_ld")
        passed_dve = sem(f"{tag}_passed_dve")
        passed_pool = sem(f"{tag}_passed_pool")
        memset_done = sem(f"{tag}_memset_done")
        ones_done = sem(f"{tag}_ones_done")
        stack_ld = [sem(f"{tag}_stack_ld{i}") for i in range(RING)]
        v_ld = [sem(f"{tag}_v_ld{i}") for i in range(2)]
        v_placed = sem(f"{tag}_v_placed")
        x_ld = [sem(f"{tag}_x_ld{i}") for i in range(2)]
        x_biased = sem(f"{tag}_x_biased")
        s1_full = sem(f"{tag}_s1_full")
        max_done = sem(f"{tag}_max_done")
        st_full = sem(f"{tag}_st_full")
        exp_done = sem(f"{tag}_exp_done")
        av_done = sem(f"{tag}_av_done")
        o_copied = sem(f"{tag}_o_copied")
        sums_full = sem(f"{tag}_sums_full")
        recip_done = sem(f"{tag}_recip_done")
        o_full = sem(f"{tag}_o_full")
        o_normed = sem(f"{tag}_o_normed")
        proj_full = sem(f"{tag}_proj_full")
        mT_full = sem(f"{tag}_mT_full")
        m_step = sem(f"{tag}_m_step")
        m_ld = sem(f"{tag}_m_ld")
        y_done = sem(f"{tag}_y_done")
        ln_step = sem(f"{tag}_ln_step")
        rstd_done = sem(f"{tag}_rstd_done")
        x_done = sem(f"{tag}_x_done")
        x_stored = [sem(f"{tag}_x_stored{i}") for i in range(2)]

        def rounds(eng, body):
            body(0, True, False)
            with eng.Fori(1, UNITS // RING - 1) as it:
                body(it, False, False)
            body(UNITS // RING - 1, False, True)

        def unit_exists(u_off, last):
            return not (last and u_off >= RING)

        with nc.Block() as block:
            @block.sync
            def _(sp):
                for dst, src in ((ident, ident_d), (sel_o, sel_o_d), (sel_s, sel_s_d), (minus_half, half_d),
                                 (ident_bf, ident_bf_d), (mask, mask_d), (mask_t, mask_t_d), (bo, bo_d)):
                    sp.dma_start(dst[:, :], src).then_inc(const_ld, 16)
                sp.dma_start(wo[:, :, :], wo_d).then_inc(const_ld, 16)

                def load_stack(it, j):
                    b, g, s = it * NBS + j // NG, j % NG, j % RING

                    def parts(src, p, n, width):
                        heads = slice(g * G * width, (g + 1) * G * width)
                        return src[bass.ds(b, 1), p * C:(p + n) * C, heads].rearrange("o c t -> (o c) t")

                    row = 0
                    for n in (3, 2, 1):
                        sp.dma_start(q_st[row:row + n * C, s, :, :].rearrange("p h t -> p (h t)"),
                                     parts(q_parts, 0, n, L)).then_inc(stack_ld[s], 16)
                        a = parts(k_parts, 3 - n, 1, P)
                        a = bass.AP(a.tensor, a.offset, [[0, n]] + [list(x) for x in a.ap])
                        sp.dma_start(k_st[row:row + n * C, s, :, :].rearrange("p h t -> p (h t)"),
                                     a).then_inc(stack_ld[s], 16)
                        row += n * C

                def load_v(b, i):
                    sp.dma_start(v_raw[:, i % 2, :], v_rows[bass.ds(b, 1), :, :].rearrange("o p c -> p (o c)")
                                 ).then_inc(v_ld[i % 2], 16)

                def load_x(b, i):
                    sp.dma_start(x_res[:, i % 2, :], x_in[bass.ds(b, 1), :, :].rearrange("o p t -> p (o t)")
                                 ).then_inc(x_ld[i % 2], 16)

                def send_max(b, j0):
                    sp.wait_ge(m_step, (b + 1) * 5)
                    s0 = j0 % RING
                    for p in range(MPARTS):
                        dst = q_st[MROW + p:MROW + p + 1, s0:s0 + NG, :, :].rearrange("p u h t -> p (u h t)")
                        sp.dma_start(dst, m_parts[:, (j0 // NG) % 2, p, :]).then_inc(m_ld, 16)

                sp.wait_ge(memset_done, 1)
                load_stack(0, 0)
                load_v(0, 0)
                for j in range(1, RING - 1):
                    load_stack(0, j)
                send_max(0, 0)

                def body(it, first, last):
                    for j in range(RING):
                        b, jb, g = it * NBS + j // NG, j // NG, j % NG
                        if unit_exists(j + RING - 1, last):
                            if begun(it * RING + j):
                                sp.wait_ge(av_done, it * RING + j)
                            load_stack(it + (j + RING - 1) // RING, (j + RING - 1) % RING)
                        if g == 0 and unit_exists(j + NG, last):
                            if begun(b):
                                sp.wait_ge(v_placed, b)
                            load_v(b + 1, jb + 1)
                        if g == 0:
                            if begun(b - 1):
                                sp.wait_ge(x_biased, b - 1)
                            load_x(b, jb)
                        if g == NG - 1 and unit_exists(j + 1, last):
                            send_max(b + 1, j + 1)

                rounds(sp, body)

            @block.tensor
            def _(pe):
                pe.wait_ge(const_ld, 16 * NCONST)

                def scores(it, j, h):
                    s = j % RING
                    n = ((it + j // RING) * RING + j % RING) * G + h
                    if h == 0:
                        pe.wait_ge(stack_ld[s], 96 * (it + j // RING + 1))
                    if begun(n - 1):
                        pe.wait_ge(max_done, n - 1)
                    nc.tensor.matmul(s1_ps[:, h % 2, :].rearrange("p (i s) -> p i s", i=I), ident_bf[:, :],
                                     mask[:, :].rearrange("p (o s) -> p o s", o=1).to_broadcast([P, I, P]),
                                     start=True, stop=False, skip_group_check=True)
                    for i in range(I):
                        mm = nc.tensor.matmul(s1_ps[:, h % 2, i * P:(i + 1) * P],
                                              q_st[0:MROW, s, h, i * P:(i + 1) * P],
                                              k_st[0:MROW, s, h, :], start=False, stop=(i == I - 1),
                                              skip_group_check=True)
                    mm.then_inc(s1_full, 1)

                def scores_t(it, j, pair):
                    s, u = j % RING, it * RING + j
                    if pair == 0:
                        pe.wait_ge(m_ld, 16 * MPARTS * (it * NBS + j // NG + 1))
                    if begun(u * 2 + pair - 1):
                        pe.wait_ge(exp_done, u * 2 + pair - 1)
                    for i in range(2):
                        h = pair * 2 + i
                        nc.tensor.matmul(st_ps[:, pair, i, :],
                                         k_st[0:MROW + MPARTS, s, h, :],
                                         q_st[0:MROW + MPARTS, s, h, :], start=True, stop=False)
                        mm = nc.tensor.matmul(st_ps[:, pair, i, :].rearrange("p (i t) -> p i t", i=I),
                                              ident_bf[:, :],
                                              mask_t[:, :].rearrange("p (o s) -> p o s", o=1).to_broadcast([P, I, P]),
                                              start=False, stop=True)
                    mm.then_inc(st_full, 1)

                def values(it, j):
                    u = it * RING + j
                    pe.wait_ge(v_placed, it * NBS + j // NG + 1)
                    if begun(u):
                        pe.wait_ge(o_copied, u)
                    pe.wait_ge(exp_done, 2 * (u + 1))
                    for h in range(G):
                        mm = nc.tensor.matmul(o_ps[32 * h:32 * h + 32, :],
                                              v_aug[:, (j // NG) % NBS, (j % NG) * G + h, :],
                                              probs[:, j % 2, h, :], start=True, stop=True,
                                              skip_group_check=True)
                    mm.then_inc(av_done, 1)

                def transpose_max(b, i):
                    pe.wait_ge(max_done, (b + 1) * NG * G)
                    if begun(b - 2):
                        pe.wait_ge(y_done, b - 2)
                    nc.tensor.transpose(misc_ps[0:H * I, 0:P], maxes[:, i % 2, :], ident[:, :]
                                        ).then_inc(mT_full, 1)

                def select(b, i, sel, done):
                    for g in range(NG):
                        mm = nc.tensor.matmul(misc_ps[g * G * C:(g + 1) * G * C, :], sel[:, :],
                                              o_raw[:, i % 2, g, :], start=True, stop=True,
                                              skip_group_check=True)
                    mm.then_inc(done, 1)

                def select_sums(b, i, more):
                    pe.wait_ge(o_copied, (b + 1) * NG)
                    if begun(more):
                        pe.wait_ge(m_step, more)
                    if begun(b):
                        pe.wait_ge(y_done, b)
                    select(b, i, sel_s, sums_full)

                def select_o(b, i):
                    pe.wait_ge(recip_done, b + 1)
                    select(b, i, sel_o, o_full)

                def project(b, parts):
                    if 0 in parts:
                        pe.wait_ge(o_normed, b + 1)
                    for i in parts:
                        mm = nc.tensor.matmul(misc_ps[:, :], o_norm[:, i * P:(i + 1) * P], wo[:, i, :],
                                              start=(i == 0), stop=(i == I - 1))
                    if I - 1 in parts:
                        mm.then_inc(proj_full, 1)

                for j in range(AHEAD):
                    for h in range(G):
                        scores(0, j, h)
                    if j == NG - 1:
                        transpose_max(0, 0)

                def body(it, first, last):
                    for j in range(RING):
                        b, jb, g = it * NBS + j // NG, j // NG, j % NG
                        finish = not (first and jb == 0)
                        more = unit_exists(j - g + NG, last)
                        ahead = unit_exists(j + AHEAD, last)
                        finish2 = g == 0 and not (first and jb < 2)
                        if ahead:
                            scores(it, j + AHEAD, 0)
                        scores_t(it, j, 0)
                        if finish and g == 1:
                            select_sums(b - 1, jb + 1, 5 * (b + 1) + 1 if more else 0)
                        if ahead:
                            scores(it, j + AHEAD, 1)
                        if finish2:
                            project(b - 2, [0])
                        scores_t(it, j, 1)
                        if finish2:
                            project(b - 2, [1])
                        if ahead:
                            scores(it, j + AHEAD, 2)
                        if finish2:
                            project(b - 2, [2])
                        if j > 0:
                            values(it, j - 1)
                        elif not first:
                            values(it - 1, RING - 1)
                        if ahead:
                            scores(it, j + AHEAD, 3)
                        if finish2:
                            project(b - 2, [3])
                        if more and g == 0:
                            transpose_max(b + 1, jb + 1)
                        if finish and g == 1:
                            select_o(b - 1, jb + 1)

                rounds(pe, body)
                values(UNITS // RING - 1, RING - 1)
                project(B - 2, range(I))
                select_sums(B - 1, B - 1, 0)
                select_o(B - 1, B - 1)
                project(B - 1, range(I))

            @block.scalar
            def _(act):
                def exps(it, j):
                    u = it * RING + j
                    for pair in range(2):
                        act.wait_ge(st_full, 2 * u + pair + 1)
                        if begun(u - 1):
                            act.wait_ge(av_done, u - 1)
                        nc.scalar.activation(probs[:, j % 2, 2 * pair:2 * pair + 2, :],
                                             st_ps[:, pair, :, :], ACT.Exp).then_inc(exp_done, 1)

                def copy_o(it, j):
                    u, b = it * RING + j, it * NBS + j // NG
                    act.wait_ge(av_done, u + 1)
                    if begun(b - 1):
                        act.wait_ge(o_full, b - 1)
                    nc.scalar.activation(o_raw[:, (j // NG) % 2, j % NG, :], o_ps[:, :], ACT.Copy
                                         ).then_inc(o_copied, 1)

                def body(it, first, last):
                    for j in range(RING):
                        exps(it, j)
                        if j > 0:
                            copy_o(it, j - 1)
                        elif not first:
                            copy_o(it - 1, RING - 1)

                rounds(act, body)
                copy_o(UNITS // RING - 1, RING - 1)

            @block.vector
            def _(dve):
                nc.vector.memset(k_st[MROW:MROW + MPARTS, :, :, :].rearrange("p u h t -> p (u h t)"), 1.0
                                 ).then_inc(memset_done, 1)
                dve.wait_ge(const_ld, 16 * NCONST)

                def row_max(it, j, h):
                    n = ((it + j // RING) * RING + j % RING) * G + h
                    jb, g = j // NG, j % NG
                    if h == 0 and g == 0:
                        if begun((it * NBS + jb) - 1):
                            dve.wait_ge(mT_full, (it * NBS + jb) - 1)
                    dve.wait_ge(s1_full, n + 1)
                    c = (g * G + h) * I
                    nc.vector.tensor_reduce(maxes[:, jb % 2, c:c + I],
                                            s1_ps[:, h % 2, :].rearrange("p (i s) -> p i s", i=I), AX.X, ALU.max
                                            ).then_inc(max_done, 1)

                def split_max(b, i, steps):
                    out = m_parts[:, i % 2, :, :]
                    if 0 in steps:
                        dve.wait_ge(mT_full, b + 1)
                        if begun(16 * MPARTS * (b - 1)):
                            dve.wait_ge(m_ld, 16 * MPARTS * (b - 1))
                        nc.vector.tensor_scalar(m_neg[:, :], misc_ps[0:H * I, 0:P], -1.0, None, ALU.mult
                                                ).then_inc(m_step, 1)
                    if 1 in steps:
                        dve.wait_ge(m_step, b * 5 + 1)
                        nc.vector.tensor_copy(out[:, 0, :], m_neg[:, :]).then_inc(m_step, 1)
                    if 2 in steps:
                        dve.wait_ge(m_step, b * 5 + 2)
                        nc.vector.tensor_tensor(m_rest[:, :], m_neg[:, :], out[:, 0, :], ALU.subtract
                                                ).then_inc(m_step, 1)
                    if 3 in steps:
                        dve.wait_ge(m_step, b * 5 + 3)
                        nc.vector.tensor_copy(out[:, 1, :], m_rest[:, :]).then_inc(m_step, 1)
                    if 4 in steps:
                        dve.wait_ge(m_step, b * 5 + 4)
                        nc.vector.tensor_tensor(out[:, 2, :], m_rest[:, :], out[:, 1, :], ALU.subtract
                                                ).then_inc(m_step, 1)

                def recip_chunk(b, c):
                    if c == 0:
                        dve.wait_ge(sums_full, b + 1)
                        if begun(b):
                            dve.wait_ge(o_normed, b)
                    r = nc.vector.reciprocal(recip[:, c * P:(c + 1) * P], misc_ps[:, c * P:(c + 1) * P])
                    if c == I - 1:
                        r.then_inc(recip_done, 1)

                def norm_o(b):
                    dve.wait_ge(o_full, b + 1)
                    dve.wait_ge(recip_done, b + 1)
                    if begun(b):
                        dve.wait_ge(proj_full, b)
                    nc.vector.tensor_tensor(o_norm[:, :], misc_ps[:, :], recip[:, :], ALU.mult
                                            ).then_inc(o_normed, 1)

                def layer_norm(b, steps):
                    if 0 in steps:
                        dve.wait_ge(proj_full, b + 1)
                        dve.wait_ge(x_biased, b + 1)
                        if begun(b):
                            dve.wait_ge(x_done, b)
                        nc.vector.tensor_tensor(y[:, :], misc_ps[:, :], x_bias[:, :], ALU.add).then_inc(y_done, 1)
                    if 1 in steps:
                        dve.wait_ge(y_done, b + 1)
                        nc.vector.bn_stats(stats[:, :], y[:, :]).then_inc(ln_step, 1)
                    if 2 in steps:
                        dve.wait_ge(ln_step, b * 3 + 1)
                        dve.sem_inc(passed_dve, 1)
                        nc.vector.bn_aggr(mv[:, :], stats[:, :]).then_inc(ln_step, 1)
                    if 3 in steps:
                        dve.wait_ge(ln_step, b * 3 + 2)
                        nc.vector.tensor_scalar(var_eps[:, :], mv[:, 1:2], LN_EPS, None, ALU.add).then_inc(ln_step, 1)

                def finish_norm(b, i, rnd):
                    dve.wait_ge(rstd_done, b + 1)
                    if begun(16 * rnd):
                        dve.wait_ge(x_stored[i % 2], 16 * rnd)
                    nc.vector.tensor_scalar(x_new[:, i % 2, :], y[:, :], mv[:, 0:1], rstd[:, 0:1],
                                            ALU.subtract, ALU.mult).then_inc(x_done, 1)

                for j in range(AHEAD):
                    for h in range(G):
                        row_max(0, j, h)
                    if j == NG:
                        split_max(0, 0, range(5))

                def rnd_of(it, jb):
                    return it * (NBS // 2) + jb // 2

                def body(it, first, last):
                    for j in range(RING):
                        b, jb, g = it * NBS + j // NG, j // NG, j % NG
                        finish = not (first and jb == 0)
                        more = unit_exists(j - g + NG, last)
                        finish2 = not (first and jb < 2)
                        back = (it, jb - 2) if jb > 1 else (it - 1, NBS - 2 + jb)
                        for h in range(G):
                            if unit_exists(j + AHEAD, last):
                                row_max(it, j + AHEAD, h)
                            if finish2 and g == 0 and h == 0:
                                norm_o(b - 2)
                            if finish2 and g == 0 and h == G - 1:
                                layer_norm(b - 2, [0])
                            if g == 1:
                                if more and h < 3:
                                    split_max(b + 1, jb + 1, [2 * h])
                                if finish2 and h < 3:
                                    layer_norm(b - 2, [h + 1])
                                if more and h < 2:
                                    split_max(b + 1, jb + 1, [2 * h + 1])
                                if finish and h > 0:
                                    recip_chunk(b - 1, h - 1)
                                if finish2 and h == 3:
                                    finish_norm(b - 2, jb, rnd_of(*back))
                                if finish and h == 3:
                                    recip_chunk(b - 1, 3)

                rounds(dve, body)
                norm_o(B - 2)
                layer_norm(B - 2, range(4))
                finish_norm(B - 2, 0, B // 2 - 1)
                for c in range(I):
                    recip_chunk(B - 1, c)
                norm_o(B - 1)
                layer_norm(B - 1, range(4))
                finish_norm(B - 1, 1, B // 2 - 1)

            @block.gpsimd
            def _(pool):
                nc.gpsimd.memset(v_aug[:, :, :, :], 1.0).then_inc(ones_done, 1)
                pool.wait_ge(ones_done, 1)
                pool.wait_ge(const_ld, 16 * NCONST)

                def place_v(it, jb):
                    b = it * NBS + jb
                    pool.wait_ge(v_ld[jb % 2], 16 * (it * (NBS // 2) + jb // 2 + 1))
                    if begun((b - NBS + 1) * NG):
                        pool.wait_ge(av_done, (b - NBS + 1) * NG)
                    pool.sem_inc(passed_pool, 1)
                    nc.gpsimd.tensor_copy(v_aug[:, jb % NBS, :, 0:C],
                                          v_raw[:, jb % 2, :].rearrange("p (h c) -> p h c", c=C)
                                          ).then_inc(v_placed, 1)

                def add_bias(b, i, rnd):
                    pool.wait_ge(x_ld[i % 2], 16 * (rnd + 1))
                    if begun(b):
                        pool.wait_ge(y_done, b)
                    nc.gpsimd.tensor_tensor(x_bias[:, :], x_res[:, i % 2, :], bo[:, :], ALU.add
                                            ).then_inc(x_biased, 1)

                def power(b, i):
                    pool.wait_ge(ln_step, (b + 1) * 3)
                    nc.gpsimd.tensor_tensor(rstd[:, :], var_eps[:, :], minus_half[:, :], ALU.pow
                                            ).then_inc(rstd_done, 1)
                    pool.wait_ge(x_done, b + 1)
                    pool.dma_start(x_out[bass.ds(b, 1), :, :].rearrange("o p t -> p (o t)"),
                                   x_new[:, i % 2, :]).then_inc(x_stored[i % 2], 16)

                place_v(0, 0)

                def rnd_of(it, jb):
                    return it * (NBS // 2) + jb // 2

                def body(it, first, last):
                    for jb in range(NBS):
                        if not (last and jb == NBS - 1):
                            if jb == NBS - 1:
                                place_v(it + 1, 0)
                            else:
                                place_v(it, jb + 1)
                        if not (first and jb == 0):
                            pit, pj = (it, jb - 1) if jb else (it - 1, NBS - 1)
                            add_bias(it * NBS + jb - 1, jb + 1, rnd_of(pit, pj))
                        if not (first and jb < 2):
                            power(it * NBS + jb - 2, jb)

                rounds(pool, body)
                power(B - 2, 0)
                add_bias(B - 1, B - 1, B // 2 - 1)
                power(B - 1, B - 1)
                pool.wait_ge(x_stored[0], 16 * (B // 2))
                pool.wait_ge(x_stored[1], 16 * (B // 2))


RMS_EPS = 1e-6
HEADS, HD = 16, 32
DK = D // P
NJ = P // HD


def batches(eng, body):
    body(0, 0)
    body(1, 1)
    with eng.Fori(1, B // 2 - 1) as it:
        body(it * 2, 0)
        body(it * 2 + 1, 1)
    body(B - 2, 0)
    body(B - 1, 1)


def before(b, n):
    return not isinstance(b, int) or b + n < B


def gate_attention(nc, tag, x_in, h_t_out, mod_out, wq_d, wk_d, wv_d, wo_d, a_d, ln_d, ident_d, half_d,
                   ident_bf_d, mask_d, mask_t_d):
    R = 16
    SCALE = HD ** -0.5
    with Phase(nc) as ph:
        sem, sb = ph.sem, ph.sb
        wq = sb(f"{tag}_wq", [P, DK, D])
        wk = sb(f"{tag}_wk", [P, DK, D])
        wv = sb(f"{tag}_wv", [P, DK, D])
        wo = sb(f"{tag}_wo", [P, DK, D])
        a_w = sb(f"{tag}_a", [P, DK, R])
        ln_w = sb(f"{tag}_ln_w", [P, 2, DK])
        ident = sb(f"{tag}_ident", [P, P])
        minus_half = sb(f"{tag}_minus_half", [P, 1])
        ident_bf = sb(f"{tag}_ident_bf", [P, P], BF16)
        mask = sb(f"{tag}_mask", [P, P], BF16)
        mask_t = sb(f"{tag}_mask_t", [P, P], BF16)
        wo_a = sb(f"{tag}_wo_a", [P, DK, R])
        ones = sb(f"{tag}_ones", [P, HD])
        ones_bf = sb(f"{tag}_ones_bf", [3, P], BF16)
        x = sb(f"{tag}_x", [P, 2, D])
        squares = sb(f"{tag}_squares", [P, D])
        sumsq = sb(f"{tag}_sumsq", [P, 1])
        mean_eps = sb(f"{tag}_mean_eps", [P, 1])
        rstd = sb(f"{tag}_rstd", [P, 1])
        x_rms = sb(f"{tag}_x_rms", [P, 2, D])
        x1_t = sb(f"{tag}_x1_t", [P, 2, DK, P])
        h_t = sb(f"{tag}_h_t", [P, 2, DK, P])
        q_own = sb(f"{tag}_q_own", [P, 2, DK, NJ, P])
        k_t = sb(f"{tag}_k_t", [P, 2, DK, P])
        v = sb(f"{tag}_v", [P, 2, D])
        maxes = sb(f"{tag}_maxes", [P, 2, HEADS])
        m_neg = sb(f"{tag}_m_neg", [HEADS, P])
        m_rest = sb(f"{tag}_m_rest", [HEADS, P])
        m_parts = sb(f"{tag}_m_parts", [HEADS, 3, P], BF16)
        m_row = sb(f"{tag}_m_row", [3, 2, HEADS * P], BF16)
        probs = sb(f"{tag}_probs", [P, 2, DK, NJ, P])
        recip = sb(f"{tag}_recip", [P, D])
        o_norm = sb(f"{tag}_o_norm", [P, D])
        mod = sb(f"{tag}_mod", [R, 2, P])

        proj_ps = ph.ps(f"{tag}_proj", [P, 2, D])
        s1_ps = ph.ps(f"{tag}_s1", [P, 2, D])
        st_ps = ph.ps(f"{tag}_st", [P, 2, D])
        o_ps = ph.ps(f"{tag}_o", [P, D])
        misc_ps = ph.ps(f"{tag}_misc", [P, D])

        const_ld = sem(f"{tag}_const_ld")
        w_ld = [sem(f"{tag}_w_ld{i}") for i in range(4)]
        x_ld = [sem(f"{tag}_x_ld{i}") for i in range(2)]
        h_stored = [sem(f"{tag}_h_stored{i}") for i in range(2)]
        mod_stored = [sem(f"{tag}_mod_stored{i}") for i in range(2)]
        names = ("zeros wo_a_full wo_a_done sumsq_done mean_done rstd_done rms_done tr_full x1_done h_done q_full "
                 "q_done_act q_done_dve k_full k_done v_full v_done s1_full max_done mT_full m_step m_ld st_full "
                 "exp_done o_full sums_full recip_done o_normed mod_full mod_done").split()
        (zeros, wo_a_full, wo_a_done, sumsq_done, mean_done, rstd_done, rms_done, tr_full, x1_done, h_done, q_full,
         q_done_act, q_done_dve, k_full, k_done, v_full, v_done, s1_full, max_done, mT_full, m_step, m_ld, st_full,
         exp_done, o_full, sums_full, recip_done, o_normed, mod_full, mod_done) = [sem(f"{tag}_{n}") for n in names]
        NCONST = 6

        def bcast(m):
            return m[:, :].rearrange("p (o s) -> p o s", o=1).to_broadcast([P, NJ, P])

        with nc.Block() as block:
            @block.sync
            def _(sp):
                def load(b, i):
                    if begun(b - 1):
                        sp.wait_ge(rms_done, b - 1)
                    sp.dma_start(x[:, i, :], x_in[bass.ds(b, 1), :, :].rearrange("o p t -> p (o t)")
                                 ).then_inc(x_ld[i], 16)

                def store_h(b, i):
                    sp.wait_ge(h_done, b + 1)
                    sp.dma_start(h_t_out[bass.ds(b, 1), :, :, :].rearrange("o p k t -> p (o k) t"),
                                 h_t[:, i, :, :]).then_inc(h_stored[i], 16)

                def send_max(b, i):
                    sp.wait_ge(m_step, 5 * (b + 1))
                    for p in range(3):
                        sp.dma_start(m_row[p:p + 1, i, :], m_parts[:, p, :]).then_inc(m_ld, 16)

                def store_mod(b, i):
                    sp.wait_ge(mod_done, b + 1)
                    sp.dma_start(mod_out[bass.ds(b, 1), :, :].rearrange("o r t -> r (o t)"), mod[:, i, :]
                                 ).then_inc(mod_stored[i], 16)

                load(0, 0)
                load(1, 1)
                for dst, src in ((minus_half, half_d), (ident, ident_d), (ident_bf, ident_bf_d), (mask, mask_d),
                                 (mask_t, mask_t_d)):
                    sp.dma_start(dst[:, :], src).then_inc(const_ld, 16)
                sp.dma_start(ln_w[:, :, :], ln_d).then_inc(const_ld, 16)
                for n, dst, src in ((0, wq, wq_d), (1, wk, wk_d), (2, wv, wv_d), (3, a_w, a_d), (3, wo, wo_d)):
                    sp.dma_start(dst[:, :, :], src).then_inc(w_ld[n], 16)
                load(2, 0)
                store_h(0, 0)
                send_max(0, 0)
                store_h(1, 1)

                def body(b, i):
                    if before(b, 3):
                        load(b + 3, 1 - i)
                    if not (isinstance(b, int) and b == 0):
                        store_mod(b - 1, 1 - i)
                    if before(b, 1):
                        send_max(b + 1, 1 - i)
                    if before(b, 2):
                        store_h(b + 2, i)

                body(0, 0)
                body(1, 1)
                with sp.Fori(1, B // 2 - 2) as it:
                    body(it * 2, 0)
                    body(it * 2 + 1, 1)
                for b in range(B - 4, B):
                    body(b, b % 2)
                store_mod(B - 1, 1)
                for i in range(2):
                    sp.wait_ge(h_stored[i], 16 * (B // 2))
                    sp.wait_ge(mod_stored[i], 16 * (B // 2) + 1)

            @block.tensor
            def _(pe):
                pe.wait_ge(const_ld, 16 * NCONST)
                pe.wait_ge(zeros, 2)

                def transposes(b, i):
                    pe.wait_ge(rms_done, b + 1)
                    if begun(b):
                        pe.wait_ge(k_done, b)
                    for dk in range(DK):
                        mm = nc.tensor.transpose(proj_ps[:, 0, dk * P:(dk + 1) * P], x_rms[:, i, dk * P:(dk + 1) * P],
                                                 ident[:, :])
                    mm.then_inc(tr_full, 1)

                def project_t(b, i, w, bank, done):
                    for f in range(DK):
                        for dk in range(DK):
                            mm = nc.tensor.matmul(proj_ps[:, bank, f * P:(f + 1) * P], w[:, dk, f * P:(f + 1) * P],
                                                  x1_t[:, i, dk, :], start=(dk == 0), stop=(dk == DK - 1),
                                                  skip_group_check=True)
                    mm.then_inc(done, 1)

                def project_q(b, i):
                    pe.wait_ge(x1_done, b + 1)
                    if begun(b):
                        pe.wait_ge(v_done, b)
                    project_t(b, i, wq, 1, q_full)

                def project_k(b, i):
                    pe.wait_ge(h_done, b + 1)
                    project_t(b, i, wk, 0, k_full)

                def project_v(b, i):
                    pe.wait_ge(q_done_act, b + 1)
                    pe.wait_ge(q_done_dve, b + 1)
                    for dk in range(DK):
                        mm = nc.tensor.matmul(proj_ps[:, 1, :], x1_t[:, i, dk, :], wv[:, dk, :], start=(dk == 0),
                                              stop=(dk == DK - 1))
                    mm.then_inc(v_full, 1)

                def scores(b, i):
                    pe.wait_ge(k_done, b + 1)
                    if begun(5 * b):
                        pe.wait_ge(m_step, 5 * b)
                    for f in range(DK):
                        if begun(b * DK + f - 1):
                            pe.wait_ge(max_done, b * DK + f - 1)
                        nc.tensor.matmul(s1_ps[:, f % 2, :].rearrange("p (i s) -> p i s", i=NJ), ident_bf[:, :],
                                         bcast(mask), start=True, stop=False, skip_group_check=True)
                        for j in range(NJ):
                            mm = nc.tensor.matmul(s1_ps[:, f % 2, j * P:(j + 1) * P], q_own[:, i, f, j, :],
                                                  k_t[:, i, f, :], start=False, stop=(j == NJ - 1),
                                                  skip_group_check=True)
                        mm.then_inc(s1_full, 1)

                def transpose_max(b, i):
                    pe.wait_ge(max_done, (b + 1) * DK)
                    nc.tensor.transpose(s1_ps[0:HEADS, 0, 0:P], maxes[:, i, :], ident[:, :]).then_inc(mT_full, 1)

                def scores_t(b, i, f):
                    if f == 0:
                        pe.wait_ge(m_ld, 48 * (b + 1))
                    if begun(b * DK + f - 1):
                        pe.wait_ge(exp_done, b * DK + f - 1)
                    nc.tensor.matmul(st_ps[:, f % 2, :], k_t[:, i, f, :],
                                     q_own[:, i, f, :, :].rearrange("p j t -> p (j t)"), start=True, stop=False)
                    nc.tensor.matmul(st_ps[:, f % 2, :].rearrange("p (i s) -> p i s", i=NJ), ident_bf[:, :],
                                     bcast(mask_t), start=False, stop=False)
                    nc.tensor.matmul(st_ps[:, f % 2, :], ones_bf[:, :], m_row[:, i, f * D:(f + 1) * D],
                                     start=False, stop=True).then_inc(st_full, 1)

                def values(b, i):
                    pe.wait_ge(v_done, b + 1)
                    pe.wait_ge(exp_done, (b + 1) * DK)
                    if begun(b):
                        pe.wait_ge(o_normed, b)
                    for f in range(DK):
                        for j in range(NJ):
                            mm = nc.tensor.matmul(o_ps[HD * j:HD * j + HD, f * P:(f + 1) * P],
                                                  v[:, i, (f * NJ + j) * HD:(f * NJ + j + 1) * HD],
                                                  probs[:, i, f, j, :], start=True, stop=True, skip_group_check=True)
                    mm.then_inc(o_full, 1)
                    if begun(b):
                        pe.wait_ge(mod_done, b)
                    for j in range(NJ):
                        mm = nc.tensor.matmul(misc_ps[HD * j:HD * j + HD, :].rearrange("p (f t) -> p f t", f=DK),
                                              ones[:, :], probs[:, i, :, j, :], start=True, stop=True,
                                              skip_group_check=True)
                    mm.then_inc(sums_full, 1)

                def modulate(b, i):
                    pe.wait_ge(o_normed, b + 1)
                    for f in range(DK):
                        mm = nc.tensor.matmul(misc_ps[0:R, 0:P], wo_a[:, f, :], o_norm[:, f * P:(f + 1) * P],
                                              start=(f == 0), stop=(f == DK - 1))
                    mm.then_inc(mod_full, 1)

                transposes(0, 0)
                pe.wait_ge(w_ld[0], 16)
                project_q(0, 0)
                pe.wait_ge(w_ld[1], 16)
                project_k(0, 0)
                pe.wait_ge(w_ld[2], 16)
                project_v(0, 0)
                scores(0, 0)
                transpose_max(0, 0)
                transposes(1, 1)
                pe.wait_ge(w_ld[3], 32)
                for f in range(DK):
                    for dk in range(DK):
                        mm = nc.tensor.matmul(misc_ps[:, f * R:(f + 1) * R], wo[:, dk, f * P:(f + 1) * P],
                                              a_w[:, dk, :], start=(dk == 0), stop=(dk == DK - 1),
                                              skip_group_check=True)
                mm.then_inc(wo_a_full, 1)
                pe.wait_ge(wo_a_done, 1)

                def body(b, i):
                    more = before(b, 1)
                    if more:
                        project_q(b + 1, 1 - i)
                    scores_t(b, i, 0)
                    scores_t(b, i, 1)
                    if more:
                        project_k(b + 1, 1 - i)
                    scores_t(b, i, 2)
                    scores_t(b, i, 3)
                    if not (isinstance(b, int) and b == 0):
                        modulate(b - 1, 1 - i)
                    if more:
                        project_v(b + 1, 1 - i)
                    values(b, i)
                    if more:
                        scores(b + 1, 1 - i)
                        transpose_max(b + 1, 1 - i)
                    if before(b, 2):
                        transposes(b + 2, i)

                batches(pe, body)
                modulate(B - 1, 1)

            @block.scalar
            def _(act):
                def norm(b, i):
                    act.wait_ge(x_ld[i], (b - i) * 8 + 16)
                    if begun(b):
                        act.wait_ge(mean_done, b)
                    nc.scalar.activation(squares[:, :], x[:, i, :], ACT.Square, accum_out=sumsq[:, :]
                                         ).then_inc(sumsq_done, 1)
                    act.wait_ge(rstd_done, b + 1)
                    if begun(b - 1):
                        act.wait_ge(tr_full, b - 1)
                    nc.scalar.activation(x_rms[:, i, :], x[:, i, :], ACT.Copy, scale=rstd[:, 0:1]
                                         ).then_inc(rms_done, 1)

                def take_q(b, i):
                    act.wait_ge(q_full, b + 1)
                    if begun((b - 1) * DK):
                        act.wait_ge(st_full, (b - 1) * DK)
                    for j in range(2):
                        op = nc.scalar.activation(q_own[HD * j:HD * j + HD, i, :, j, :],
                                                  proj_ps[HD * j:HD * j + HD, 1, :].rearrange("p (f t) -> p f t", f=DK),
                                                  ACT.Copy, scale=SCALE)
                    op.then_inc(q_done_act, 1)

                def take_k(b, i):
                    act.wait_ge(k_full, b + 1)
                    if begun((b - 1) * DK):
                        act.wait_ge(st_full, (b - 1) * DK)
                    nc.scalar.activation(k_t[:, i, :, :].rearrange("p f t -> p (f t)"), proj_ps[:, 0, :], ACT.Copy
                                         ).then_inc(k_done, 1)

                def take_v(b, i):
                    act.wait_ge(v_full, b + 1)
                    if begun(b - 1):
                        act.wait_ge(o_full, b - 1)
                    nc.scalar.activation(v[:, i, :], proj_ps[:, 1, :], ACT.Copy).then_inc(v_done, 1)

                def exps(b, i, f):
                    act.wait_ge(st_full, b * DK + f + 1)
                    if begun(b - 1):
                        act.wait_ge(sums_full, b - 1)
                    nc.scalar.activation(probs[:, i, f, :, :].rearrange("p j t -> p (j t)"), st_ps[:, f % 2, :],
                                         ACT.Exp).then_inc(exp_done, 1)

                def tanh(b, i):
                    act.wait_ge(mod_full, b + 1)
                    act.wait_ge(mod_stored[i], (b - i) * 8 + 1)
                    nc.scalar.activation(mod[:, i, :], misc_ps[0:R, 0:P], ACT.Tanh).then_inc(mod_done, 1)

                for i in range(2):
                    act.sem_inc(mod_stored[i], 1)
                act.wait_ge(zeros, 2)
                norm(0, 0)
                norm(1, 1)
                take_q(0, 0)
                take_k(0, 0)
                take_v(0, 0)
                act.wait_ge(wo_a_full, 1)
                nc.scalar.activation(wo_a[:, :, :].rearrange("p f r -> p (f r)"), misc_ps[:, 0:DK * R], ACT.Copy
                                     ).then_inc(wo_a_done, 1)

                def body(b, i):
                    more = before(b, 1)
                    if more:
                        take_q(b + 1, 1 - i)
                    exps(b, i, 0)
                    exps(b, i, 1)
                    if more:
                        take_k(b + 1, 1 - i)
                    exps(b, i, 2)
                    exps(b, i, 3)
                    if not (isinstance(b, int) and b == 0):
                        tanh(b - 1, 1 - i)
                    if more:
                        take_v(b + 1, 1 - i)
                    if before(b, 2):
                        norm(b + 2, i)

                batches(act, body)
                tanh(B - 1, 1)

            @block.vector
            def _(dve):
                nc.vector.memset(ones[:, :], 1.0)
                nc.vector.memset(ones_bf[:, :], 1.0)
                nc.vector.memset(q_own[:, 0, :, :, :], 0.0).then_inc(zeros, 1)
                dve.wait_ge(const_ld, 16 * NCONST)

                def mean(b):
                    dve.wait_ge(sumsq_done, b + 1)
                    if begun(b):
                        dve.wait_ge(rstd_done, b)
                    nc.vector.tensor_scalar(mean_eps[:, :], sumsq[:, :], 1.0 / D, RMS_EPS, ALU.mult, ALU.add
                                            ).then_inc(mean_done, 1)

                def take_x(b, i):
                    dve.wait_ge(tr_full, b + 1)
                    src = proj_ps[:, 0, :].rearrange("p (f t) -> p f t", f=DK)
                    if begun(b - 1):
                        dve.wait_ge(v_full, b - 1)
                    nc.vector.tensor_tensor(x1_t[:, i, :, :], src,
                                            ln_w[:, 0, :].rearrange("p (f o) -> p f o", o=1).to_broadcast([P, DK, P]),
                                            ALU.mult).then_inc(x1_done, 1)
                    if begun((b - i) * 8):
                        dve.wait_ge(h_stored[i], (b - i) * 8)
                    nc.vector.tensor_tensor(h_t[:, i, :, :], src,
                                            ln_w[:, 1, :].rearrange("p (f o) -> p f o", o=1).to_broadcast([P, DK, P]),
                                            ALU.mult).then_inc(h_done, 1)

                def take_q(b, i):
                    dve.wait_ge(q_full, b + 1)
                    if begun((b - 1) * DK):
                        dve.wait_ge(st_full, (b - 1) * DK)
                    for j in range(2, NJ):
                        op = nc.vector.tensor_scalar(q_own[HD * j:HD * j + HD, i, :, j, :],
                                                     proj_ps[HD * j:HD * j + HD, 1, :].rearrange("p (f t) -> p f t", f=DK),
                                                     SCALE, None, ALU.mult)
                    op.then_inc(q_done_dve, 1)

                def row_max(b, i):
                    if begun(b - 1):
                        dve.wait_ge(mT_full, b - 1)
                    for f in range(DK):
                        dve.wait_ge(s1_full, b * DK + f + 1)
                        nc.vector.tensor_reduce(maxes[:, i, f * NJ:(f + 1) * NJ],
                                                s1_ps[:, f % 2, :].rearrange("p (i s) -> p i s", i=NJ), AX.X, ALU.max
                                                ).then_inc(max_done, 1)

                def split_max(b):
                    dve.wait_ge(mT_full, b + 1)
                    if begun(48 * b):
                        dve.wait_ge(m_ld, 48 * b)
                    nc.vector.tensor_scalar(m_neg[:, :], s1_ps[0:HEADS, 0, 0:P], -1.0, None, ALU.mult).then_inc(m_step, 1)
                    dve.wait_ge(m_step, b * 5 + 1)
                    nc.vector.tensor_copy(m_parts[:, 0, :], m_neg[:, :]).then_inc(m_step, 1)
                    dve.wait_ge(m_step, b * 5 + 2)
                    nc.vector.tensor_tensor(m_rest[:, :], m_neg[:, :], m_parts[:, 0, :], ALU.subtract).then_inc(m_step, 1)
                    dve.wait_ge(m_step, b * 5 + 3)
                    nc.vector.tensor_copy(m_parts[:, 1, :], m_rest[:, :]).then_inc(m_step, 1)
                    dve.wait_ge(m_step, b * 5 + 4)
                    nc.vector.tensor_tensor(m_parts[:, 2, :], m_rest[:, :], m_parts[:, 1, :], ALU.subtract
                                            ).then_inc(m_step, 1)

                def normalize(b):
                    dve.wait_ge(sums_full, b + 1)
                    if begun(b):
                        dve.wait_ge(o_normed, b)
                    nc.vector.reciprocal(recip[:, :], misc_ps[:, :]).then_inc(recip_done, 1)
                    dve.wait_ge(recip_done, b + 1)
                    if begun(b):
                        dve.wait_ge(mod_full, b)
                    nc.vector.tensor_tensor(o_norm[:, :], o_ps[:, :], recip[:, :], ALU.mult).then_inc(o_normed, 1)

                mean(0)
                mean(1)
                take_x(0, 0)
                take_q(0, 0)
                row_max(0, 0)
                split_max(0)
                take_x(1, 1)

                def body(b, i):
                    more = before(b, 1)
                    if not (isinstance(b, int) and b == 0):
                        normalize(b - 1)
                    if more:
                        take_q(b + 1, 1 - i)
                    if before(b, 2):
                        mean(b + 2)
                    if more:
                        row_max(b + 1, 1 - i)
                        split_max(b + 1)
                    if before(b, 2):
                        take_x(b + 2, i)

                batches(dve, body)
                normalize(B - 1)

            @block.gpsimd
            def _(pool):
                nc.gpsimd.memset(q_own[:, 1, :, :, :], 0.0).then_inc(zeros, 1)
                pool.wait_ge(const_ld, 16 * NCONST)

                def body(b, i):
                    pool.wait_ge(mean_done, b + 1)
                    if begun(b):
                        pool.wait_ge(rms_done, b)
                    nc.gpsimd.tensor_tensor(rstd[:, :], mean_eps[:, :], minus_half[:, :], ALU.pow
                                            ).then_inc(rstd_done, 1)

                batches(pool, body)


def squared_attention(nc, tag, x_in, x_out, wq_d, wk_d, wv_d, wo_d, gamma_d, beta_d, ident_d, keep_t_d,
                      q_parts, q_scale, q_heads):
    NG = 2 * HEADS
    W = 2 * D
    SCALE = HD ** -0.5
    with Phase(nc) as ph:
        sem, sb = ph.sem, ph.sb
        wq = sb(f"{tag}_wq", [P, DK, D])
        wk = sb(f"{tag}_wk", [P, DK, D])
        wv = sb(f"{tag}_wv", [P, DK, D])
        wo = sb(f"{tag}_wo", [P, DK, D])
        gamma = sb(f"{tag}_gamma", [P, HD])
        beta = sb(f"{tag}_beta", [P, HD])
        ident = sb(f"{tag}_ident", [P, P])
        keep_t = sb(f"{tag}_keep_t", [P, P])
        ones = sb(f"{tag}_ones", [P, HD])
        x = sb(f"{tag}_x", [P, 2, D])
        x_res = sb(f"{tag}_x_res", [P, 2, D])
        x_t = sb(f"{tag}_x_t", [P, DK, P])
        scaled = sb(f"{tag}_scaled", [P, W])
        shifted = sb(f"{tag}_shifted", [P, W])
        group_sum = sb(f"{tag}_group_sum", [P, NG])
        group_mean = sb(f"{tag}_group_mean", [P, NG])
        centred = sb(f"{tag}_centred", [P, W])
        squares = sb(f"{tag}_squares", [P, W])
        group_sq = sb(f"{tag}_group_sq", [P, NG])
        group_var = sb(f"{tag}_group_var", [P, NG])
        group_std = sb(f"{tag}_group_std", [P, NG])
        group_rstd = sb(f"{tag}_group_rstd", [P, NG])
        qk = sb(f"{tag}_qk", [P, W])
        q_own = sb(f"{tag}_q_own", [P, 2, DK, NJ, P])
        k_t = sb(f"{tag}_k_t", [P, 2, DK, P])
        v = sb(f"{tag}_v", [P, 2, D])
        weights = sb(f"{tag}_weights", [P, DK, NJ, P])
        kept = sb(f"{tag}_kept", [P, 2, DK, NJ, P])
        z_eps = sb(f"{tag}_z_eps", [P, D])
        recip = sb(f"{tag}_recip", [P, D])
        o_norm = sb(f"{tag}_o_norm", [P, D])
        y = sb(f"{tag}_y", [P, D])
        stats = sb(f"{tag}_stats", [P, 6])
        mv = sb(f"{tag}_mv", [P, 2])
        var_eps = sb(f"{tag}_var_eps", [P, 1])
        group_step = sb(f"{tag}_group_step", [P, 3, NG])
        row_step = sb(f"{tag}_row_step", [P, 3, 1])
        std = sb(f"{tag}_std", [P, 1])
        rstd = sb(f"{tag}_rstd", [P, 1])
        x_new = sb(f"{tag}_x_new", [P, 2, D])

        x_scaled = sb(f"{tag}_x_scaled", [P, D])
        rest = sb(f"{tag}_rest", [P, D])
        parts = sb(f"{tag}_parts", [P, 2, 3, D], BF16)

        tr_ps = ph.ps(f"{tag}_tr", [P, D])
        qk_ps = ph.ps(f"{tag}_qk_ps", [P, 2, D])
        v_ps = ph.ps(f"{tag}_v_ps", [P, D])
        st_ps = ph.ps(f"{tag}_st", [P, 2, D])
        o_ps = ph.ps(f"{tag}_o", [P, D])
        misc_ps = ph.ps(f"{tag}_misc", [P, D])

        const_ld = sem(f"{tag}_const_ld")
        w_ld = [sem(f"{tag}_w_ld{i}") for i in range(4)]
        passed_pool = sem(f"{tag}_passed_pool")
        passed_dve = sem(f"{tag}_passed_dve")
        x_ld = [sem(f"{tag}_x_ld{i}") for i in range(2)]
        res_ld = [sem(f"{tag}_res_ld{i}") for i in range(2)]
        parts_stored = [sem(f"{tag}_parts_stored{i}") for i in range(2)]
        split_step = sem(f"{tag}_split_step")
        CREDIT = 10
        x_stored = [sem(f"{tag}_x_stored{i}") for i in range(2)]
        names = ("zeros x_tr_full x_t_done qk_full v_full v_done scaled_done shifted_done stat_step sq_done grstd_done "
                 "qk_done q_tr_full q_done_act q_done_dve k_tr_full k_done st_full square_done kept_done o_full "
                 "sums_full z_done recip_done o_normed proj_full y_done ln_step rstd_done x_done group_std_done std_done root_step row_root_step").split()
        (zeros, x_tr_full, x_t_done, qk_full, v_full, v_done, scaled_done, shifted_done, stat_step, sq_done, grstd_done,
         qk_done, q_tr_full, q_done_act, q_done_dve, k_tr_full, k_done, st_full, square_done, kept_done, o_full,
         sums_full, z_done, recip_done, o_normed, proj_full, y_done, ln_step, rstd_done, x_done,
         group_std_done, std_done, root_step, row_root_step
         ) = [sem(f"{tag}_{n}") for n in names]
        NCONST = 4

        def groups(ap):
            return ap.rearrange("p (g c) -> p g c", c=HD)

        def by_channel(ap):
            return ap.rearrange("p (o c) -> p o c", o=1).to_broadcast([P, NG, HD])

        def by_group(ap):
            return ap.rearrange("p (g o) -> p g o", o=1).to_broadcast([P, NG, HD])

        with nc.Block() as block:
            @block.sync
            def _(sp):
                def load(b, i, dst, done):
                    sp.dma_start(dst[:, i, :], x_in[bass.ds(b, 1), :, :].rearrange("o p t -> p (o t)")
                                 ).then_inc(done[i], 16)

                def store(b, i):
                    sp.wait_ge(x_done, b + 1)
                    sp.dma_start(x_out[bass.ds(b, 1), :, :].rearrange("o p t -> p (o t)"), x_new[:, i, :]
                                 ).then_inc(x_stored[i], 16)

                load(0, 0, x, x_ld)
                for dst, src in ((ident, ident_d), (gamma, gamma_d), (beta, beta_d), (keep_t, keep_t_d)):
                    sp.dma_start(dst[:, :], src).then_inc(const_ld, 16)
                for n, dst, src in ((0, wq, wq_d), (1, wk, wk_d), (2, wv, wv_d)):
                    sp.dma_start(dst[:, :, :], src).then_inc(w_ld[n], 16)
                load(1, 1, x, x_ld)
                sp.dma_start(wo[:, :, :], wo_d).then_inc(w_ld[3], 16)

                def store_parts(b, i):
                    sp.wait_ge(split_step, CREDIT + 5 * (b + 1))
                    for p in range(3):
                        c = P // q_heads
                        dst = q_parts[bass.ds(b, 1), p * c:(p + 1) * c, :].rearrange("o c (h t) -> (o h) c t", t=D)
                        sp.dma_start(dst, parts[:, i, p, :]).then_inc(parts_stored[i], 16)

                for i in range(2):
                    sp.wait_ge(x_tr_full, i + 1)
                    load(i + 2, i, x, x_ld)

                def body(b, i):
                    if begun(b - 1):
                        sp.wait_ge(y_done, b - 1)
                    load(b, i, x_res, res_ld)
                    if not (isinstance(b, int) and b == 0):
                        store(b - 1, 1 - i)
                    if before(b, 4):
                        sp.wait_ge(x_tr_full, b + 3)
                        load(b + 4, i, x, x_ld)
                    if not isinstance(b, int) or b >= 2:
                        store_parts(b - 2, i)

                body(0, 0)
                body(1, 1)
                with sp.Fori(1, B // 2 - 2) as it:
                    body(it * 2, 0)
                    body(it * 2 + 1, 1)
                for b in range(B - 4, B):
                    body(b, b % 2)
                store(B - 1, 1)
                for i in range(2):
                    store_parts(B - 2 + i, i)
                for i in range(2):
                    sp.wait_ge(parts_stored[i], 48 * (B // 2) + 1)
                    sp.wait_ge(x_stored[i], 16 * (B // 2) + 1)

            @block.tensor
            def _(pe):
                pe.wait_ge(const_ld, 16 * NCONST)
                pe.wait_ge(zeros, 2)

                def transpose_x(b, i):
                    pe.wait_ge(x_ld[i], (b - i) * 8 + 16)
                    if begun(b - 1):
                        pe.wait_ge(q_done_act, b - 1)
                    if begun(b - 1):
                        pe.wait_ge(q_done_dve, b - 1)
                    for dk in range(DK):
                        mm = nc.tensor.transpose(tr_ps[:, dk * P:(dk + 1) * P], x[:, i, dk * P:(dk + 1) * P], ident[:, :])
                    mm.then_inc(x_tr_full, 1)

                def project(dst, w):
                    for dk in range(DK):
                        mm = nc.tensor.matmul(dst, x_t[:, dk, :], w[:, dk, :], start=(dk == 0), stop=(dk == DK - 1))
                    return mm

                def project_qk(b):
                    pe.wait_ge(x_t_done, b + 1)
                    if begun(b):
                        pe.wait_ge(scaled_done, b)
                    project(qk_ps[:, 0, :], wq)
                    project(qk_ps[:, 1, :], wk).then_inc(qk_full, 1)

                def project_v(b):
                    if begun(b):
                        pe.wait_ge(k_done, b)
                    project(v_ps[:, :], wv).then_inc(v_full, 1)

                def transpose_qk(b, more):
                    pe.wait_ge(qk_done, b + 1)
                    pe.wait_ge(v_done, b + 1)
                    for f in range(DK):
                        mm = nc.tensor.transpose(v_ps[:, f * P:(f + 1) * P], qk[:, D + f * P:D + (f + 1) * P],
                                                 ident[:, :])
                    mm.then_inc(k_tr_full, 1)
                    if more:
                        pe.wait_ge(x_t_done, b + 2)
                    for f in range(DK):
                        mm = nc.tensor.transpose(tr_ps[:, f * P:(f + 1) * P], qk[:, f * P:(f + 1) * P], ident[:, :])
                    mm.then_inc(q_tr_full, 1)

                def products(b, i, f):
                    if f == 0:
                        pe.wait_ge(k_done, b + 1)
                        pe.wait_ge(q_done_act, b + 1)
                        pe.wait_ge(q_done_dve, b + 1)
                    if begun(b * DK + f - 1):
                        pe.wait_ge(square_done, b * DK + f - 1)
                    nc.tensor.matmul(st_ps[:, f % 2, :], k_t[:, i, f, :],
                                     q_own[:, i, f, :, :].rearrange("p j t -> p (j t)"), start=True, stop=True
                                     ).then_inc(st_full, 1)

                def values(b, i):
                    pe.wait_ge(v_done, b + 1)
                    pe.wait_ge(kept_done, (b + 1) * DK)
                    if begun(b):
                        pe.wait_ge(o_normed, b)
                    for f in range(DK):
                        for j in range(NJ):
                            mm = nc.tensor.matmul(o_ps[HD * j:HD * j + HD, f * P:(f + 1) * P],
                                                  v[:, i, (f * NJ + j) * HD:(f * NJ + j + 1) * HD],
                                                  kept[:, i, f, j, :], start=True, stop=True, skip_group_check=True)
                    mm.then_inc(o_full, 1)
                    if begun(b):
                        pe.wait_ge(y_done, b)
                    for j in range(NJ):
                        mm = nc.tensor.matmul(misc_ps[HD * j:HD * j + HD, :].rearrange("p (f t) -> p f t", f=DK),
                                              ones[:, :], kept[:, i, :, j, :], start=True, stop=True,
                                              skip_group_check=True)
                    mm.then_inc(sums_full, 1)

                def project_o(b):
                    pe.wait_ge(o_normed, b + 1)
                    pe.wait_ge(z_done, b + 1)
                    for f in range(DK):
                        mm = nc.tensor.matmul(misc_ps[:, :], o_norm[:, f * P:(f + 1) * P], wo[:, f, :],
                                              start=(f == 0), stop=(f == DK - 1))
                    mm.then_inc(proj_full, 1)

                transpose_x(0, 0)
                pe.wait_ge(w_ld[0], 16)
                pe.wait_ge(w_ld[1], 16)
                project_qk(0)
                pe.wait_ge(w_ld[2], 16)
                project_v(0)
                transpose_x(1, 1)
                transpose_qk(0, True)
                pe.wait_ge(w_ld[3], 16)

                def body(b, i):
                    more = before(b, 1)
                    if more:
                        project_qk(b + 1)
                    for f in range(DK):
                        products(b, i, f)
                    if more:
                        project_v(b + 1)
                    if not (isinstance(b, int) and b == 0):
                        project_o(b - 1)
                    values(b, i)
                    if before(b, 2):
                        transpose_x(b + 2, i)
                    if more:
                        transpose_qk(b + 1, before(b, 2))

                batches(pe, body)
                project_o(B - 1)

            @block.scalar
            def _(act):
                act.wait_ge(zeros, 2)

                def take_x(b):
                    act.wait_ge(x_tr_full, b + 1)
                    if begun(b):
                        act.wait_ge(v_full, b)
                    nc.scalar.activation(x_t[:, :, :].rearrange("p k t -> p (k t)"), tr_ps[:, :], ACT.Copy
                                         ).then_inc(x_t_done, 1)

                def square(b):
                    act.wait_ge(stat_step, b * 5 + 3)
                    nc.scalar.activation(squares[:, :], centred[:, :], ACT.Square).then_inc(sq_done, 1)

                def deviation(b):
                    act.wait_ge(stat_step, (b + 1) * 5)
                    if begun(b):
                        act.wait_ge(grstd_done, b)
                    nc.scalar.activation(group_std[:, :], group_var[:, :], ACT.Sqrt).then_inc(group_std_done, 1)

                def row_deviation(b):
                    act.wait_ge(ln_step, (b + 1) * 3)
                    nc.scalar.activation(std[:, :], var_eps[:, :], ACT.Sqrt).then_inc(std_done, 1)

                def take_v(b, i):
                    act.wait_ge(v_full, b + 1)
                    if begun(b - 1):
                        act.wait_ge(o_full, b - 1)
                    nc.scalar.activation(v[:, i, :], v_ps[:, :], ACT.Copy).then_inc(v_done, 1)

                def take_qk(b, i):
                    act.wait_ge(k_tr_full, b + 1)
                    nc.scalar.activation(k_t[:, i, :, :].rearrange("p f t -> p (f t)"), v_ps[:, :], ACT.Copy
                                         ).then_inc(k_done, 1)
                    act.wait_ge(q_tr_full, b + 1)
                    for j in range(2):
                        op = nc.scalar.activation(q_own[HD * j:HD * j + HD, i, :, j, :],
                                                  tr_ps[HD * j:HD * j + HD, :].rearrange("p (f t) -> p f t", f=DK),
                                                  ACT.Copy, scale=SCALE)
                    op.then_inc(q_done_act, 1)

                def squared(b, f):
                    act.wait_ge(st_full, b * DK + f + 1)
                    if begun((b - 1) * DK + f + 1):
                        act.wait_ge(kept_done, (b - 1) * DK + f + 1)
                    nc.scalar.activation(weights[:, f, :, :].rearrange("p j t -> p (j t)"), st_ps[:, f % 2, :],
                                         ACT.Square).then_inc(square_done, 1)

                take_x(0)
                square(0)
                deviation(0)
                take_v(0, 0)
                take_x(1)
                take_qk(0, 0)

                def body(b, i):
                    more = before(b, 1)
                    for f in range(DK):
                        squared(b, f)
                    if more:
                        square(b + 1)
                        deviation(b + 1)
                        take_v(b + 1, 1 - i)
                    if not (isinstance(b, int) and b == 0):
                        row_deviation(b - 1)
                    if before(b, 2):
                        take_x(b + 2)
                    if more:
                        take_qk(b + 1, 1 - i)

                batches(act, body)
                row_deviation(B - 1)

            @block.vector
            def _(dve):
                for i in range(2):
                    dve.sem_inc(x_stored[i], 1)
                nc.vector.memset(ones[:, :], 1.0)
                nc.vector.memset(q_own[:, 0, :, :, :], 0.0).then_inc(zeros, 1)
                dve.wait_ge(const_ld, 16 * NCONST)
                dve.wait_ge(zeros, 2)

                def inverse_root(out, root, value, tmp, step, b, done):
                    nc.vector.reciprocal(tmp[:, 0, :], root[:, :]).then_inc(step, 1)
                    dve.wait_ge(step, b * 3 + 1)
                    nc.vector.tensor_tensor(tmp[:, 1, :], tmp[:, 0, :], tmp[:, 0, :], ALU.mult).then_inc(step, 1)
                    dve.wait_ge(step, b * 3 + 2)
                    nc.vector.scalar_tensor_tensor(out=tmp[:, 2, :], in0=tmp[:, 1, :], scalar=-0.5, in1=value[:, :],
                                                   op0=ALU.mult, op1=ALU.mult).then_inc(step, 1)
                    dve.wait_ge(step, b * 3 + 3)
                    nc.vector.scalar_tensor_tensor(out=out[:, :], in0=tmp[:, 2, :], scalar=1.5, in1=tmp[:, 0, :],
                                                   op0=ALU.add, op1=ALU.mult).then_inc(done, 1)

                def feature_map(b):
                    s = b * 5
                    dve.wait_ge(qk_full, b + 1)
                    if begun(b):
                        dve.wait_ge(shifted_done, b)
                    nc.vector.tensor_tensor(groups(scaled[:, :]), groups(qk_ps[:, :, :].rearrange("p a c -> p (a c)")),
                                            by_channel(gamma[:, :]), ALU.mult).then_inc(scaled_done, 1)
                    dve.wait_ge(scaled_done, b + 1)
                    if begun(s):
                        dve.wait_ge(stat_step, s)
                    nc.vector.tensor_tensor(groups(shifted[:, :]), groups(scaled[:, :]), by_channel(beta[:, :]), ALU.add
                                            ).then_inc(shifted_done, 1)
                    dve.wait_ge(shifted_done, b + 1)
                    nc.vector.tensor_reduce(group_sum[:, :], groups(shifted[:, :]), AX.X, ALU.add).then_inc(stat_step, 1)
                    dve.wait_ge(stat_step, s + 1)
                    nc.vector.tensor_scalar(group_mean[:, :], group_sum[:, :], 1.0 / HD, None, ALU.mult
                                            ).then_inc(stat_step, 1)
                    dve.wait_ge(stat_step, s + 2)
                    nc.vector.tensor_tensor(groups(centred[:, :]), groups(shifted[:, :]), by_group(group_mean[:, :]),
                                            ALU.subtract).then_inc(stat_step, 1)
                    dve.wait_ge(sq_done, b + 1)
                    nc.vector.tensor_reduce(group_sq[:, :], groups(squares[:, :]), AX.X, ALU.add).then_inc(stat_step, 1)
                    dve.wait_ge(stat_step, s + 4)
                    nc.vector.tensor_scalar(group_var[:, :], group_sq[:, :], 1.0 / HD, LN_EPS, ALU.mult, ALU.add
                                            ).then_inc(stat_step, 1)
                    dve.wait_ge(group_std_done, b + 1)
                    inverse_root(group_rstd, group_std, group_var, group_step, root_step, b, grstd_done)
                    dve.wait_ge(grstd_done, b + 1)
                    if begun(b):
                        dve.wait_ge(q_tr_full, b)
                    nc.vector.tensor_tensor(groups(qk[:, :]), groups(centred[:, :]), by_group(group_rstd[:, :]),
                                            ALU.mult).then_inc(qk_done, 1)

                def take_q(b, i):
                    dve.wait_ge(q_tr_full, b + 1)
                    for j in range(2, NJ):
                        op = nc.vector.tensor_scalar(q_own[HD * j:HD * j + HD, i, :, j, :],
                                                     tr_ps[HD * j:HD * j + HD, :].rearrange("p (f t) -> p f t", f=DK),
                                                     SCALE, None, ALU.mult)
                    op.then_inc(q_done_dve, 1)

                def normalize(b):
                    dve.wait_ge(sums_full, b + 1)
                    if begun(b):
                        dve.wait_ge(recip_done, b)
                    nc.vector.tensor_scalar(z_eps[:, :], misc_ps[:, :], LN_EPS, None, ALU.add).then_inc(z_done, 1)
                    dve.wait_ge(z_done, b + 1)
                    if begun(b):
                        dve.wait_ge(o_normed, b)
                    nc.vector.reciprocal(recip[:, :], z_eps[:, :]).then_inc(recip_done, 1)
                    dve.wait_ge(recip_done, b + 1)
                    if begun(b):
                        dve.wait_ge(proj_full, b)
                    nc.vector.tensor_tensor(o_norm[:, :], o_ps[:, :], recip[:, :], ALU.mult).then_inc(o_normed, 1)

                def layer_norm(b, i):
                    dve.wait_ge(proj_full, b + 1)
                    dve.wait_ge(res_ld[i], (b - i) * 8 + 16)
                    if begun(b):
                        dve.wait_ge(x_done, b)
                    nc.vector.tensor_tensor(y[:, :], misc_ps[:, :], x_res[:, i, :], ALU.add).then_inc(y_done, 1)
                    dve.wait_ge(y_done, b + 1)
                    nc.vector.bn_stats(stats[:, :], y[:, :]).then_inc(ln_step, 1)
                    dve.wait_ge(ln_step, b * 3 + 1)
                    dve.sem_inc(passed_dve, 1)
                    nc.vector.bn_aggr(mv[:, :], stats[:, :]).then_inc(ln_step, 1)
                    dve.wait_ge(ln_step, b * 3 + 2)
                    nc.vector.tensor_scalar(var_eps[:, :], mv[:, 1:2], LN_EPS, None, ALU.add).then_inc(ln_step, 1)
                    dve.wait_ge(std_done, b + 1)
                    inverse_root(rstd, std, var_eps, row_step, row_root_step, b, rstd_done)
                    dve.wait_ge(rstd_done, b + 1)
                    dve.wait_ge(x_stored[i], (b - i) * 8 + 1)
                    dve.wait_ge(split_step, CREDIT + 5 * (b - 2) + 1)
                    nc.vector.tensor_scalar(x_new[:, i, :], y[:, :], mv[:, 0:1], rstd[:, 0:1],
                                            ALU.subtract, ALU.mult).then_inc(x_done, 1)

                feature_map(0)
                take_q(0, 0)

                def body(b, i):
                    if before(b, 1):
                        feature_map(b + 1)
                    if not (isinstance(b, int) and b == 0):
                        layer_norm(b - 1, 1 - i)
                    normalize(b)
                    if before(b, 1):
                        take_q(b + 1, 1 - i)

                batches(dve, body)
                layer_norm(B - 1, 1)

            @block.gpsimd
            def _(pool):
                for i in range(2):
                    pool.sem_inc(parts_stored[i], 1)
                pool.sem_inc(split_step, CREDIT)
                nc.gpsimd.memset(q_own[:, 1, :, :, :], 0.0).then_inc(zeros, 1)
                pool.wait_ge(const_ld, 16 * NCONST)

                def mask(b, i, f):
                    pool.wait_ge(square_done, b * DK + f + 1)
                    if begun(b - 1):
                        pool.wait_ge(sums_full, b - 1)
                    nc.gpsimd.tensor_tensor(kept[:, i, f, :, :], weights[:, f, :, :],
                                            keep_t[:, :].rearrange("p (o s) -> p o s", o=1).to_broadcast([P, NJ, P]),
                                            ALU.mult).then_inc(kept_done, 1)

                def split(b, i):
                    n = CREDIT + 5 * b
                    pool.wait_ge(x_done, b + 1)
                    pool.sem_inc(passed_pool, 1)
                    nc.gpsimd.tensor_scalar(x_scaled[:, :], x_new[:, i, :], q_scale, None, ALU.mult
                                            ).then_inc(split_step, 1)
                    pool.wait_ge(parts_stored[i], (b - i) * 24 + 1)
                    pool.wait_ge(split_step, n + 1)
                    pool.sem_inc(passed_pool, 1)
                    nc.gpsimd.tensor_copy(parts[:, i, 0, :], x_scaled[:, :]).then_inc(split_step, 1)
                    pool.wait_ge(split_step, n + 2)
                    nc.gpsimd.tensor_tensor(rest[:, :], x_scaled[:, :], parts[:, i, 0, :], ALU.subtract
                                            ).then_inc(split_step, 1)
                    pool.wait_ge(split_step, n + 3)
                    pool.sem_inc(passed_pool, 1)
                    nc.gpsimd.tensor_copy(parts[:, i, 1, :], rest[:, :]).then_inc(split_step, 1)
                    pool.wait_ge(split_step, n + 4)
                    nc.gpsimd.tensor_tensor(parts[:, i, 2, :], rest[:, :], parts[:, i, 1, :], ALU.subtract
                                            ).then_inc(split_step, 1)

                def body(b, i):
                    for f in range(DK):
                        mask(b, i, f)
                    if not isinstance(b, int) or b >= 2:
                        split(b - 2, i)

                batches(pool, body)
                for i in range(2):
                    split(B - 2 + i, i)


TOK = 4
GROUPS = B // TOK
TOPK = 4
RING = 4


def feed_forward(nc, tag, NF, h_t_in, x_in, x_out, w_in_d, w_up_d, w_down_d, half_d, mod_in=None, a_d=None,
                 b_d=None, expert_rows=None, sel_w_d=None, sel_slot_d=None, ctx_in=None, k_parts=None, k_heads=None):
    R = 16
    MOD = mod_in is not None
    MOE = expert_rows is not None
    SPLIT = ctx_in is not None
    N = TOK * P
    with Phase(nc) as ph:
        sem, sb = ph.sem, ph.sb
        IN, UP, DOWN = range(3)
        w_raw = sb(f"{tag}_w_raw", [P, 2, 3, D])
        w_hi = sb(f"{tag}_w_hi", [P, RING, 3, D], F32R)
        w_lo = sb(f"{tag}_w_lo", [P, RING, 3, D], F32R)
        h_hi = sb(f"{tag}_h_hi", [P, 2, TOK, DK, P], F32R)
        h_lo = sb(f"{tag}_h_lo", [P, 2, TOK, DK, P], F32R)
        hidden_hi = sb(f"{tag}_hidden_hi", [P, 2, N], F32R)
        hidden_lo = sb(f"{tag}_hidden_lo", [P, 2, N], F32R)
        h_t = sb(f"{tag}_h_t", [P, 2, TOK, DK, P])
        x = sb(f"{tag}_x", [P, TOK, D])
        gate = sb(f"{tag}_gate", [P, 2, N])
        hidden = sb(f"{tag}_hidden", [P, 2, N])
        y = sb(f"{tag}_y", [P, TOK, D])
        minus_half = sb(f"{tag}_minus_half", [P, 1])
        stats = sb(f"{tag}_stats", [P, 6])
        mv = sb(f"{tag}_mv", [P, 2])
        var_eps = sb(f"{tag}_var_eps", [P, 1])
        rstd = sb(f"{tag}_rstd", [P, 1])
        x_new = sb(f"{tag}_x_new", [P, 2, D])
        if MOD:
            a_w = sb(f"{tag}_a_w", [P, DK, R])
            b_w = sb(f"{tag}_b_w", [R, NF * P])
            mod = sb(f"{tag}_mod", [R, 2, N])
            mod_h = sb(f"{tag}_mod_h", [R, N])
        if SPLIT:
            ctx = sb(f"{tag}_ctx", [P, D])
            rest = sb(f"{tag}_rest", [P, D])
            parts = sb(f"{tag}_parts", [P, 3, D], BF16)
        if MOE:
            sel_w = sb(f"{tag}_sel_w", [P, B, TOPK])
            sel_slot = sb(f"{tag}_sel_slot", [P, B * TOPK], U32)
            rows = sb(f"{tag}_rows", [P, 2, TOPK, D])
        gate_ps = ph.ps(f"{tag}_gate_ps", [P, 2, N])
        up_ps = ph.ps(f"{tag}_up_ps", [P, 2, N])
        out_ps = ph.ps(f"{tag}_out_ps", [P, TOK, D])

        w_ld = [sem(f"{tag}_w_ld{i}") for i in range(2)]
        (w_hi_done, w_lo_done, h_hi_done, h_lo_done, hidden_hi_done, hidden_lo_done) = [sem(f"{tag}_{n}") for n in (
            "w_hi_done w_lo_done h_hi_done h_lo_done hidden_hi_done hidden_lo_done").split()]
        const_ld = sem(f"{tag}_const_ld")
        ctx_ld, parts_stored, split_step = [sem(f"{tag}_{n}") for n in ("ctx_ld", "parts_stored", "split_step")]
        passed_pool = sem(f"{tag}_passed_pool")
        passed_dve = sem(f"{tag}_passed_dve")
        consts = [(minus_half[:, :], half_d)]
        if MOD:
            consts += [(a_w[:, :, :], a_d), (b_w[:, :], b_d)]
        if MOE:
            consts += [(sel_w[:, :, :], sel_w_d), (sel_slot[:, :], sel_slot_d)]
        CONSTS = 16 * len(consts)
        h_ld = [sem(f"{tag}_h_ld{i}") for i in range(2)]
        x_ld = [sem(f"{tag}_x_ld{t}") for t in range(TOK)]
        stored = [sem(f"{tag}_stored{i}") for i in range(2)]
        rows_ld = [sem(f"{tag}_rows_ld{i}") for i in range(2)]
        (ha_full, ha_done, gate_full, up_full, silu_done, hidden_done, down_done, out_full, y_done, ln_step, rstd_done,
         x_done, rows_done) = [sem(f"{tag}_{n}") for n in ("ha_full ha_done gate_full up_full silu_done hidden_done down_done "
                                                "out_full y_done ln_step rstd_done x_done rows_done").split()]
        STEPS = GROUPS * NF

        def each_step(eng, body):
            for n in range(STEPS):
                body(n, n // NF, n % NF)

        def wait_weights_free(eng, n):
            g, f = (n - RING) // NF, (n - RING) % NF
            if n < RING:
                return
            if f == NF - 1:
                eng.wait_ge(out_full, (g + 1) * TOK)
            else:
                eng.wait_ge(down_done, g * (NF - 1) + f + 1)

        with nc.Block() as block:
            @block.sync
            def _(sp):
                def load_h(g, i):
                    for t in range(TOK):
                        sp.dma_start(h_t[:, i, t, :, :],
                                     h_t_in[bass.ds(g * TOK + t, 1), :, :, :].rearrange("o p k t -> p (o k) t")
                                     ).then_inc(h_ld[i], 16)
                        if MOD:
                            sp.dma_start(mod[:, i, t * P:(t + 1) * P],
                                         mod_in[bass.ds(g * TOK + t, 1), :, :].rearrange("o r t -> r (o t)")
                                         ).then_inc(h_ld[i], 16)

                for dst, src in consts:
                    sp.dma_start(dst, src).then_inc(const_ld, 16)
                load_h(0, 0)
                load_h(1, 1)

                def body(g, i):
                    for t in range(TOK):
                        if begun((g - 1) * TOK + t + 1):
                            sp.wait_ge(y_done, (g - 1) * TOK + t + 1)
                        sp.dma_start(x[:, t, :], x_in[bass.ds(g * TOK + t, 1), :, :].rearrange("o p t -> p (o t)")
                                     ).then_inc(x_ld[t], 16)
                    for t in range(TOK):
                        sp.wait_ge(x_done, g * TOK + t + 1)
                        sp.dma_start(x_out[bass.ds(g * TOK + t, 1), :, :].rearrange("o p t -> p (o t)"),
                                     x_new[:, t % 2, :]).then_inc(stored[t % 2], 16)

                body(0, 0)
                load_h(2, 0)
                body(1, 1)
                load_h(3, 1)
                body(2, 0)
                body(3, 1)
                for i in range(2):
                    sp.wait_ge(stored[i], 16 * (B // 2))

            @block.tensor
            def _(pe):
                HL = 16 * TOK * (1 + MOD)
                if MOD:
                    pe.wait_ge(const_ld, CONSTS)

                def low_rank(g, i):
                    if begun(g * NF - 1):
                        pe.wait_ge(silu_done, g * NF - 1)
                    for dk in range(DK):
                        mm = nc.tensor.matmul(gate_ps[0:R, 0, :], a_w[:, dk, :], h_t[:, i, :, dk, :],
                                              start=(dk == 0), stop=(dk == DK - 1))
                    mm.then_inc(ha_full, 1)

                def project(bank, which, n, i, more):
                    last = (w_hi, h_lo)
                    for w, h in ((w_hi, h_hi), (w_lo, h_hi), last):
                        for dk in range(DK):
                            mm = nc.tensor.matmul(bank, w[:, n % RING, which, dk * P:(dk + 1) * P], h[:, i, :, dk, :],
                                                  start=(w is w_hi and h is h_hi and dk == 0),
                                                  stop=(h is h_lo and dk == DK - 1 and not more))
                    return mm

                def gate_up(n, g, i, f):
                    pe.wait_ge(w_hi_done, n + 1)
                    pe.wait_ge(w_lo_done, n + 1)
                    if begun(n - 1):
                        pe.wait_ge(silu_done, n - 1)
                    if MOD and f == 0:
                        pe.wait_ge(ha_done, g + 1)
                    mm = project(gate_ps[:, f % 2, :], IN, n, i, MOD)
                    if MOD:
                        mm = nc.tensor.matmul(gate_ps[:, f % 2, :], b_w[:, f * P:(f + 1) * P], mod_h[:, :],
                                              start=False, stop=True)
                    mm.then_inc(gate_full, 1)
                    if begun(n - 1):
                        pe.wait_ge(hidden_done, n - 1)
                    project(up_ps[:, f % 2, :], UP, n, i, False).then_inc(up_full, 1)

                def down(n, g, f):
                    pe.wait_ge(hidden_hi_done, n + 1)
                    pe.wait_ge(hidden_lo_done, n + 1)
                    for t in range(TOK):
                        if f == 0:
                            if begun((g - 1) * TOK + t + 1):
                                pe.wait_ge(y_done, (g - 1) * TOK + t + 1)
                        tokens = slice(t * P, (t + 1) * P)
                        for k, (a, w) in enumerate(((hidden_hi, w_hi), (hidden_lo, w_hi), (hidden_hi, w_lo))):
                            mm = nc.tensor.matmul(out_ps[:, t, :], a[:, f % 2, tokens], w[:, n % RING, DOWN, :],
                                                  start=(f == 0 and k == 0), stop=(f == NF - 1 and k == 2))
                        if f == NF - 1:
                            mm.then_inc(out_full, 1)
                        elif t == TOK - 1:
                            mm.then_inc(down_done, 1)

                for g in range(GROUPS):
                    i = g % 2
                    pe.wait_ge(h_ld[i], (g // 2 + 1) * HL)
                    pe.wait_ge(h_hi_done, g + 1)
                    pe.wait_ge(h_lo_done, g + 1)
                    if MOD:
                        low_rank(g, i)
                    gate_up(g * NF, g, i, 0)
                    for f in range(1, NF):
                        gate_up(g * NF + f, g, i, f)
                        down(g * NF + f - 1, g, f - 1)
                    down((g + 1) * NF - 1, g, NF - 1)

            @block.scalar
            def _(act):
                def load_ctx(b):
                    if begun(4 * b):
                        act.wait_ge(split_step, 4 * b)
                    act.dma_start(ctx[:, :], ctx_in[bass.ds(b, 1), :, :].rearrange("o p t -> p (o t)")
                                  ).then_inc(ctx_ld, 16)

                def store_parts(b):
                    act.wait_ge(split_step, 4 * (b + 1))
                    for p in range(3):
                        c = P // k_heads
                        dst = k_parts[bass.ds(b, 1), p * c:(p + 1) * c, :].rearrange("o c (h t) -> (o h) c t", t=D)
                        act.dma_start(dst, parts[:, p, :]).then_inc(parts_stored, 16)

                def load_weights(n):
                    f = n % NF
                    if begun(n - 1):
                        act.wait_ge(w_hi_done, n - 1)
                    if begun(n - 1):
                        act.wait_ge(w_lo_done, n - 1)
                    cols = slice(f * P, (f + 1) * P)
                    for which, src in ((IN, w_in_d), (UP, w_up_d)):
                        act.dma_start(w_raw[:, n % 2, which, :].rearrange("p (k c) -> p k c", c=P), src[:, :, cols]
                                      ).then_inc(w_ld[n % 2], 16)
                    act.dma_start(w_raw[:, n % 2, DOWN, :], w_down_d[:, f, :]).then_inc(w_ld[n % 2], 16)

                def weights_hi(n):
                    act.wait_ge(w_ld[n % 2], 48 * (n // 2 + 1))
                    wait_weights_free(act, n)
                    nc.scalar.activation(w_hi[:, n % RING, :, :], w_raw[:, n % 2, :, :], ACT.Copy
                                         ).then_inc(w_hi_done, 1)

                def h_high(g):
                    act.wait_ge(h_ld[g % 2], (g // 2 + 1) * 16 * TOK * (1 + MOD))
                    nc.scalar.activation(h_hi[:, g % 2, :, :, :], h_t[:, g % 2, :, :, :], ACT.Copy
                                         ).then_inc(h_hi_done, 1)

                load_weights(0)
                load_weights(1)
                h_high(0)
                for n in range(2):
                    weights_hi(n)
                    load_weights(n + 2)

                def body(n, g, f):
                    if n + 2 < STEPS:
                        weights_hi(n + 2)
                    if SPLIT and n % (NF // TOK) == 0:
                        if n > 0:
                            store_parts(n // (NF // TOK) - 1)
                        load_ctx(n // (NF // TOK))
                    act.wait_ge(gate_full, n + 1)
                    if begun(n - 1):
                        act.wait_ge(hidden_done, n - 1)
                    nc.scalar.activation(gate[:, f % 2, :], gate_ps[:, f % 2, :], ACT.Silu).then_inc(silu_done, 1)
                    if f == NF - 2 and g < GROUPS - 1:
                        h_high(g + 1)
                    act.wait_ge(hidden_done, n + 1)
                    nc.scalar.activation(hidden_hi[:, f % 2, :], hidden[:, f % 2, :], ACT.Copy
                                         ).then_inc(hidden_hi_done, 1)
                    if n + 4 < STEPS:
                        load_weights(n + 4)

                each_step(act, body)
                if SPLIT:
                    store_parts(B - 1)
                    act.wait_ge(parts_stored, 48 * B)

            @block.vector
            def _(dve):
                def take_output(g, t):
                    n = g * TOK + t
                    dve.wait_ge(out_full, n + 1)
                    dve.wait_ge(x_ld[t], 16 * (g + 1))
                    if begun((g - 1) * TOK + t + 1):
                        dve.wait_ge(x_done, (g - 1) * TOK + t + 1)
                    if MOE:
                        nc.vector.tensor_tensor(y[:, t, :], out_ps[:, t, :], x[:, t, :], ALU.add).then_inc(y_done, 1)
                    else:
                        nc.vector.scalar_tensor_tensor(out=y[:, t, :], in0=x[:, t, :], scalar=2.0,
                                                       in1=out_ps[:, t, :], op0=ALU.mult, op1=ALU.add
                                                       ).then_inc(y_done, 1)

                def normalize(g, t):
                    n = g * TOK + t
                    dve.wait_ge(y_done, n + 1)
                    if MOE:
                        dve.wait_ge(rows_ld[t % 2], (g * (TOK // 2) + t // 2 + 1) * 16 * TOPK)
                        for k in range(TOPK):
                            nc.vector.scalar_tensor_tensor(
                                out=y[:, t, :], in0=rows[:, t % 2, k, :], in1=y[:, t, :],
                                scalar=sel_w[:, n, k:k + 1], op0=ALU.mult, op1=ALU.add).then_inc(rows_done, 1)
                            dve.wait_ge(rows_done, n * TOPK + k + 1)
                    nc.vector.bn_stats(stats[:, :], y[:, t, :]).then_inc(ln_step, 1)
                    dve.wait_ge(ln_step, n * 3 + 1)
                    dve.sem_inc(passed_dve, 1)
                    nc.vector.bn_aggr(mv[:, :], stats[:, :]).then_inc(ln_step, 1)
                    dve.wait_ge(ln_step, n * 3 + 2)
                    nc.vector.tensor_scalar(var_eps[:, :], mv[:, 1:2], LN_EPS, None, ALU.add).then_inc(ln_step, 1)
                    dve.wait_ge(rstd_done, n + 1)
                    if begun(g * (TOK // 2) * 16 + 16 * (t // 2)):
                        dve.wait_ge(stored[t % 2], g * (TOK // 2) * 16 + 16 * (t // 2))
                    nc.vector.tensor_scalar(x_new[:, t % 2, :], y[:, t, :], mv[:, 0:1], rstd[:, 0:1],
                                            ALU.subtract, ALU.mult).then_inc(x_done, 1)

                if MOE:
                    dve.wait_ge(const_ld, CONSTS)

                def weights_lo(n):
                    dve.wait_ge(w_hi_done, n + 1)
                    wait_weights_free(dve, n)
                    nc.vector.tensor_tensor(w_lo[:, n % RING, :, :], w_raw[:, n % 2, :, :], w_hi[:, n % RING, :, :],
                                            ALU.subtract).then_inc(w_lo_done, 1)

                def h_low(g):
                    dve.wait_ge(h_hi_done, g + 1)
                    nc.vector.tensor_tensor(h_lo[:, g % 2, :, :, :], h_t[:, g % 2, :, :, :], h_hi[:, g % 2, :, :, :],
                                            ALU.subtract).then_inc(h_lo_done, 1)

                h_low(0)
                weights_lo(0)
                weights_lo(1)

                def body(n, g, f):
                    if MOD and f == 0:
                        dve.wait_ge(ha_full, g + 1)
                        if begun(g * NF):
                            dve.wait_ge(gate_full, g * NF)
                        nc.vector.scalar_tensor_tensor(out=mod_h[:, :], in0=mod[:, g % 2, :], scalar=0.1,
                                                       in1=gate_ps[0:R, 0, :], op0=ALU.mult, op1=ALU.mult
                                                       ).then_inc(ha_done, 1)
                    if n + 2 < STEPS:
                        weights_lo(n + 2)
                    dve.wait_ge(silu_done, n + 1)
                    dve.wait_ge(up_full, n + 1)
                    if begun(n - 1):
                        dve.wait_ge(hidden_hi_done, n - 1)
                    if begun(n - 1):
                        dve.wait_ge(hidden_lo_done, n - 1)
                    nc.vector.tensor_tensor(hidden[:, f % 2, :], gate[:, f % 2, :], up_ps[:, f % 2, :], ALU.mult
                                            ).then_inc(hidden_done, 1)
                    if f == NF - 2 and g < GROUPS - 1:
                        h_low(g + 1)
                    dve.wait_ge(hidden_hi_done, n + 1)
                    nc.vector.tensor_tensor(hidden_lo[:, f % 2, :], hidden[:, f % 2, :], hidden_hi[:, f % 2, :],
                                            ALU.subtract).then_inc(hidden_lo_done, 1)
                    if g > 0 and f < TOK:
                        normalize(g - 1, f)
                    if f == NF - 1:
                        for t in range(TOK):
                            take_output(g, t)

                each_step(dve, body)
                for t in range(TOK):
                    normalize(GROUPS - 1, t)

            @block.gpsimd
            def _(pool):
                pool.wait_ge(const_ld, CONSTS)

                def gather(n):
                    if begun((n - 1) * TOPK):
                        pool.wait_ge(rows_done, (n - 1) * TOPK)
                    for k in range(TOPK):
                        col = n * TOPK + k
                        nc.gpsimd.indirect_dma_start(
                            rows[:, n % 2, k, :], None, expert_rows,
                            bass.IndirectOffsetOnAxis(ap=sel_slot[:, col:col + 1], axis=0)
                        ).then_inc(rows_ld[n % 2], 16)

                def power(n):
                    pool.wait_ge(ln_step, n * 3 + 3)
                    nc.gpsimd.tensor_tensor(rstd[:, :], var_eps[:, :], minus_half[:, :], ALU.pow
                                            ).then_inc(rstd_done, 1)

                def split(b):
                    pool.wait_ge(ctx_ld, 16 * (b + 1))
                    if begun(48 * b):
                        pool.wait_ge(parts_stored, 48 * b)
                    pool.sem_inc(passed_pool, 1)
                    nc.gpsimd.tensor_copy(parts[:, 0, :], ctx[:, :]).then_inc(split_step, 1)
                    pool.wait_ge(split_step, 4 * b + 1)
                    nc.gpsimd.tensor_tensor(rest[:, :], ctx[:, :], parts[:, 0, :], ALU.subtract).then_inc(split_step, 1)
                    pool.wait_ge(split_step, 4 * b + 2)
                    pool.sem_inc(passed_pool, 1)
                    nc.gpsimd.tensor_copy(parts[:, 1, :], rest[:, :]).then_inc(split_step, 1)
                    pool.wait_ge(split_step, 4 * b + 3)
                    nc.gpsimd.tensor_tensor(parts[:, 2, :], rest[:, :], parts[:, 1, :], ALU.subtract
                                            ).then_inc(split_step, 1)

                def split_and_power(g):
                    for t in range(TOK):
                        split(g * TOK + t)
                    for t in range(TOK):
                        power(g * TOK + t)

                if MOE:
                    gather(0)
                    gather(1)
                    for n in range(B):
                        power(n)
                        if n + 2 < B:
                            gather(n + 2)
                elif SPLIT:
                    for g in range(GROUPS):
                        split_and_power(g)
                else:
                    with pool.Fori(0, B) as n:
                        power(n)


E = 64
CAP = 64
SLOTS = E * CAP
NSEL = B * TOPK
TABLE = SLOTS + NSEL * P


def router(nc, tag, x_in, h_t_out, table_out, sel_w_out, sel_slot_out, rw_d, rbias_d, ident_d, before_d, ones_d,
           iota_d, trash_d, token_d, zero_d):
    with Phase(nc) as ph:
        sem, sb = ph.sem, ph.sb
        rw = sb(f"{tag}_rw", [P, DK, E])
        rbias = sb(f"{tag}_rbias", [P, E])
        ident = sb(f"{tag}_ident", [P, P])
        earlier = sb(f"{tag}_earlier", [P, P], BF16)
        ones = sb(f"{tag}_ones", [P, P], BF16)
        iota = sb(f"{tag}_iota", [P, E])
        trash = sb(f"{tag}_trash", [P, NSEL])
        token = sb(f"{tag}_token", [P, B], U32)
        x = sb(f"{tag}_x", [P, 2, D])
        x_t = sb(f"{tag}_x_t", [P, 2, DK, P])
        logits = sb(f"{tag}_logits", [P, B, E])
        biased = sb(f"{tag}_biased", [P, B, E])
        top = sb(f"{tag}_top", [P, B, 8])
        top_i = sb(f"{tag}_top_i", [P, B, 8], U32)
        expert = sb(f"{tag}_expert", [P, B, TOPK])
        row_max = sb(f"{tag}_row_max", [P, B])
        row_sum = sb(f"{tag}_row_sum", [P, B])
        row_inv = sb(f"{tag}_row_inv", [P, B])
        shifted = sb(f"{tag}_shifted", [P, B, E])
        probs = sb(f"{tag}_probs", [P, B, E])
        onehot = sb(f"{tag}_onehot", [P, TOPK, B, E], BF16)
        chosen = sb(f"{tag}_chosen", [P, B, E], BF16)
        pair = sb(f"{tag}_pair", [P, 2, B, E], BF16)
        prefix = sb(f"{tag}_prefix", [P, 2, B, E], BF16)
        picked = sb(f"{tag}_picked", [P, 2, B, E])
        sel_p = sb(f"{tag}_sel_p", [P, B, TOPK])
        sel_sum = sb(f"{tag}_sel_sum", [P, B])
        sel_inv = sb(f"{tag}_sel_inv", [P, B])
        sel_w = sb(f"{tag}_sel_w", [P, B, TOPK])
        place = sb(f"{tag}_place", [P, B, TOPK])
        kept = sb(f"{tag}_kept", [P, B, TOPK])
        slot = sb(f"{tag}_slot", [P, B, TOPK])
        slot_i = sb(f"{tag}_slot_i", [P, NSEL], U32)
        read_slot = sb(f"{tag}_read_slot", [P, B, TOPK], U32)
        t_ps = ph.ps(f"{tag}_t_ps", [P, 2, DK, P])
        logit_ps = ph.ps(f"{tag}_logit_ps", [P, 2, D])
        count_ps = ph.ps(f"{tag}_count_ps", [P, B, E])

        const_ld = sem(f"{tag}_const_ld")
        x_ld = [sem(f"{tag}_x_ld{i}") for i in range(2)]
        h_stored = [sem(f"{tag}_h_stored{i}") for i in range(2)]
        (table_zero, sel_stored, scattered, t_full, x_t_done, logit_full, logit_done, counted, probs_ready, exp_done,
         step, slots_ready, weights_ready, chosen_ready) = [sem(f"{tag}_{n}") for n in (
             "table_zero sel_stored scattered t_full x_t_done logit_full logit_done counted probs_ready exp_done "
             "step slots_ready weights_ready chosen_ready").split()]
        CONSTS = ((rw[:, :, :], rw_d), (rbias[:, :], rbias_d), (ident[:, :], ident_d), (earlier[:, :], before_d),
                  (ones[:, :], ones_d), (iota[:, :], iota_d), (trash[:, :], trash_d), (token[:, :], token_d))

        def tiles(eng, body):
            body(0, 0)
            body(1, 1)
            with eng.Fori(1, B // 2) as it:
                body(it * 2, 0)
                body(it * 2 + 1, 1)

        with nc.Block() as block:
            @block.sync
            def _(sp):
                for dst, src in CONSTS:
                    sp.dma_start(dst, src).then_inc(const_ld, 16)
                sp.dma_start(table_out.rearrange("(p n) o -> p (n o)", p=P), zero_d).then_inc(table_zero, 16)

                def load(b, i):
                    sp.dma_start(x[:, i, :], x_in[bass.ds(b, 1), :, :].rearrange("o p t -> p (o t)")
                                 ).then_inc(x_ld[i], 16)

                def store(b, i):
                    sp.wait_ge(x_t_done, b + 1)
                    sp.dma_start(h_t_out[bass.ds(b, 1), :, :, :].rearrange("o p k t -> p (o k) t"), x_t[:, i, :, :]
                                 ).then_inc(h_stored[i], 16)

                load(0, 0)
                load(1, 1)

                def body(b, i):
                    sp.wait_ge(t_full, b + 1)
                    if not (isinstance(b, int) and b >= B - 2):
                        load(b + 2, i)
                    store(b, i)

                body(0, 0)
                body(1, 1)
                with sp.Fori(1, B // 2 - 1) as it:
                    body(it * 2, 0)
                    body(it * 2 + 1, 1)
                body(B - 2, 0)
                body(B - 1, 1)
                sp.wait_ge(slots_ready, 1)
                sp.dma_start(sel_slot_out, read_slot[:, :, :].rearrange("p b k -> p (b k)")).then_inc(sel_stored, 16)
                sp.wait_ge(weights_ready, 1)
                sp.dma_start(sel_w_out, sel_w[:, :, :].rearrange("p b k -> p (b k)")).then_inc(sel_stored, 16)
                for i in range(2):
                    sp.wait_ge(h_stored[i], 16 * (B // 2))
                sp.wait_ge(sel_stored, 32)

            @block.tensor
            def _(pe):
                pe.wait_ge(const_ld, 16 * len(CONSTS))

                def transpose(b, i):
                    pe.wait_ge(x_ld[i], (b - i) * 8 + 16)
                    if begun(b - 1):
                        pe.wait_ge(x_t_done, b - 1)
                    for dk in range(DK):
                        mm = nc.tensor.transpose(t_ps[:, i, dk, :], x[:, i, dk * P:(dk + 1) * P], ident[:, :])
                    mm.then_inc(t_full, 1)

                def product(b, i):
                    pe.wait_ge(x_t_done, b + 1)
                    if begun(b - 1):
                        pe.wait_ge(logit_done, b - 1)
                    for dk in range(DK):
                        mm = nc.tensor.matmul(logit_ps[:, i, 0:E], x_t[:, i, dk, :], rw[:, dk, :], start=(dk == 0),
                                              stop=(dk == DK - 1))
                    mm.then_inc(logit_full, 1)

                transpose(0, 0)
                transpose(1, 1)
                product(0, 0)
                transpose(2, 0)
                product(1, 1)
                transpose(3, 1)
                product(2, 0)
                with pe.Fori(1, B // 2 - 1) as it:
                    transpose(it * 2 + 2, 0)
                    product(it * 2 + 1, 1)
                    transpose(it * 2 + 3, 1)
                    product(it * 2 + 2, 0)
                product(B - 1, 1)

                pe.wait_ge(chosen_ready, 2)
                for h in range(2):
                    half = slice(h * (B // 2), (h + 1) * (B // 2))
                    nc.tensor.matmul(count_ps[:, half, :], earlier[:, :], chosen[:, half, :], start=True, stop=False)
                    mm = nc.tensor.matmul(count_ps[:, half, :], ones[:, :], prefix[:, 0, half, :], start=False,
                                          stop=True)
                mm.then_inc(counted, 1)

            @block.scalar
            def _(act):
                def body(b, i):
                    act.wait_ge(t_full, b + 1)
                    if begun((b - i) * 8):
                        act.wait_ge(h_stored[i], (b - i) * 8)
                    if begun(b - 1):
                        act.wait_ge(logit_full, b - 1)
                    nc.scalar.activation(x_t[:, i, :, :], t_ps[:, i, :, :], ACT.Copy).then_inc(x_t_done, 1)

                tiles(act, body)
                act.wait_ge(probs_ready, 1)
                nc.scalar.activation(probs[:, :, :], shifted[:, :, :], ACT.Exp).then_inc(exp_done, 1)

            @block.vector
            def _(dve):
                done = 0

                def chain(op):
                    nonlocal done
                    op.then_inc(step, 1)
                    done += 1
                    dve.wait_ge(step, done)

                def per_tile(a):
                    return a.rearrange("p (b o) -> p b o", o=1).to_broadcast([P, B, E])

                def per_expert(a):
                    return a.rearrange("p (o e) -> p o e", o=1).to_broadcast([P, B, E])

                dve.wait_ge(const_ld, 16 * len(CONSTS))

                def take(b, i):
                    dve.wait_ge(logit_full, b + 1)
                    nc.vector.tensor_copy(logits[:, bass.ds(b, 1), :].rearrange("p o e -> p (o e)"),
                                          logit_ps[:, i, 0:E]).then_inc(logit_done, 1)

                tiles(dve, take)
                dve.wait_ge(logit_done, B)
                chain(nc.vector.tensor_reduce(row_max[:, :], logits[:, :, :], AX.X, ALU.max))
                nc.vector.tensor_tensor(shifted[:, :, :], logits[:, :, :], per_tile(row_max[:, :]), ALU.subtract
                                        ).then_inc(probs_ready, 1)
                chain(nc.vector.tensor_tensor(biased[:, :, :], logits[:, :, :], per_expert(rbias[:, :]), ALU.add))
                for b in range(B):
                    nc.vector.max(top[:, b, :], biased[:, b, :]).then_inc(step, 1)
                done += B
                dve.wait_ge(step, done)
                for b in range(B):
                    nc.vector.max_index(top_i[:, b, :], top[:, b, :], biased[:, b, :]).then_inc(step, 1)
                done += B
                dve.wait_ge(step, done)
                chain(nc.vector.tensor_copy(expert[:, :, :], top_i[:, :, 0:TOPK]))
                for k in range(TOPK):
                    nc.vector.tensor_tensor(onehot[:, k, :, :], per_expert(iota[:, :]),
                                            expert[:, :, k:k + 1].to_broadcast([P, B, E]), ALU.is_equal
                                            ).then_inc(step, 1)
                done += TOPK
                dve.wait_ge(step, done)
                nc.vector.tensor_tensor(pair[:, 0, :, :], onehot[:, 0, :, :], onehot[:, 1, :, :], ALU.add
                                        ).then_inc(step, 1)
                nc.vector.tensor_tensor(pair[:, 1, :, :], onehot[:, 2, :, :], onehot[:, 3, :, :], ALU.add
                                        ).then_inc(step, 1)
                done += 2
                dve.wait_ge(step, done)
                chain(nc.vector.tensor_tensor(chosen[:, :, :], pair[:, 0, :, :], pair[:, 1, :, :], ALU.add))
                nc.vector.memset(prefix[:, 0, 0:1, :], 0.0).then_inc(step, 1)
                nc.vector.tensor_copy(prefix[:, 0, 1:B, :], chosen[:, 0:B - 1, :]).then_inc(step, 1)
                done += 2
                dve.wait_ge(step, done)
                cur, reach = 0, 1
                while reach < B:
                    last = reach * 2 >= B
                    signal = chosen_ready if last else step
                    nc.vector.tensor_copy(prefix[:, 1 - cur, 0:reach, :], prefix[:, cur, 0:reach, :]
                                          ).then_inc(signal, 1)
                    nc.vector.tensor_tensor(prefix[:, 1 - cur, reach:B, :], prefix[:, cur, reach:B, :],
                                            prefix[:, cur, 0:B - reach, :], ALU.add).then_inc(signal, 1)
                    if not last:
                        done += 2
                        dve.wait_ge(step, done)
                    cur, reach = 1 - cur, reach * 2
                assert cur == 0

                dve.wait_ge(counted, 1)
                for k in range(TOPK):
                    chain(nc.vector.tensor_tensor(picked[:, 1, :, :], count_ps[:, :, :], onehot[:, k, :, :],
                                                  ALU.mult))
                    chain(nc.vector.tensor_reduce(place[:, :, k], picked[:, 1, :, :], AX.X, ALU.add))
                chain(nc.vector.tensor_scalar(kept[:, :, :], place[:, :, :], float(CAP), None, ALU.is_lt))
                chain(nc.vector.scalar_tensor_tensor(out=slot[:, :, :], in0=expert[:, :, :], scalar=float(CAP),
                                                     in1=place[:, :, :], op0=ALU.mult, op1=ALU.add))
                flat = "p b k -> p (b k)"
                chain(nc.vector.tensor_tensor(slot[:, :, :].rearrange(flat), slot[:, :, :].rearrange(flat),
                                              trash[:, :], ALU.subtract))
                chain(nc.vector.tensor_tensor(slot[:, :, :], slot[:, :, :], kept[:, :, :], ALU.mult))
                chain(nc.vector.tensor_tensor(slot[:, :, :].rearrange(flat), slot[:, :, :].rearrange(flat),
                                              trash[:, :], ALU.add))
                chain(nc.vector.tensor_copy(slot_i[:, :], slot[:, :, :].rearrange(flat)))
                nc.vector.tensor_scalar(read_slot[:, :, :], slot[:, :, :], float(SLOTS), None, ALU.min
                                        ).then_inc(slots_ready, 1)

                dve.wait_ge(exp_done, 1)
                chain(nc.vector.tensor_reduce(row_sum[:, :], probs[:, :, :], AX.X, ALU.add))
                chain(nc.vector.reciprocal(row_inv[:, :], row_sum[:, :]))
                for k in range(TOPK):
                    chain(nc.vector.tensor_tensor(picked[:, 0, :, :], probs[:, :, :], onehot[:, k, :, :], ALU.mult))
                    chain(nc.vector.tensor_reduce(sel_w[:, :, k], picked[:, 0, :, :], AX.X, ALU.add))
                chain(nc.vector.tensor_tensor(sel_p[:, :, :], sel_w[:, :, :], row_inv[:, :].rearrange(
                    "p (b o) -> p b o", o=1).to_broadcast([P, B, TOPK]), ALU.mult))
                chain(nc.vector.tensor_reduce(sel_sum[:, :], sel_p[:, :, :], AX.X, ALU.add))
                chain(nc.vector.reciprocal(sel_inv[:, :], sel_sum[:, :]))
                nc.vector.tensor_tensor(sel_w[:, :, :], sel_p[:, :, :], sel_inv[:, :].rearrange(
                    "p (b o) -> p b o", o=1).to_broadcast([P, B, TOPK]), ALU.mult).then_inc(weights_ready, 1)

            @block.gpsimd
            def _(pool):
                pool.wait_ge(const_ld, 16 * len(CONSTS))
                pool.wait_ge(table_zero, 16)
                pool.wait_ge(slots_ready, 1)
                for n in range(NSEL):
                    nc.gpsimd.indirect_dma_start(
                        table_out, bass.IndirectOffsetOnAxis(ap=slot_i[:, n:n + 1], axis=0),
                        token[:, n // TOPK:n // TOPK + 1], None).then_inc(scattered, 16)
                pool.wait_ge(scattered, 16 * NSEL)


def experts(nc, tag, x_rows, table, y_out, gate_d, up_d, down_d, ident_d):
    PAIRS = E // 2
    RING = 4
    with Phase(nc) as ph:
        sem, sb = ph.sem, ph.sb
        token = sb(f"{tag}_token", [P, PAIRS], U32)
        ident = sb(f"{tag}_ident", [P, P])
        zero_row = sb(f"{tag}_zero_row", [1, D])
        w_gate = sb(f"{tag}_w_gate", [P, RING, 2, DK, P])
        w_up = sb(f"{tag}_w_up", [P, RING, 2, DK, P])
        w_down = sb(f"{tag}_w_down", [P, RING, 2, D])
        x = sb(f"{tag}_x", [P, RING, D])
        x_t = sb(f"{tag}_x_t", [P, 2, DK, P])
        gate = sb(f"{tag}_gate", [P, 2, P])
        hidden = sb(f"{tag}_hidden", [P, 2, P])
        y = sb(f"{tag}_y", [P, 2, D])
        t_ps = ph.ps(f"{tag}_t_ps", [P, 2, DK, P])
        gate_ps = ph.ps(f"{tag}_gate_ps", [P, 2, D])
        up_ps = ph.ps(f"{tag}_up_ps", [P, 2, D])
        y_ps = ph.ps(f"{tag}_y_ps", [P, 2, D])

        w_ld = [sem(f"{tag}_w_ld{i}") for i in range(RING)]
        x_ld = [sem(f"{tag}_x_ld{i}") for i in range(RING)]
        stored = [sem(f"{tag}_stored{i}") for i in range(2)]
        (table_ld, ident_ld, zeros, zero_stored, t_full, x_t_done, gate_full, up_full, silu_done, hidden_done, y_full,
         y_done) = [sem(f"{tag}_{n}") for n in ("table_ld ident_ld zeros zero_stored t_full x_t_done gate_full "
                                                "up_full silu_done hidden_done y_full y_done").split()]

        def pairs(eng, body):
            for i in range(RING):
                body(i, i)
            with eng.Fori(1, PAIRS // RING) as it:
                for i in range(RING):
                    body(it * RING + i, i)

        with nc.Block() as block:
            @block.sync
            def _(sp):
                sp.dma_start(token[:, :], table[0:SLOTS, :].rearrange("(n p) o -> p (n o)", p=P),
                             allow_slow_non_contiguous=True
                             ).then_inc(table_ld, 16)
                sp.dma_start(ident[:, :], ident_d).then_inc(ident_ld, 16)

                def body(n, i):
                    if begun(n - RING + 1):
                        sp.wait_ge(y_full, n - RING + 1)
                    for dst, src in ((w_gate[:, i, :, :, :], gate_d), (w_up[:, i, :, :, :], up_d)):
                        for e in range(2):
                            sp.dma_start(dst[:, e, :, :], src[bass.ds(n * 2 + e, 1), :, :, :].rearrange(
                                "o p k f -> p (o k) f")).then_inc(w_ld[i], 16)
                    sp.dma_start(w_down[:, i, :, :], down_d[bass.ds(n * 2, 2), :, :].rearrange("e p f -> p e f")
                                 ).then_inc(w_ld[i], 16)

                pairs(sp, body)

            @block.scalar
            def _(act):
                act.wait_ge(zeros, 1)
                act.dma_start(y_out[SLOTS:SLOTS + 1, :], zero_row[:, :]).then_inc(zero_stored, 16)

                def store(n, i):
                    act.wait_ge(y_done, n + 1)
                    act.dma_start(y_out[bass.ds(n * P, P), :], y[:, i % 2, :]).then_inc(stored[i % 2], 16)

                def body(n, i):
                    act.wait_ge(t_full, n + 1)
                    if begun(n - 1):
                        act.wait_ge(up_full, n - 1)
                    nc.scalar.activation(x_t[:, i % 2, :, :], t_ps[:, i % 2, :, :], ACT.Copy).then_inc(x_t_done, 1)
                    act.wait_ge(gate_full, n + 1)
                    if begun(n - 1):
                        act.wait_ge(hidden_done, n - 1)
                    nc.scalar.activation(gate[:, i % 2, :], gate_ps[:, i % 2, 0:P], ACT.Silu).then_inc(silu_done, 1)
                    if isinstance(n, int) and n == 0:
                        return
                    store(n - 1, i - 1 + RING)

                pairs(act, body)
                store(PAIRS - 1, RING - 1)
                for i in range(2):
                    act.wait_ge(stored[i], 16 * (PAIRS // 2))
                act.wait_ge(zero_stored, 16)

            @block.tensor
            def _(pe):
                pe.wait_ge(ident_ld, 16)

                def transpose(n, i):
                    pe.wait_ge(x_ld[i], (n - i) * (16 // RING) + 16)
                    if begun(n - 1):
                        pe.wait_ge(x_t_done, n - 1)
                    for dk in range(DK):
                        mm = nc.tensor.transpose(t_ps[:, i % 2, dk, :], x[:, i, dk * P:(dk + 1) * P], ident[:, :])
                    mm.then_inc(t_full, 1)

                def gate_up(n, i):
                    pe.wait_ge(w_ld[i], (n - i) * (80 // RING) + 80)
                    pe.wait_ge(x_t_done, n + 1)
                    for bank, w, taken, full in ((gate_ps, w_gate, silu_done, gate_full),
                                                 (up_ps, w_up, hidden_done, up_full)):
                        if begun(n - 1):
                            pe.wait_ge(taken, n - 1)
                        for e in range(2):
                            tokens = slice(e * CAP, (e + 1) * CAP)
                            for dk in range(DK):
                                mm = nc.tensor.matmul(bank[:, i % 2, tokens], w[:, i, e, dk, :],
                                                      x_t[:, i % 2, dk, tokens], start=(dk == 0), stop=(dk == DK - 1))
                        mm.then_inc(full, 1)

                def down(n, i):
                    pe.wait_ge(hidden_done, n + 1)
                    if begun(n - 1):
                        pe.wait_ge(y_done, n - 1)
                    for e in range(2):
                        tokens = slice(e * CAP, (e + 1) * CAP)
                        mm = nc.tensor.matmul(y_ps[tokens, i % 2, :], hidden[:, i % 2, tokens], w_down[:, i, e, :],
                                              start=True, stop=True)
                    mm.then_inc(y_full, 1)

                transpose(0, 0)

                def step(n, i):
                    gate_up(n, i)
                    transpose(n + 1, (i + 1) % RING) if not (isinstance(n, int) and n == PAIRS - 1) else None
                    down(n, i)

                for i in range(RING - 1):
                    step(i, i)
                with pe.Fori(0, PAIRS // RING - 1) as it:
                    for i in range(RING):
                        step(it * RING + (RING - 1 + i), (RING - 1 + i) % RING)
                step(PAIRS - 1, RING - 1)

            @block.vector
            def _(dve):
                def body(n, i):
                    dve.wait_ge(silu_done, n + 1)
                    dve.wait_ge(up_full, n + 1)
                    if begun(n - 1):
                        dve.wait_ge(y_full, n - 1)
                    nc.vector.tensor_tensor(hidden[:, i % 2, :], gate[:, i % 2, :], up_ps[:, i % 2, 0:P], ALU.mult
                                            ).then_inc(hidden_done, 1)
                    dve.wait_ge(y_full, n + 1)
                    if begun((n - i % 2) * 8):
                        dve.wait_ge(stored[i % 2], (n - i % 2) * 8)
                    nc.vector.tensor_copy(y[:, i % 2, :], y_ps[:, i % 2, :]).then_inc(y_done, 1)

                pairs(dve, body)

            @block.gpsimd
            def _(pool):
                nc.gpsimd.memset(zero_row[:, :], 0.0).then_inc(zeros, 1)
                pool.wait_ge(table_ld, 16)

                for n in range(PAIRS):
                    i = n % RING
                    if begun(n - RING + 1):
                        pool.wait_ge(t_full, n - RING + 1)
                    nc.gpsimd.indirect_dma_start(x[:, i, :], None, x_rows,
                                                 bass.IndirectOffsetOnAxis(ap=token[:, n:n + 1], axis=0)
                                                 ).then_inc(x_ld[i], 16)


def decoder(nc, i, out):
    def dram(name, shape, dt=F32):
        return nc.dram_tensor(f"{name}_dram", shape, dt).ap()

    x1, x2, x3, x4, x5 = [dram(f"x{n}", (B, P, D)) for n in range(1, 6)]

    q, k = dram("a0_q", (B, 48, 8 * D), BF16), dram("a0_k", (B, 48, 8 * P), BF16)
    v = dram("a0_v", (B, P, P))
    prepare(nc, "a0p", "gqa", 8, q, k, i["x_t"], None, v, [i["a0_wq"], i["a0_wk"], i["a0_wv"]], i["rope_perm"],
            i["a0_cos"], i["a0_sin"])
    causal_gqa(nc, "a0", 8, i["x"], q, k, v, x1, i["ident"], i["sel_o16"], i["sel_s16"], i["half"],
               i["ident_bf"], i["mask"], i["mask_t"], i["a0_wo"], i["a0_bo"])

    q, k = dram("c0_q", (B, 48, 8 * D), BF16), dram("c0_k", (B, 48, 8 * D), BF16)
    v = dram("c0_v", (B, D, P))
    prepare(nc, "c0p", "cross", 8, q, k, x1, i["ctx"], v, [i["c0_wq"], i["c0_wk"], i["c0_wv"]], i["rope_perm"],
            i["c0_cos"], i["c0_sin"], i["c0_bqk"], i["c0_bv"])
    cross_attention(nc, "c0", 8, x1, q, k, v, x2, i["ident"], i["sel_o16"], i["sel_s16"], i["half"],
                    i["c0_wo"], i["c0_bo"])

    q1, k1 = dram("c1_q", (B, 24, 16 * D), BF16), dram("c1_k", (B, 24, 16 * D), BF16)
    h_t, mod = dram("f0_h_t", (B, P, DK, P)), dram("f0_mod", (B, 16, P))
    gate_attention(nc, "g0", x2, h_t, mod, i["f0_wq"], i["f0_wk"], i["f0_wv"], i["f0_wo"], i["f0_a"], i["f0_ln"],
                   i["ident"], i["half"], i["ident_bf"], i["mask"], i["mask_t"])
    feed_forward(nc, "f0", 16, h_t, x2, x3, i["f0_win"], i["f0_wup"], i["f0_wdown"], i["half"], mod,
                 i["f0_a"], i["f0_b"], ctx_in=i["ctx"], k_parts=k1, k_heads=16)

    squared_attention(nc, "a1", x3, x4, i["a1_wq"], i["a1_wk"], i["a1_wv"], i["a1_wo"], i["a1_gamma"], i["a1_beta"],
                      i["ident"], i["keep_t"], q1, 8 ** -0.5, 16)

    cross_attention(nc, "c1", 16, x4, q1, k1, i["ctx_t"], x5, i["ident"], i["sel_o8"], i["sel_s8"],
                    i["half"])

    h_t1, table = dram("f1_h_t", (B, P, DK, P)), dram("f1_table", (TABLE, 1), U32)
    sel_w, sel_slot = dram("f1_sel_w", (P, NSEL)), dram("f1_sel_slot", (P, NSEL), U32)
    rows = dram("f1_rows", (SLOTS + 1, D))
    router(nc, "r1", x5, h_t1, table, sel_w, sel_slot, i["f1_rw"], i["f1_rbias"], i["ident"], i["earlier"],
           i["ones_bf"], i["iota"], i["trash"], i["token"], i["zero_table"])
    experts(nc, "e1", x5.rearrange("b t d -> (b t) d"), table, rows, i["f1_gate"], i["f1_up"], i["f1_down"],
            i["ident"])
    feed_forward(nc, "f1", 8, h_t1, x5, out, i["f1_win"], i["f1_wup"], i["f1_wdown"], i["half"],
                 expert_rows=rows, sel_w_d=sel_w.rearrange("p (b k) -> p b k", k=TOPK), sel_slot_d=sel_slot)


def kernel(**inputs):
    import numpy as np
    import ml_dtypes
    import concourse.bacc as _bacc
    from concourse import mybir as _mybir
    from concourse.bass_utils import run_bass_kernel_spmd as _run

    w = {name: np.asarray(a) for name, a in inputs.items()}
    a = {}

    def rows(m):
        return m.reshape(m.shape[0] // P, P, -1).transpose(1, 0, 2)

    a["x"] = w["x"]
    a["x_t"] = w["x"].reshape(B, P, D // P, P).transpose(0, 3, 2, 1)
    a["ctx"] = w["ctx_2048"]
    a["ctx_t"] = w["ctx_2048"].transpose(0, 2, 1)
    a["a0_wq"] = w["L0_attn_Wq"].reshape(4, P, 8, 4, 16).transpose(1, 0, 3, 2, 4).reshape(P, 4, D)
    a["a0_wk"] = rows(w["L0_attn_Wk"])
    a["a0_wv"] = rows(w["L0_attn_Wv"])
    a["a0_wo"] = w["L0_attn_Wo"].reshape(8, 4, 16, D).transpose(0, 2, 1, 3).reshape(P, 4, D)
    a["a0_bo"] = np.broadcast_to(w["L0_attn_b_out"], (P, D))
    for n in "qkvo":
        a[f"c0_w{n}"] = w[f"L0_xattn_W{n}"].T
        a[f"a1_w{n}"] = rows(w[f"L1_attn_W{n}"].T)
    a["c0_bqk"] = np.stack([w["L0_xattn_bq"], w["L0_xattn_bk"]], 1)
    a["c0_bv"] = np.broadcast_to(np.tile(w["L0_xattn_bv"], 4), (P, D))
    a["c0_bo"] = w["L0_xattn_bo"].reshape(P, 1)
    for n in "qkv":
        a[f"f0_w{n}"] = rows(w[f"L0_ffn_W{n}"].T)
    a["f0_wo"] = rows(w["L0_ffn_Wo"])
    a["f0_a"] = rows(w["L0_ffn_A"])
    a["f0_b"] = w["L0_ffn_B"]
    a["f0_ln"] = np.stack([w[f"L0_ffn_ln{n}_w"].reshape(4, P).T for n in (1, 2)], 1)
    a["f0_win"] = rows(w["L0_ffn_W_in_base"].T)
    a["f0_wup"] = rows(w["L0_ffn_W_up_base"].T)
    a["f0_wdown"] = rows(w["L0_ffn_W_down"].T)
    a["a1_gamma"] = np.broadcast_to(w["L1_attn_gamma"], (P, 32))
    a["a1_beta"] = np.broadcast_to(w["L1_attn_beta"], (P, 32))
    a["f1_rw"] = rows(w["L1_ffn_router_w"].T)
    a["f1_rbias"] = np.broadcast_to(w["L1_ffn_router_bias"], (P, E))
    for n in ("gate", "up"):
        a[f"f1_{n}"] = w[f"L1_ffn_{n}_w"].transpose(0, 2, 1).reshape(E, 4, P, P).transpose(0, 2, 1, 3)
    a["f1_down"] = w["L1_ffn_down_w"].transpose(0, 2, 1)
    a["f1_win"] = rows(w["L1_ffn_sh_gate_w"].reshape(-1, D).T)
    a["f1_wup"] = rows(w["L1_ffn_sh_up_w"].reshape(-1, D).T)
    a["f1_wdown"] = rows(w["L1_ffn_sh_down_w"].transpose(0, 2, 1).reshape(-1, D))

    c = np.arange(P)
    a["ident"] = np.eye(P, dtype=np.float32)
    a["ident_bf"] = a["ident"].astype(ml_dtypes.bfloat16)
    a["half"] = np.full((P, 1), -0.5, np.float32)
    a["mask"] = np.where(c[None, :] > c[:, None], -1e30, 0.0).astype(ml_dtypes.bfloat16)
    a["mask_t"] = a["mask"].T
    a["keep_t"] = np.triu(np.ones((P, P), np.float32))
    a["earlier"] = (c[:, None] < c[None, :]).astype(ml_dtypes.bfloat16)
    a["ones_bf"] = np.ones((P, P), ml_dtypes.bfloat16)
    a["iota"] = np.broadcast_to(np.arange(E, dtype=np.float32), (P, E))
    a["trash"] = (SLOTS + np.arange(NSEL)[None, :] * P + c[:, None]).astype(np.float32)
    a["token"] = (np.arange(B)[None, :] * P + c[:, None]).astype(np.uint32)
    a["zero_table"] = np.zeros((P, TABLE // P), np.uint32)
    for ch in (16, 8):
        sel_o, sel_s = np.zeros((P, 4 * ch), np.float32), np.zeros((P, 4 * ch), np.float32)
        for r in range(4 * ch):
            sel_o[32 * (r // ch) + r % ch, r] = 1
            sel_s[32 * (r // ch) + ch + r % ch, r] = 1
        a[f"sel_o{ch}"], a[f"sel_s{ch}"] = sel_o, sel_s
    inv_freq = (1.0 / 10000.0 ** (np.arange(0, 16, 2, dtype=np.float32) / np.float32(16))).astype(np.float32)
    angle = np.arange(D, dtype=np.float32)[None, :] * inv_freq[:, None]
    cos = np.tile(np.concatenate([np.cos(angle), np.cos(angle)]), (8, 1)).astype(np.float32)
    sin = np.tile(np.concatenate([-np.sin(angle), np.sin(angle)]), (8, 1)).astype(np.float32)
    for name, t in (("cos", cos), ("sin", sin)):
        a[f"a0_{name}"] = np.concatenate([np.tile(t[:, :P] / 4, (1, 4)), t[:, :P]], 1)
        a[f"c0_{name}"] = np.concatenate([t / 4, t], 1)
    a["rope_perm"] = np.zeros((P, P), np.float32)
    a["rope_perm"][c - c % 16 + (c % 16 + 8) % 16, c] = 1

    nc = _bacc.Bacc("TRN2", target_bir_lowering=False, num_devices=1)
    arrays, aps = {}, {}
    for name, value in a.items():
        value = np.ascontiguousarray(value)
        arrays[f"in_{name}"] = value
        aps[name] = nc.dram_tensor(f"in_{name}", value.shape, _mybir.dt.from_np(value.dtype),
                                   kind="ExternalInput").ap()
    out = nc.dram_tensor("out_0", (B, P, D), F32, kind="ExternalOutput").ap()
    decoder(nc, aps, out)
    return _run(nc, [arrays], core_ids=[0]).results[0]["out_0"]
```
